# Optimizing a Trainium2 kernel written in Bass

```python
import numpy as np
import jax
import jax.numpy as jnp

def _softmax(x, axis=-1):
    return jax.nn.softmax(x, axis=axis)

def _gelu(x):
    return jax.nn.gelu(x, approximate=True)

def _silu(x):
    return jax.nn.silu(x)

def _sigmoid(x):
    return jax.nn.sigmoid(x)

def _layernorm(x, axis=-1, eps=1e-05):
    m = jnp.mean(x, axis=axis, keepdims=True)
    v = jnp.var(x, axis=axis, keepdims=True)
    return (x - m) / jnp.sqrt(v + eps)

def _scatter_add(tgt, idx, src, axis=0):
    return tgt.at[idx].add(src)

def _segment_sum(src, seg, n):
    return jax.ops.segment_sum(src, seg, n)
kernel_name = 'mk_gnn_resnorm_d4_gnn_r64_79467c'

def setup_inputs(seed: int=0):
    np.random.seed(seed)
    _w = jnp.asarray

    def _rec_inputs():
        import jax
        import jax.numpy as jnp
        _gk = jax.random.key(seed)
        x = -0.000202 + 1 * jax.random.normal(jax.random.fold_in(_gk, 1), (50000, 128), jnp.float32)
        src = jax.random.randint(jax.random.fold_in(_gk, 2), (25000,), 0, 50000, jnp.int32)
        dst = jax.random.randint(jax.random.fold_in(_gk, 3), (25000,), 0, 50000, jnp.int32)
        _o = jnp.argsort(dst, stable=True)
        src = src[_o]
        dst = dst[_o]
        edge_type_8 = jax.random.randint(jax.random.fold_in(_gk, 13), (25000,), 0, 8, jnp.int32)
        return (x, src, dst, edge_type_8)
    x, src, dst, edge_type_8 = _rec_inputs()

    def _L0_gnn_setup():
        import jax, jax.numpy as jnp
        import numpy as np
        N = 50000
        E = 9375
        D = 128
        R = 8

        def rgcn_conv(x, W, root, b, src, dst, etype):
            seg = etype * N + dst
            msg = x[src]
            agg = jax.ops.segment_sum(msg, seg, num_segments=R * N)
            cnt = jax.ops.segment_sum(jnp.ones((src.shape[0],), x.dtype), seg, num_segments=R * N)
            mean = agg.reshape(R, N, D) / jnp.maximum(cnt, 1.0).reshape(R, N, 1)
            out = jnp.einsum('rni,rio->no', mean, W)
            out = out + x @ root + b
            return out
        key = jax.random.key(seed)
        ks = jax.random.split(key, 10)
        x = jax.random.normal(ks[0], (N, D), dtype=jnp.float32)
        edge_index = jax.random.randint(ks[1], (2, E), 0, N, dtype=jnp.int64)
        edge_type = jax.random.randint(ks[2], (E,), 0, R, dtype=jnp.int64)
        s = 1.0 / np.sqrt(D)
        W1 = jax.random.normal(ks[3], (R, D, D), dtype=jnp.float32) * s
        root1 = jax.random.normal(ks[4], (D, D), dtype=jnp.float32) * s
        b1 = jnp.zeros((D,), dtype=jnp.float32)
        W2 = jax.random.normal(ks[5], (R, D, D), dtype=jnp.float32) * s
        root2 = jax.random.normal(ks[6], (D, D), dtype=jnp.float32) * s
        b2 = jnp.zeros((D,), dtype=jnp.float32)
        return {'x': x, 'W1': W1, 'root1': root1, 'b1': b1, 'W2': W2, 'root2': root2, 'b2': b2, 'edge_index': edge_index, 'edge_type': edge_type}
    _L0_gnn_all = _L0_gnn_setup()
    _L0_gnn_in = {k: v for k, v in _L0_gnn_all.items() if k in ('W1', 'root1', 'b1', 'W2', 'root2', 'b2')}
    del _L0_gnn_all

    def _L1_gnn_setup():
        import jax, jax.numpy as jnp
        import numpy as np
        N_NODES = 100000
        N_EDGES = 9375
        DIM = 128
        LN_EPS = 1e-05
        key = jax.random.key(seed)
        ks = jax.random.split(key, 12)
        s = 1.0 / np.sqrt(DIM)
        return {'h': jax.random.normal(ks[0], (N_NODES, DIM), dtype=jnp.float32), 'edge_src': jax.random.randint(ks[1], (N_EDGES,), 0, N_NODES, dtype=jnp.int32), 'edge_dst': jax.random.randint(ks[2], (N_EDGES,), 0, N_NODES, dtype=jnp.int32), 'W_self': jax.random.uniform(ks[3], (DIM, DIM), jnp.float32, -s, s), 'b_self': jax.random.uniform(ks[4], (DIM,), jnp.float32, -s, s), 'W_neigh': jax.random.uniform(ks[5], (DIM, DIM), jnp.float32, -s, s), 'b_neigh': jax.random.uniform(ks[6], (DIM,), jnp.float32, -s, s), 'W_gate': jax.random.uniform(ks[7], (DIM, 2 * DIM), jnp.float32, -s, s), 'b_gate': jax.random.uniform(ks[8], (DIM,), jnp.float32, -s, s), 'ln_gamma': jnp.ones((DIM,), jnp.float32), 'ln_beta': jnp.zeros((DIM,), jnp.float32)}
    _L1_gnn_all = _L1_gnn_setup()
    _L1_gnn_in = {k: v for k, v in _L1_gnn_all.items() if k in ('W_self', 'b_self', 'W_neigh', 'b_neigh', 'W_gate', 'b_gate', 'ln_gamma', 'ln_beta')}
    del _L1_gnn_all

    def _L2_gnn_setup():
        import jax, jax.numpy as jnp
        import numpy as np
        NEG_SLOPE = 0.2
        EPS = 1e-16
        N_NODES = 100000
        N_EDGES = 25000
        D = 128
        H = 4
        C = 32
        L = 3

        def _gat_layer(h, src, dst, Ws, Wd, a_s, a_d, bias):
            N = h.shape[0]
            xs = (h @ Ws).reshape(N, H, C)
            xd = (h @ Wd).reshape(N, H, C)
            alpha_s = jnp.sum(xs * a_s, axis=-1)
            alpha_d = jnp.sum(xd * a_d, axis=-1)
            e = alpha_s[src] + alpha_d[dst]
            e = jax.nn.leaky_relu(e, NEG_SLOPE)
            emax = jax.ops.segment_max(e, dst, num_segments=N)
            ex = jnp.exp(e - emax[dst])
            denom = jax.ops.segment_sum(ex, dst, num_segments=N)
            alpha = ex / (denom[dst] + EPS)
            msg = xs[src] * alpha[:, :, None]
            out = jax.ops.segment_sum(msg, dst, num_segments=N)
            return out.reshape(N, H * C) + bias
        key = jax.random.key(seed)
        ks = jax.random.split(key, 7)
        x = jax.random.normal(ks[0], (N_NODES, D), dtype=jnp.float32)
        edge_index = jax.random.randint(ks[1], (2, N_EDGES), 0, N_NODES, dtype=jnp.int32)
        scale = 1.0 / np.sqrt(D)
        Ws = jax.random.normal(ks[2], (L, D, H * C), dtype=jnp.float32) * scale
        Wd = jax.random.normal(ks[3], (L, D, H * C), dtype=jnp.float32) * scale
        att_s = jax.random.normal(ks[4], (L, H, C), dtype=jnp.float32) * scale
        att_d = jax.random.normal(ks[5], (L, H, C), dtype=jnp.float32) * scale
        b = jnp.zeros((L, H * C), dtype=jnp.float32)
        return {'x': x, 'edge_index': edge_index, 'Ws': Ws, 'Wd': Wd, 'att_s': att_s, 'att_d': att_d, 'b': b}
    _L2_gnn_all = _L2_gnn_setup()
    _L2_gnn_in = {k: v for k, v in _L2_gnn_all.items() if k in ('Ws', 'Wd', 'att_s', 'att_d', 'b')}
    del _L2_gnn_all

    def _L3_gnn_setup():
        import jax, jax.numpy as jnp
        import numpy as np
        N = 100000
        E = 25000
        IN_DIM = 128
        HEADS = 4
        OUT_DIM = 32
        ALPHA = 0.2
        EPS = 1e-08
        key = jax.random.key(seed)
        k1, k2, k3, k4, k5, k6 = jax.random.split(key, 6)
        x = jax.random.normal(k1, (N, IN_DIM), dtype=jnp.float32)
        edge_index = jax.random.randint(k2, (2, E), 0, N, dtype=jnp.int64)
        W = jax.random.normal(k3, (IN_DIM, HEADS * OUT_DIM), dtype=jnp.float32) * (2.0 / IN_DIM) ** 0.5
        A_left = jax.random.normal(k4, (HEADS, OUT_DIM, 1), dtype=jnp.float32) * (2.0 / OUT_DIM) ** 0.5
        A_right = jax.random.normal(k5, (HEADS, OUT_DIM, 1), dtype=jnp.float32) * (2.0 / OUT_DIM) ** 0.5
        residual_projection = jax.random.normal(k6, (IN_DIM, HEADS * OUT_DIM), dtype=jnp.float32) * (2.0 / IN_DIM) ** 0.5
        return {'x': x, 'edge_index': edge_index, 'W': W, 'A_left': A_left, 'A_right': A_right, 'residual_projection': residual_projection}
    _L3_gnn_all = _L3_gnn_setup()
    _L3_gnn_in = {k: v for k, v in _L3_gnn_all.items() if k in ('W', 'A_left', 'A_right', 'residual_projection')}
    del _L3_gnn_all
    return {'x': x, 'src': src, 'dst': dst, 'edge_type_8': edge_type_8, 'L0_gnn_W1': _L0_gnn_in['W1'], 'L0_gnn_root1': _L0_gnn_in['root1'], 'L0_gnn_b1': _L0_gnn_in['b1'], 'L0_gnn_W2': _L0_gnn_in['W2'], 'L0_gnn_root2': _L0_gnn_in['root2'], 'L0_gnn_b2': _L0_gnn_in['b2'], 'L1_gnn_W_self': _L1_gnn_in['W_self'], 'L1_gnn_b_self': _L1_gnn_in['b_self'], 'L1_gnn_W_neigh': _L1_gnn_in['W_neigh'], 'L1_gnn_b_neigh': _L1_gnn_in['b_neigh'], 'L1_gnn_W_gate': _L1_gnn_in['W_gate'], 'L1_gnn_b_gate': _L1_gnn_in['b_gate'], 'L1_gnn_ln_gamma': _L1_gnn_in['ln_gamma'], 'L1_gnn_ln_beta': _L1_gnn_in['ln_beta'], 'L2_gnn_Ws': _L2_gnn_in['Ws'], 'L2_gnn_Wd': _L2_gnn_in['Wd'], 'L2_gnn_att_s': _L2_gnn_in['att_s'], 'L2_gnn_att_d': _L2_gnn_in['att_d'], 'L2_gnn_b': _L2_gnn_in['b'], 'L3_gnn_W': _L3_gnn_in['W'], 'L3_gnn_A_left': _L3_gnn_in['A_left'], 'L3_gnn_A_right': _L3_gnn_in['A_right'], 'L3_gnn_residual_projection': _L3_gnn_in['residual_projection']}

def reference(x, src, dst, edge_type_8, L0_gnn_W1, L0_gnn_root1, L0_gnn_b1, L0_gnn_W2, L0_gnn_root2, L0_gnn_b2, L1_gnn_W_self, L1_gnn_b_self, L1_gnn_W_neigh, L1_gnn_b_neigh, L1_gnn_W_gate, L1_gnn_b_gate, L1_gnn_ln_gamma, L1_gnn_ln_beta, L2_gnn_Ws, L2_gnn_Wd, L2_gnn_att_s, L2_gnn_att_d, L2_gnn_b, L3_gnn_W, L3_gnn_A_left, L3_gnn_A_right, L3_gnn_residual_projection):
    import jax
    import jax.numpy as jnp

    def _L0_gnn_ref(x, W1, root1, b1, W2, root2, b2, edge_index, edge_type):
        import jax, jax.numpy as jnp
        import numpy as np
        N = 50000
        E = 9375
        D = 128
        R = 8

        def rgcn_conv(x, W, root, b, src, dst, etype):
            seg = etype * N + dst
            msg = x[src]
            agg = jax.ops.segment_sum(msg, seg, num_segments=R * N)
            cnt = jax.ops.segment_sum(jnp.ones((src.shape[0],), x.dtype), seg, num_segments=R * N)
            mean = agg.reshape(R, N, D) / jnp.maximum(cnt, 1.0).reshape(R, N, 1)
            out = jnp.einsum('rni,rio->no', mean, W)
            out = out + x @ root + b
            return out
        src, dst = (edge_index[0], edge_index[1])
        z = jax.nn.relu(rgcn_conv(x, W1, root1, b1, src, dst, edge_type))
        z = jax.nn.relu(rgcn_conv(z, W2, root2, b2, src, dst, edge_type))
        return z

    def _L1_gnn_ref(h, edge_src, edge_dst, W_self, b_self, W_neigh, b_neigh, W_gate, b_gate, ln_gamma, ln_beta):
        import jax, jax.numpy as jnp
        import numpy as np
        N_NODES = 100000
        N_EDGES = 9375
        DIM = 128
        LN_EPS = 1e-05
        n = h.shape[0]
        hs = h @ W_self.T + b_self
        neigh_sum = jax.ops.segment_sum(h[edge_src], edge_dst, num_segments=n)
        counts = jax.ops.segment_sum(jnp.ones((edge_src.shape[0],), h.dtype), edge_dst, num_segments=n)
        has_pred = (counts > 0).astype(h.dtype)[:, None]
        neigh_mean = neigh_sum / jnp.maximum(counts, 1.0)[:, None]
        hn = neigh_mean @ W_neigh.T + b_neigh
        m = hs + has_pred * hn
        gate = jax.nn.sigmoid(jnp.concatenate([h, m], axis=-1) @ W_gate.T + b_gate)
        v = gate * m + (1.0 - gate) * h
        mu = jnp.mean(v, axis=-1, keepdims=True)
        var = jnp.mean(jnp.square(v - mu), axis=-1, keepdims=True)
        out = (v - mu) * jax.lax.rsqrt(var + LN_EPS) * ln_gamma + ln_beta
        return jax.nn.relu(out)

    def _L2_gnn_ref(x, edge_index, Ws, Wd, att_s, att_d, b):
        import jax, jax.numpy as jnp
        import numpy as np
        NEG_SLOPE = 0.2
        EPS = 1e-16
        N_NODES = 100000
        N_EDGES = 25000
        D = 128
        H = 4
        C = 32
        L = 3

        def _gat_layer(h, src, dst, Ws, Wd, a_s, a_d, bias):
            N = h.shape[0]
            xs = (h @ Ws).reshape(N, H, C)
            xd = (h @ Wd).reshape(N, H, C)
            alpha_s = jnp.sum(xs * a_s, axis=-1)
            alpha_d = jnp.sum(xd * a_d, axis=-1)
            e = alpha_s[src] + alpha_d[dst]
            e = jax.nn.leaky_relu(e, NEG_SLOPE)
            emax = jax.ops.segment_max(e, dst, num_segments=N)
            ex = jnp.exp(e - emax[dst])
            denom = jax.ops.segment_sum(ex, dst, num_segments=N)
            alpha = ex / (denom[dst] + EPS)
            msg = xs[src] * alpha[:, :, None]
            out = jax.ops.segment_sum(msg, dst, num_segments=N)
            return out.reshape(N, H * C) + bias
        src = edge_index[0]
        dst = edge_index[1]
        h = x
        for i in range(L):
            h = _gat_layer(h, src, dst, Ws[i], Wd[i], att_s[i], att_d[i], b[i])
            if i < L - 1:
                h = jax.nn.relu(h)
        return h

    def _L3_gnn_ref(x, edge_index, W, A_left, A_right, residual_projection):
        import jax, jax.numpy as jnp
        import numpy as np
        N = 100000
        E = 25000
        IN_DIM = 128
        HEADS = 4
        OUT_DIM = 32
        ALPHA = 0.2
        EPS = 1e-08
        n = x.shape[0]
        H = jnp.matmul(x, W).reshape(n, HEADS, OUT_DIM).transpose(1, 0, 2)
        H_s = jnp.einsum('hnd,hd->hn', H, A_left[..., 0])
        H_t = jnp.einsum('hnd,hd->hn', H, A_right[..., 0])
        src = edge_index[0]
        tgt = edge_index[1]
        s = H_s[:, src] + H_t[:, tgt]
        s = jnp.where(s >= 0, s, ALPHA * s)
        s = jnp.exp(s - jnp.max(s))
        denom = jnp.zeros((HEADS, n), dtype=s.dtype).at[:, src].add(s)
        alpha = s / (denom[:, src] + EPS)
        H_sf = H[:, tgt]
        agg = jnp.zeros((HEADS, n, OUT_DIM), dtype=H.dtype).at[:, src].add(alpha[..., None] * H_sf)
        agg = agg + jnp.matmul(x, residual_projection).reshape(n, HEADS, OUT_DIM).transpose(1, 0, 2)
        res = agg.transpose(1, 0, 2).reshape(n, HEADS * OUT_DIM)
        return jax.nn.elu(res)
    edge_index = jnp.stack([src, dst])
    x = _layernorm(x + _L0_gnn_ref(x, L0_gnn_W1, L0_gnn_root1, L0_gnn_b1, L0_gnn_W2, L0_gnn_root2, L0_gnn_b2, edge_index, edge_type_8), axis=-1)
    x = _layernorm(x + _L1_gnn_ref(x, src, dst, L1_gnn_W_self, L1_gnn_b_self, L1_gnn_W_neigh, L1_gnn_b_neigh, L1_gnn_W_gate, L1_gnn_b_gate, L1_gnn_ln_gamma, L1_gnn_ln_beta), axis=-1)
    x = _layernorm(x + _L2_gnn_ref(x, edge_index, L2_gnn_Ws, L2_gnn_Wd, L2_gnn_att_s, L2_gnn_att_d, L2_gnn_b), axis=-1)
    x = _layernorm(x + _L3_gnn_ref(x, edge_index, L3_gnn_W, L3_gnn_A_left, L3_gnn_A_right, L3_gnn_residual_projection), axis=-1)
    return x

_drawn_inputs = setup_inputs


def setup_inputs(seed=0):
    import zlib

    import numpy as np

    out = dict(_drawn_inputs(seed))
    spreads = {'L0_gnn_b1': (0.0, 0.1),
     'L0_gnn_b2': (0.0, 0.1),
     'L1_gnn_ln_gamma': (1.0, 0.2),
     'L1_gnn_ln_beta': (0.0, 0.1),
     'L2_gnn_b': (0.0, 0.1)}
    factors = {'L1_gnn_b_neigh': 3.958,
     'L1_gnn_b_gate': 4.418,
     'L2_gnn_Wd': 8.0,
     'L2_gnn_att_s': 6.637,
     'L2_gnn_att_d': 8.0}
    for name, (base, spread) in spreads.items():
        noise = np.random.default_rng([zlib.crc32(name.encode()), seed]).standard_normal(out[name].shape)
        drawn = base * np.exp(spread * noise) if base else spread * noise
        out[name] = jnp.asarray(drawn.astype(out[name].dtype))
    for name, factor in factors.items():
        out[name] = (out[name] * factor).astype(out[name].dtype)
    return out
```

```python
from contextlib import ExitStack

import numpy as np
import concourse.bass as bass
from concourse import mybir

F32 = mybir.dt.float32
I32 = mybir.dt.int32
ALU = mybir.AluOpType
ACT = mybir.ActivationFunctionType
AX_X = mybir.AxisListType.X

P = 128
N = 50000
E = 25000
D = 128
R = 8
H = 4
C = D // H
T = -(-E // P)
PAD = P * T
FULL = E // T
REST = E - FULL * T
R1 = R + 1
W = D + H
UROWS = 392 * P
SKIP = 1 << 20
LN_EPS = 1e-5
RING = 14


class Program:
    pass


class Phase:

    def __init__(self, nc, name):
        self.nc, self.name, self.sems = nc, name, []

    def sem(self, what):
        s = self.nc.alloc_semaphore(f"{self.name}_{what}")
        self.sems.append(s)
        return s

    def end(self):
        self.nc.clear_and_free_semaphores(self.sems)
        self.nc.all_engine_barrier()


def setup(g):
    nc, a = g.nc, g.args
    ph = Phase(nc, "setup")
    s_const, s_edges, s_w, s_dve, s_pe, s_iota, s_tab0, s_zero = (
        ph.sem(n) for n in ("const", "edges_loaded", "weights_loaded", "dve_steps", "pe_steps",
                            "iota", "table_filled", "zeros_stored"))
    src_r = a["src"].rearrange("(p t) -> p t", t=T) if E % T == 0 else None
    done = {}
    with nc.Block() as block:
        @block.sync
        def _(sp):
            sp.wait_ge(s_const, 1)
            for dram, tile in ((a["src"], g.src_i), (a["dst"], g.dst_i), (a["edge_type_8"], g.type_i)):
                sp.dma_start(tile[0:FULL, :], dram[0:FULL * T].rearrange("(p t) -> p t", t=T)).then_inc(s_edges, 16)
                sp.dma_start(tile[FULL:FULL + 1, 0:REST],
                             dram[FULL * T:E].rearrange("(p t) -> p t", t=REST)).then_inc(s_edges, 16)
            with nc.allow_non_contiguous_dma(reason="one value a partition"):
                sp.dma_start(g.dst_next_i[0:P - 1, :],
                             a["dst"][0:FULL * T].rearrange("(p t) -> p t", t=T)[:, 0:1] if False else
                             g.dst_next_view).then_inc(s_edges, 16)
            for tile, view in g.weight_loads:
                sp.dma_start(tile, view).then_inc(s_w, 16)
            sp.wait_ge(s_iota, 1)
            sp.dma_start(g.tab_dram.rearrange("(p t) o -> p (t o)", p=125), g.node_iota[0:125, :]).then_inc(s_tab0, 16)
            sp.wait_ge(s_const, 2)
            sp.dma_start(g.U_dram.rearrange("(p b r) w -> p b (r w)", p=P, b=g.ZB),
                         g.zero_row[:, None, :].to_broadcast([P, g.ZB, g.ZW])).then_inc(s_zero, 16)
            sp.wait_ge(s_w, 16 * len(g.weight_loads))
            sp.wait_ge(s_edges, 16 * 7)
            sp.wait_ge(s_tab0, 16)
            sp.wait_ge(s_zero, 16)

        @block.gpsimd
        def _(pool):
            nc.gpsimd.memset(g.src_i[:], 0)
            nc.gpsimd.memset(g.dst_i[:], N)
            nc.gpsimd.memset(g.type_i[:], 0)
            nc.gpsimd.memset(g.dst_next_i[:], -1).then_inc(s_const, 1)
            nc.gpsimd.memset(g.zero_row, 0.0).then_inc(s_const, 1)
            nc.gpsimd.memset(g.ones[:], 1.0)
            nc.gpsimd.memset(g.ident[:], 0.0).then_inc(s_const, 1)
            nc.gpsimd.iota(g.node_iota, [[1, 400]], base=0, channel_multiplier=400).then_inc(s_iota, 1)
            pool.wait_ge(s_const, 3)
            nc.gpsimd.affine_select(out=g.ident[:], in_=g.ident[:], compare_op=ALU.not_equal, fill=1.0,
                                    base=0, pattern=[[-1, P]], channel_multiplier=1).then_inc(s_const, 1)
            nc.gpsimd.affine_select(out=g.below[:], in_=g.ones[:], compare_op=ALU.is_gt, fill=0.0,
                                    base=0, pattern=[[-1, P]], channel_multiplier=1).then_inc(s_const, 1)
            nc.gpsimd.affine_select(out=g.above[:], in_=g.ones[:], compare_op=ALU.is_gt, fill=0.0,
                                    base=0, pattern=[[1, P]], channel_multiplier=-1).then_inc(s_const, 1)
            nc.gpsimd.iota(g.spare_i[:], [[1, 1]], base=N, channel_multiplier=1).then_inc(s_const, 1)
            nc.gpsimd.iota(g.slot_i[:], [[1, T]], base=0, channel_multiplier=T).then_inc(s_const, 1)

        @block.vector
        def _(dve):
            n = [0]

            def link(ins):
                n[0] += 1
                ins.then_inc(s_dve, 1)
                dve.wait_ge(s_dve, n[0])

            def mark(what):
                done[what] = n[0]
            V = nc.vector
            dve.wait_ge(s_const, 8)
            dve.wait_ge(s_w, 16 * len(g.weight_loads))
            link(V.tensor_scalar(g.bself_rep, g.ones[:], g.bself_col[:, 0:1], None, ALU.mult))
            link(V.tensor_scalar(g.bneigh_rep, g.ones[:], g.bneigh_col[:, 0:1], None, ALU.mult))
            mark("biases")
            dve.wait_ge(s_edges, 16 * 7)
            link(V.tensor_copy(g.dstf[:, 1:T + 1], g.dst_i[:]))
            link(V.tensor_copy(g.dstf[:, T + 1:T + 2], g.dst_next_i[:]))
            link(V.tensor_copy(g.typef[:], g.type_i[:]))
            link(V.memset(g.eps[:], LN_EPS))
            link(V.tensor_scalar(g.own_i[:], g.dst_i[:], float(N - 1), None, ALU.min))
            dst = g.dstf[:, 1:T + 1]
            first, last = g.dstf[:, 1:2], g.dstf[:, T:T + 1]
            link(V.tensor_scalar(g.diag_first, g.ident[:], first, None, ALU.mult))
            link(V.tensor_scalar(g.diag_last, g.ident[:], last, None, ALU.mult))
            mark("ends")
            link(V.memset(g.same[:], 0.0))
            link(V.tensor_tensor(g.same[:, 1:T], g.dstf[:, 2:T + 1], g.dstf[:, 1:T], ALU.is_equal))
            link(V.tensor_tensor(g.is_last[:], dst, g.dstf[:, 2:T + 2], ALU.not_equal))
            link(V.scalar_tensor_tensor(g.is_last[:], dst, float(N), g.is_last[:], ALU.is_lt, ALU.mult))
            link(V.tensor_scalar(g.in_first[:], dst, first, None, ALU.is_equal))
            link(V.tensor_scalar(g.in_last[:], dst, last, None, ALU.is_equal))
            link(V.tensor_scalar(g.tmpT[:], g.is_last[:], -float(SKIP), float(SKIP), ALU.mult, ALU.add))
            link(V.tensor_tensor(g.tmpT[:], g.tmpT[:], dst, ALU.add))
            link(V.tensor_copy(g.last_node_i[:], g.tmpT[:]))
            link(V.tensor_scalar(g.tab_row_i[:], g.slot_i[:], float(N), None, ALU.add))
            dve.wait_ge(s_pe, 6)
            rowF, rowL = g.ps[1][:, 0:P], g.ps[1][:, P:2 * P]
            link(V.scalar_tensor_tensor(g.link_in[:], rowF, last, g.above[:], ALU.is_equal, ALU.mult))
            link(V.scalar_tensor_tensor(g.link_out[:], rowL, first, g.below[:], ALU.is_equal, ALU.mult))
            link(V.scalar_tensor_tensor(g.no_in[:], rowL, first, g.below[:], ALU.is_equal, ALU.mult))
            link(V.scalar_tensor_tensor(g.no_out[:], rowF, last, g.above[:], ALU.is_equal, ALU.mult))
            link(V.tensor_scalar(g.no_in[:], g.no_in[:], 1e30, -1e30, ALU.mult, ALU.add))
            link(V.tensor_scalar(g.no_out[:], g.no_out[:], 1e30, -1e30, ALU.mult, ALU.add))
            link(V.tensor_copy(g.tmpT[:], g.slot_i[:]))
            for r in range(R1):
                oh, fwd, bwd = g.wrel[:, r, :], g.cnt_fwd[:, r, :], g.cnt_bwd[:, r, :]
                if r < R:
                    link(V.tensor_scalar(oh, g.typef[:], float(r), None, ALU.is_equal))
                else:
                    link(V.tensor_tensor(oh, g.tmpT[:], g.is_last[:], ALU.mult))
                link(V.tensor_tensor_scan(fwd, g.same[:, 0:T], oh, 0.0, ALU.mult, ALU.add))
                link(V.tensor_tensor_scan(bwd[:, ::-1], g.same[:, 1:T + 1][:, ::-1], oh[:, ::-1], 0.0, ALU.mult, ALU.add))
            link(V.tensor_copy(g.edge_ends[:, 0:R1], g.cnt_fwd[:, :, T - 1]))
            link(V.tensor_copy(g.edge_ends[:, R1:2 * R1], g.cnt_bwd[:, :, 0]))
            mark("counts")
            dve.wait_ge(s_pe, 8)
            link(V.tensor_copy(g.edge_ends[:], g.ps[2][:, 0:2 * R1]))
            link(V.memset(g.rcnt[:], 0.0))
            for r in range(R1):
                oh, fwd, bwd = g.wrel[:, r, :], g.cnt_fwd[:, r, :], g.cnt_bwd[:, r, :]
                link(V.tensor_tensor(fwd, fwd, bwd, ALU.add))
                link(V.tensor_tensor(fwd, fwd, oh, ALU.subtract))
                link(V.scalar_tensor_tensor(fwd, g.in_first[:], g.edge_ends[:, r:r + 1], fwd, ALU.mult, ALU.add))
                link(V.scalar_tensor_tensor(fwd, g.in_last[:], g.edge_ends[:, R1 + r:R1 + r + 1], fwd, ALU.mult, ALU.add))
                if r == R:
                    link(V.tensor_copy(g.dst_slot_i[:], fwd))
                    continue
                link(V.tensor_tensor(g.rcnt[:], g.rcnt[:], fwd, ALU.add))
                link(V.tensor_scalar(fwd, fwd, 1.0, None, ALU.max))
                link(V.reciprocal(fwd, fwd))
                link(V.tensor_tensor(oh, oh, fwd, ALU.mult))
            link(V.reciprocal(g.rcnt[:], g.rcnt[:]))
            link(V.tensor_copy(g.w_slot[:].rearrange("p t r -> p r t"), g.wrel[:, 0:R, :]))
            dve.wait_ge(s_pe, 4)
            link(V.tensor_tensor(g.A_gate[:, 0:D], g.WselfT, g.ident[:], ALU.subtract))
            link(V.tensor_tensor(g.A_gate[:, D:2 * D], g.WgaT, g.ps[0][:, 0:D], ALU.add))
            link(V.tensor_copy(g.B_gate[:, 0:D], g.WneighT))
            link(V.tensor_copy(g.B_gate[:, D:2 * D], g.ps[0][:, D:2 * D]))
            link(V.tensor_tensor(g.bias_gate[:, D:2 * D], g.bgate_row[:], g.ps[0][0:1, 2 * D:3 * D], ALU.add))
            link(V.tensor_copy(g.bias_gate[:, 0:D], g.bself_row[:]))
            link(V.tensor_tensor(g.bias_gate_n[:, 0:D], g.bself_row[:], g.bneigh_row[:], ALU.add))
            link(V.tensor_tensor(g.bias_gate_n[:, D:2 * D], g.bias_gate[:, D:2 * D], g.ps[0][0:1, 3 * D:4 * D], ALU.add))
            for out, w, row in g.att_products:
                link(V.tensor_tensor(g.att_tmp, w, row, ALU.mult))
                link(V.tensor_reduce(out, g.att_tmp[:].rearrange("p (h c) -> p h c", h=H), AX_X, ALU.add))
            for i in range(2):
                link(V.tensor_scalar(g.bias_rep[i], g.ones[:], g.gat_bias_col[:, i:i + 1], 0.0, ALU.mult, ALU.max))
            mark("weights")
            dve.wait_ge(s_pe, 10)
            for i in range(2):
                link(V.tensor_copy(g.const_row[i][:], g.ps[3 + i][0:1, 0:W]))

        @block.tensor
        def _(pe):
            def step(n, ins):
                ins.then_inc(s_pe, 1)
            pe.wait_ge(s_w, 16 * len(g.weight_loads))
            step(1, nc.tensor.matmul(g.ps[0][:, 0:D], g.W_self, g.WgbT, start=True, stop=True))
            step(2, nc.tensor.matmul(g.ps[0][:, D:2 * D], g.W_neigh, g.WgbT, start=True, stop=True))
            pe.wait_ge(s_dve, done["biases"])
            step(3, nc.tensor.matmul(g.ps[0][:, 2 * D:3 * D], g.bself_rep, g.WgbT, start=True, stop=True))
            step(4, nc.tensor.matmul(g.ps[0][:, 3 * D:4 * D], g.bneigh_rep, g.WgbT, start=True, stop=True))
            pe.wait_ge(s_dve, done["ends"])
            step(5, nc.tensor.matmul(g.ps[1][:, 0:P], g.ones[:], g.diag_first, start=True, stop=True))
            step(6, nc.tensor.matmul(g.ps[1][:, P:2 * P], g.ones[:], g.diag_last, start=True, stop=True))
            pe.wait_ge(s_dve, done["counts"])
            step(7, nc.tensor.matmul(g.ps[2][:, 0:R1], g.link_in[:], g.edge_ends[:, 0:R1], start=True, stop=True))
            step(8, nc.tensor.matmul(g.ps[2][:, R1:2 * R1], g.link_out[:], g.edge_ends[:, R1:2 * R1], start=True, stop=True))
            pe.wait_ge(s_dve, done["weights"])
            for i in range(2):
                step(9 + i, nc.tensor.matmul(g.ps[3 + i][:, 0:W], g.bias_rep[i], g.WG[i + 1][:, 0:W], start=True, stop=True))
    ph.end()


def node_rows(g):
    nc = g.nc
    ph = Phase(nc, "rows")
    s_idx, s_sc, s_ga, s_tab, s_fin, s_turn = (ph.sem(n) for n in ("index_copied", "scattered", "gathered", "moved", "done", "turn"))
    with nc.Block() as block:
        @block.gpsimd
        def _(pool):
            def scatter(k, first):
                if not first:
                    pool.wait_ge(s_sc, k * (16 * RING))
                nc.gpsimd.tensor_copy(g.idx_ring[:], g.last_node_i[:, bass.ds(k * RING, RING)])
                nc.gpsimd.tensor_copy(g.row_ring[:], g.tab_row_i[:, bass.ds(k * RING, RING)]).then_inc(s_idx, 1)
                pool.wait_ge(s_idx, k + 1)
                pool.sem_inc(s_turn, 1)
                for j in range(RING):
                    nc.gpsimd.indirect_dma_start(g.tab_dram, bass.IndirectOffsetOnAxis(g.idx_ring[:, j:j + 1], 0),
                                                 g.row_ring[:, j:j + 1], None, bounds_check=N - 1,
                                                 oob_is_err=False).then_inc(s_sc, 16)
            steps = T // (RING)
            scatter(0, True)
            with pool.Fori(1, steps) as k:
                scatter(k, False)
            pool.wait_ge(s_sc, 16 * T)

            def gather(k, first):
                if not first:
                    pool.wait_ge(s_tab, k)
                nc.gpsimd.tensor_copy(g.idx_ring[:], g.src_i[:, bass.ds(k * RING, RING)]).then_inc(s_idx, 1)
                pool.wait_ge(s_idx, k + steps + 1)
                pool.sem_inc(s_turn, 1)
                for j in range(RING):
                    nc.gpsimd.indirect_dma_start(g.row_ring[:, j:j + 1], None, g.tab_dram,
                                                 bass.IndirectOffsetOnAxis(g.idx_ring[:, j:j + 1], 0)).then_inc(s_ga, 16)
            gather(0, True)
            with pool.Fori(1, steps) as k:
                gather(k, False)

        @block.vector
        def _(dve):
            def move(k):
                dve.wait_ge(s_ga, k * (16 * RING) + 16 * RING)
                nc.vector.tensor_copy(g.src_row_i[:, bass.ds(k * RING, RING)], g.row_ring[:]).then_inc(s_tab, 1)
            with dve.Fori(0, T // (RING)) as k:
                move(k)
            dve.wait_ge(s_tab, T // (RING))
            V = nc.vector
            V.tensor_scalar(g.tmpT[:], g.src_row_i[:], -float(N), None, ALU.add).then_inc(s_fin, 1)
            dve.wait_ge(s_fin, 1)
            V.tensor_scalar(g.tmpT2[:], g.tmpT[:], 0.0, float(PAD), ALU.is_lt, ALU.mult).then_inc(s_fin, 1)
            dve.wait_ge(s_fin, 2)
            V.scalar_tensor_tensor(g.tmpT[:], g.tmpT[:], 0.0, g.tmpT2[:], ALU.max, ALU.add).then_inc(s_fin, 1)
            dve.wait_ge(s_fin, 3)
            V.tensor_copy(g.src_slot_i[:], g.tmpT[:]).then_inc(s_fin, 1)
    ph.end()


G4 = 4
CH = G4 * P
NCH = -(-N // CH)
SCH = T // G4


def chunks(g, mode, layer=0):
    nc, ps = g.nc, g.ps
    dense = mode == "nodes"
    ph = Phase(nc, f"{mode}{layer}")
    sems = {}

    def s(name):
        if name not in sems:
            sems[name] = ph.sem(name)
        return sems[name]
    for name in ("load_a0", "load_a1", "load_b0", "load_b1"):
        s(name)
    A, V, ACTE = nc.tensor, nc.vector, nc.scalar
    n_chunks = NCH if dense else SCH

    def rows(table, k, h, last):
        if dense:
            start = N - CH if last and h == 1 else k * (2 * CH) + h * CH
            return table[bass.ds(start, CH), :].rearrange("(p j) f -> p j f", j=G4)
        return table.rearrange("(p t) f -> p t f", t=T)[:, bass.ds(k * (2 * G4) + h * G4, G4), :]

    def slots(t, k, h):
        return t[:, bass.ds(k * (2 * G4) + h * G4, G4)]

    part = (lambda t: t[0:N, :]) if dense else (lambda t: t[N:N + PAD, :])
    loads = {"nodes": [("a", g.X, g.args["x"])],
             "z1": [], "x1": [("a", g.X, g.z1_dram[N:N + PAD, :]), ("b", g.G, g.xd_dram)],
             "x2": [("a", g.Y, g.x1_dram[N:N + PAD, :])], "h": [],
             "x3": [("a", g.X2, g.x2_dram[N:N + PAD, :])]}[mode]
    stores = []
    if mode in ("nodes", "z1"):
        stores.append(("z1", g.Z1, part(g.z1_dram)))
    if mode == "z1":
        stores.append(("xd", g.X, g.xd_dram))
    if mode in ("nodes", "x1"):
        stores.append(("x1", g.Y, part(g.x1_dram)))
    if mode in ("nodes", "x2"):
        stores.append(("x2", g.X2, part(g.x2_dram)))
    if mode in ("nodes", "x3"):
        stores.append(("x3", g.X3, g.x3_dram if dense else g.x3s_dram))
    if mode in ("h", "x3"):
        stores.append(("rows", g.RW, g.gat_dram[0:PAD, :]))
    freed = {"nodes": {"a": "y"}, "x1": {"a": "xT", "b": "y"}, "x2": {"a": "w"}, "x3": {"a": "x3p"}}.get(mode, {})
    ready = {"z1": "z1r", "xd": "xTp", "x1": "x1", "x2": "x2", "x3": "x3", "rows": "rw"}

    def over(eng, body):
        pairs = n_chunks // 2
        body(0, (0, 1), True, False)
        if n_chunks % 2:
            with eng.Fori(1, pairs) as k:
                body(k, (0, 1), False, False)
            body(pairs, (0,), False, True)
        else:
            with eng.Fori(1, pairs - 1) as k:
                body(k, (0, 1), False, False)
            body(pairs - 1, (0, 1), False, True)

    def after(eng, name, k, h):
        eng.wait_ge(s(name), k * 2 + h + 1)

    def before(eng, name, k, h, first):
        if not first:
            eng.wait_ge(s(name), k * 2 + h - 1)

    def loaded(eng, which, k, h):
        eng.wait_ge(s(f"load_{which}{h}"), k * 16 + 16)

    def stored(eng, name, k, h, first):
        if not first:
            eng.wait_ge(s(f"store_{name}{h}"), k * 16)

    with nc.Block() as block:
        @block.sync
        def _(sp):
            if mode == "h":
                sp.dma_start(g.gat_dram[PAD:PAD + 1, :], g.const_row[layer][:]).then_inc(s("const_row"), 16)

            def load(k, hs, first, last):
                for h in hs:
                    for which, buf, table in loads:
                        before(sp, freed[which], k, h, first)
                        sp.sem_inc(s("turn_sp"), 1)
                        sp.dma_start(buf[h][:], rows(table, k, h, last)).then_inc(s(f"load_{which}{h}"), 16)

            def body(k, hs, first, last):
                load(k, hs, first, last)
                for name, buf, table in stores:
                    for h in hs:
                        after(sp, ready[name], k, h)
                        sp.sem_inc(s("turn_sp"), 1)
                        if dense and last and h == 1:
                            sp.wait_ge(s(f"store_{name}0"), 16 * (n_chunks // 2))
                        sp.dma_start(rows(table, k, h, last), buf[h][:]).then_inc(s(f"store_{name}{h}"), 16)
            over(sp, body)
            if mode == "h":
                sp.wait_ge(s("const_row"), 16)
            for name, buf, table in stores:
                for h in (0, 1):
                    sp.wait_ge(s(f"store_{name}{h}"), 16 * ((n_chunks + 1 - h) // 2))

        if mode in ("z1", "x3"):
            @block.gpsimd
            def _(pool):
                def body(k, hs, first, last):
                    for h in hs:
                        if mode == "z1":
                            stored(pool, "xd", k, h, first)
                            before(pool, "xT", k, h, first)
                            nc.gpsimd.tensor_copy(g.own_ring[h][:], slots(g.own_i, k, h)).then_inc(s("own"), 1)
                            pool.wait_ge(s("own"), k * 2 + h + 1)
                            pool.sem_inc(s("turn"), 1)
                            for j in range(G4):
                                nc.gpsimd.indirect_dma_start(
                                    g.X[h][:, j, :], None, g.args["x"],
                                    bass.IndirectOffsetOnAxis(g.own_ring[h][:, j:j + 1], 0)).then_inc(s(f"load_a{h}"), 16)
                        else:
                            if not first:
                                pool.wait_ge(s(f"scatter{h}"), k * (16 * G4))
                            nc.gpsimd.tensor_copy(g.own_ring[h][:], slots(g.last_node_i, k, h)).then_inc(s("own"), 1)
                            pool.wait_ge(s("own"), k * 2 + h + 1)
                            after(pool, "x3", k, h)
                            pool.sem_inc(s("turn"), 1)
                            for j in range(G4):
                                nc.gpsimd.indirect_dma_start(
                                    g.x3_dram, bass.IndirectOffsetOnAxis(g.own_ring[h][:, j:j + 1], 0),
                                    g.X3[h][:, j, :], None, bounds_check=N - 1, oob_is_err=False
                                ).then_inc(s(f"scatter{h}"), 16)
                over(pool, body)
                if mode == "x3":
                    for h in (0, 1):
                        pool.wait_ge(s(f"scatter{h}"), 16 * G4 * ((n_chunks + 1 - h) // 2))

        @block.tensor
        def _(pe):
            def transposes(out, src):
                for j in range(G4):
                    ins = A.transpose(out[:, j, :], src[:, j, :], g.ident[:])
                return ins

            def product(out, lhs, weights, bias=None):
                for j in range(G4):
                    if bias is not None:
                        A.matmul(out[:, j, :], g.ones[0:1, :], bias, start=True, stop=False)
                    ins = A.matmul(out[:, j, :], lhs[:, j, :], weights, start=bias is None, stop=True)
                return ins

            def body(k, hs, first, last):
                if mode in ("nodes", "z1", "x1"):
                    for h in hs:
                        if mode == "z1":
                            pe.wait_ge(s(f"load_a{h}"), k * (16 * G4) + 16 * G4)
                            before(pe, "z1r", k, h, first)
                        else:
                            loaded(pe, "a", k, h)
                        if mode == "x1":
                            before(pe, "y", k, h, first)
                        transposes(g.psT[h], g.X[h]).then_inc(s("xTp"), 1)
                if mode in ("nodes", "z1"):
                    for h in hs:
                        after(pe, "xT", k, h)
                        if dense:
                            before(pe, "v", k, h, first)
                            A.matmul(g.psL[h][:, 0:512], g.root1[:], g.XT[h][:].rearrange("p j f -> p (j f)"),
                                     start=True, stop=True).then_inc(s("z1Tp"), 1)
                        product(g.psL[h][:, 512:1024].rearrange("p (j f) -> p j f", j=G4), g.XT[h], g.root1[:],
                                g.b1_row[:]).then_inc(s("z1p"), 1)
                if mode in ("nodes", "x1"):
                    for h in hs:
                        after(pe, "z1T" if dense else "xT", k, h)
                        product(g.psT[h], g.Z1T[h] if dense else g.XT[h], g.root2[:], g.b2_row[:]).then_inc(s("z2p"), 1)
                if mode in ("nodes", "x2"):
                    for h in hs:
                        if dense:
                            after(pe, "x1", k, h)
                        else:
                            loaded(pe, "a", k, h)
                            if not first:
                                before(pe, "adT", k, h, first)
                        transposes(g.psT[h], g.Y[h]).then_inc(s("x1Tp"), 1)
                    if mode == "x2":
                        for h in hs:
                            after(pe, "mean", k, h)
                            before(pe, "ad", k, h, first)
                            transposes(g.psM[h], g.M[h]).then_inc(s("mTp"), 1)
                    for h in hs:
                        after(pe, "x1T", k, h)
                        L = g.psL[h][:].rearrange("p (j w) -> p j w", j=G4)
                        if mode == "x2":
                            after(pe, "mT", k, h)
                            before(pe, "v", k, h, first)
                        for j in range(G4):
                            A.matmul(L[:, j, :], g.ones[0:1, :], g.bias_gate[:] if dense else g.bias_gate_n[:],
                                     start=True, stop=False)
                            ins = A.matmul(L[:, j, :], g.XT[h][:, j, :], g.A_gate[:], start=False, stop=dense)
                            if not dense:
                                ins = A.matmul(L[:, j, :], g.MT[h][:, j, :], g.B_gate[:], start=False, stop=True)
                        ins.then_inc(s("Lp"), 1)
                if mode == "x2":
                    for h in hs:
                        after(pe, "x2", k, h)
                        transposes(g.psT[h], g.X2[h]).then_inc(s("adTp"), 1)
                    for h in hs:
                        after(pe, "adT", k, h)
                        for j in range(G4):
                            ins = A.matmul(g.psM[h][:, j, 0:H], g.XT[h][:, j, :], g.vd[0][:], start=True, stop=True)
                        ins.then_inc(s("adp"), 1)
                if mode in ("h", "x3"):
                    src, wts, wd = (g.Y, g.WG[layer + 1], W + H) if mode == "h" else (g.X3, g.WH, W)
                    for h in hs:
                        after(pe, "hr" if mode == "h" else "x3", k, h)
                        transposes(g.psT[h], src[h]).then_inc(s("hTp"), 1)
                    for h in hs:
                        after(pe, "hT", k, h)
                        before(pe, "rw", k, h, first)
                        L = g.psL[h][:].rearrange("p (j w) -> p j w", j=G4)
                        for j in range(G4):
                            ins = A.matmul(L[:, j, 0:wd], g.XT[h][:, j, :], wts[:], start=True, stop=True)
                        ins.then_inc(s("rwp"), 1)
            over(pe, body)

        @block.scalar
        def _(act):
            def copy(out, src, name):
                ACTE.activation(out, src, ACT.Copy).then_inc(s(name), 1)

            def rstd(k, hs, t):
                for h in hs:
                    after(act, f"mv{t}", k, h)
                    ACTE.activation(g.lnv[h][:], g.mv[h][:, :, 1], ACT.Ln, bias=g.eps[:, 0:1]).then_inc(s(f"ln{t}"), 1)
                for h in hs:
                    after(act, f"ln{t}", k, h)
                    ACTE.activation(g.rs[h][:], g.lnv[h][:], ACT.Exp, scale=-0.5).then_inc(s(f"rs{t}"), 1)

            def body(k, hs, first, last):
                if mode in ("nodes", "z1", "x1"):
                    for h in hs:
                        after(act, "xTp", k, h)
                        copy(g.XT[h][:], g.psT[h][:], "xT")
                if dense:
                    for h in hs:
                        after(act, "z1Tp", k, h)
                        ACTE.activation(g.Z1T[h][:].rearrange("p j f -> p (j f)"), g.psL[h][:, 0:512], ACT.Relu,
                                        bias=g.b1_col[:, 0:1]).then_inc(s("z1T"), 1)
                if mode in ("nodes", "x1"):
                    rstd(k, hs, "a")
                if mode in ("nodes", "x2"):
                    for h in hs:
                        after(act, "x1Tp", k, h)
                        copy(g.XT[h][:], g.psT[h][:], "x1T")
                    if mode == "x2":
                        for h in hs:
                            after(act, "mTp", k, h)
                            copy(g.MT[h][:], g.psM[h][:], "mT")
                    for h in hs:
                        after(act, "Lp", k, h)
                        p = g.psL[h][:].rearrange("p (j w) -> p j w", j=G4)[:, :, D:2 * D]
                        ACTE.activation(g.G[h][:], p, ACT.Exp, scale=-1.0).then_inc(s("g1"), 1)
                    for h in hs:
                        after(act, "g1", k, h)
                        ACTE.activation(g.G[h][:], g.G[h][:], ACT.Ln, bias=g.ones[:, 0:1]).then_inc(s("g2"), 1)
                    for h in hs:
                        after(act, "g2", k, h)
                        ACTE.activation(g.G[h][:], g.G[h][:], ACT.Exp, scale=-1.0).then_inc(s("g"), 1)
                    rstd(k, hs, "b")
                    rstd(k, hs, "c")
                if mode in ("nodes", "x3"):
                    rstd(k, hs, "d")
                if mode == "x2":
                    for h in hs:
                        after(act, "adTp", k, h)
                        copy(g.XT[h][:], g.psT[h][:], "adT")
                    for h in hs:
                        after(act, "adp", k, h)
                        copy(slots(g.ad, k, h), g.psM[h][:, :, 0:H], "ad")
                if mode in ("h", "x3"):
                    for h in hs:
                        after(act, "hTp", k, h)
                        copy(g.XT[h][:], g.psT[h][:], "hT")
                    for h in hs:
                        after(act, "rwp", k, h)
                        stored(act, "rows", k, h, first)
                        L = g.psL[h][:].rearrange("p (j w) -> p j w", j=G4)
                        ACTE.activation(g.RW[h][:], L[:, :, 0:W], ACT.Copy)
                        copy(slots(g.ad, k, h), L[:, :, W:W + H] if mode == "h" else L[:, :, D:W], "rw")
            over(act, body)

        @block.vector
        def _(dve):
            def norm(k, hs, t, src, dst, name, save=None, first=None):
                for h in hs:
                    for j in range(G4):
                        ins = V.bn_stats(g.st[h][:, j, :], src[h][:, j, :])
                    ins.then_inc(s(f"st{t}"), 1)
                for h in hs:
                    after(dve, f"st{t}", k, h)
                    dve.sem_inc(s("turn_dve"), 1)
                    for j in range(G4):
                        ins = V.bn_aggr(g.mv[h][:, j, :], g.st[h][:, j, :])
                    ins.then_inc(s(f"mv{t}"), 1)
                for h in hs:
                    after(dve, f"rs{t}", k, h)
                    if save:
                        stored(dve, save, k, h, first)
                    for j in range(G4):
                        ins = V.tensor_scalar(dst[h][:, j, :], src[h][:, j, :], g.mv[h][:, j, 0:1], g.rs[h][:, j:j + 1],
                                              ALU.subtract, ALU.mult)
                    ins.then_inc(s(name), 1)

            def sums_with_carry(dst, k, h):
                for j in range(G4):
                    t = k * (2 * G4) + h * G4 + j
                    ins = V.scalar_tensor_tensor(dst[h][:, j, :], g.carry[:], g.in_first[:, bass.ds(t, 1)],
                                                 g.sums[:, bass.ds(t * W, D)], ALU.mult, ALU.add)
                return ins

            def spread(row):
                return row[:, None, :].to_broadcast([P, G4, D])

            def body(k, hs, first, last):
                if mode == "z1":
                    for h in hs:
                        before(dve, "z1r", k, h, first)
                        sums_with_carry(g.M, k, h).then_inc(s("agg"), 1)
                    for h in hs:
                        after(dve, "agg", k, h)
                        after(dve, "z1p", k, h)
                        V.tensor_tensor(g.M[h][:], g.M[h][:], g.psL[h][:, 512:1024].rearrange("p (j f) -> p j f", j=G4),
                                        ALU.add).then_inc(s("z1q"), 1)
                    for h in hs:
                        after(dve, "z1q", k, h)
                        stored(dve, "z1", k, h, first)
                        V.tensor_scalar(g.Z1[h][:], g.M[h][:], 0.0, None, ALU.max).then_inc(s("z1r"), 1)
                if dense:
                    for h in hs:
                        after(dve, "z1p", k, h)
                        stored(dve, "z1", k, h, first)
                        V.tensor_scalar(g.Z1[h][:], g.psL[h][:, 512:1024].rearrange("p (j f) -> p j f", j=G4), 0.0, None,
                                        ALU.max).then_inc(s("z1r"), 1)
                    for h in hs:
                        after(dve, "z2p", k, h)
                        stored(dve, "x1", k, h, first)
                        V.scalar_tensor_tensor(g.Y[h][:], g.psT[h][:], 0.0, g.X[h][:], ALU.max, ALU.add).then_inc(s("y"), 1)
                if mode == "x1":
                    for h in hs:
                        before(dve, "y", k, h, first)
                        sums_with_carry(g.M, k, h).then_inc(s("agg"), 1)
                    for h in hs:
                        after(dve, "agg", k, h)
                        after(dve, "z2p", k, h)
                        V.tensor_tensor(g.M[h][:], g.M[h][:], g.psT[h][:], ALU.add).then_inc(s("z2q"), 1)
                    for h in hs:
                        after(dve, "z2q", k, h)
                        loaded(dve, "b", k, h)
                        stored(dve, "x1", k, h, first)
                        V.scalar_tensor_tensor(g.Y[h][:], g.M[h][:], 0.0, g.G[h][:], ALU.max, ALU.add).then_inc(s("y"), 1)
                if mode in ("nodes", "x1"):
                    for h in hs:
                        after(dve, "y", k, h)
                    norm(k, hs, "a", g.Y, g.Y, "x1")
                if mode == "x2":
                    for h in hs:
                        before(dve, "mTp", k, h, first)
                        sums_with_carry(g.M, k, h).then_inc(s("agg"), 1)
                    for h in hs:
                        after(dve, "agg", k, h)
                        V.tensor_tensor(g.M[h][:], g.M[h][:], slots(g.rcnt, k, h)[:, :, None].to_broadcast([P, G4, D]),
                                        ALU.mult).then_inc(s("mean"), 1)
                if mode in ("nodes", "x2"):
                    for h in hs:
                        after(dve, "g", k, h)
                        Dl = g.psL[h][:].rearrange("p (j w) -> p j w", j=G4)[:, :, 0:D]
                        V.tensor_tensor(g.V[h][:], g.G[h][:], Dl, ALU.mult).then_inc(s("v"), 1)
                    for h in hs:
                        after(dve, "v", k, h)
                        V.tensor_tensor(g.V[h][:], g.V[h][:], g.Y[h][:], ALU.add).then_inc(s("v2"), 1)
                    for h in hs:
                        after(dve, "v2", k, h)
                    norm(k, hs, "b", g.V, g.V, "vn")
                    for h in hs:
                        after(dve, "vn", k, h)
                        V.tensor_tensor(g.V[h][:], g.V[h][:], spread(g.gamma), ALU.mult).then_inc(s("vg"), 1)
                    for h in hs:
                        after(dve, "vg", k, h)
                        V.tensor_tensor(g.V[h][:], g.V[h][:], spread(g.beta), ALU.add).then_inc(s("vb"), 1)
                    for h in hs:
                        after(dve, "vb", k, h)
                        V.scalar_tensor_tensor(g.V[h][:], g.V[h][:], 0.0, g.Y[h][:], ALU.max, ALU.add).then_inc(s("w"), 1)
                    for h in hs:
                        after(dve, "w", k, h)
                    norm(k, hs, "c", g.V, g.X2, "x2", "x2", first)
                if dense:
                    for h in hs:
                        after(dve, "x2", k, h)
                        stored(dve, "x3", k, h, first)
                        V.tensor_tensor(g.X3[h][:], g.X2[h][:], spread(g.gat_bias[2]), ALU.add).then_inc(s("x3p"), 1)
                if mode == "h":
                    for h in hs:
                        before(dve, "hTp", k, h, first)
                        sums_with_carry(g.Y, k, h).then_inc(s("agg"), 1)
                    for h in hs:
                        after(dve, "agg", k, h)
                        V.tensor_tensor(g.Y[h][:], g.Y[h][:], spread(g.gat_bias[layer]), ALU.add).then_inc(s("hp"), 1)
                    for h in hs:
                        after(dve, "hp", k, h)
                        V.tensor_scalar(g.Y[h][:], g.Y[h][:], 0.0, None, ALU.max).then_inc(s("hr"), 1)
                if mode == "x3":
                    for h in hs:
                        stored(dve, "x3", k, h, first)
                        before(dve, "hTp", k, h, first)
                        if not first:
                            dve.wait_ge(s(f"scatter{h}"), k * (16 * G4))
                        sums_with_carry(g.X3, k, h).then_inc(s("agg"), 1)
                    for h in hs:
                        after(dve, "agg", k, h)
                        V.tensor_tensor(g.X3[h][:], g.X3[h][:], spread(g.gat_bias[2]), ALU.add).then_inc(s("hp"), 1)
                    for h in hs:
                        after(dve, "hp", k, h)
                        loaded(dve, "a", k, h)
                        V.tensor_tensor(g.X3[h][:], g.X3[h][:], g.X2[h][:], ALU.add).then_inc(s("x3p"), 1)
                if mode in ("nodes", "x3"):
                    for h in hs:
                        after(dve, "x3p", k, h)
                    norm(k, hs, "d", g.X3, g.X3, "x3")
            over(dve, body)
    ph.end()


FT = H * T


def gather(g, mode, layer=0):
    nc, A, V, ACTE = g.nc, g.nc.tensor, g.nc.vector, g.nc.scalar
    ph = Phase(nc, f"{mode}{layer}g")
    sems = {}

    def s(name):
        if name not in sems:
            sems[name] = ph.sem(name)
        return sems[name]
    table, index, width = {
        "conv": (g.z1_dram if layer else g.args["x"], g.src_row_i if layer else g.src_i, D),
        "mean": (g.x1_dram, g.src_row_i, D), "first": (g.x2_dram, g.src_row_i, D),
        "rows": (g.gat_dram, g.src_slot_i, W), "left": (g.x3_dram, g.src_i, D)}[mode]
    steps = T // RING
    used = {"conv": "tp", "mean": "sum", "first": "tp", "rows": "put", "left": "tp"}[mode]

    def over(eng, body):
        body(0, True)
        with eng.Fori(1, steps) as k:
            body(k, False)

    def after(eng, name, k, j, back=0):
        eng.wait_ge(s(name), k * RING + j + 1 - back)

    def row_of(k, j, shift=0, width=D):
        return g.sums_all[:, bass.ds((k * RING + j + shift) * W, width)]

    with nc.Block() as block:
        @block.gpsimd
        def _(pool):
            def body(k, first):
                if not first:
                    for j in range(RING):
                        pool.wait_ge(s(f"row{j}"), k * 16)
                nc.gpsimd.tensor_copy(g.idx_ring[:, 0:RING], index[:, bass.ds(k * RING, RING)]).then_inc(s("index"), 1)
                pool.wait_ge(s("index"), k + 1)
                for j in range(RING):
                    if not first:
                        pool.wait_ge(s(used), k * RING + (j + 1 - RING))
                    pool.sem_inc(s("turn"), 1)
                    nc.gpsimd.indirect_dma_start(g.ring[j][:, 0:width], None, table,
                                                 bass.IndirectOffsetOnAxis(g.idx_ring[:, j:j + 1], 0)).then_inc(s(f"row{j}"), 16)
            over(pool, body)

        if mode in ("conv", "first", "left"):
            @block.tensor
            def _(pe):
                def turn(k, first, j):
                    pe.wait_ge(s(f"row{j}"), k * 16 + 16)
                    if not (first and j < 2):
                        after(pe, "t", k, j, 2)
                    A.transpose(g.psT[j % 2][:, 0, :], g.ring[j][:, 0:D], g.ident[:]).then_inc(s("tp"), 1)

                def product(k, first, j):
                    after(pe, "t", k, j)
                    if not (first and j < 2):
                        if mode == "conv":
                            pe.wait_ge(s("part"), (k * RING + (j - 1)) * R)
                        else:
                            after(pe, "read", k, j, 2)
                    out = g.psL[j % 2]
                    if mode == "conv":
                        A.matmul(out[:, 0:512], g.T2[j % 2], g.Wrel[layer][:, 0:512], start=True, stop=True)
                        ins = A.matmul(out[:, 512:1024], g.T2[j % 2], g.Wrel[layer][:, 512:1024], start=True, stop=True)
                    elif mode == "first":
                        ins = A.matmul(out[:, 0:W], g.T2[j % 2], g.WG[0][:, 0:W], start=True, stop=True)
                    else:
                        ins = A.matmul(out[:, 0:H], g.T2[j % 2], g.vleft[:], start=True, stop=True)
                    ins.then_inc(s("prod"), 1)

                def body(k, first):
                    turn(k, first, 0)
                    for j in range(1, RING):
                        turn(k, first, j)
                        product(k, first, j - 1)
                    product(k, first, RING - 1)
                over(pe, body)
                if mode == "conv":
                    pe.wait_ge(s("sum"), T)
                    A.matmul(g.ps[6][:, 0:D], g.link_in[:], g.sums[:, (T - 1) * W:(T - 1) * W + D],
                             start=True, stop=True).then_inc(s("carry"), 1)

            @block.scalar
            def _(act):
                def body(k, first):
                    for j in range(RING):
                        after(act, "tp", k, j)
                        if not (first and j < 2):
                            after(act, "prod", k, j, 2)
                        ACTE.activation(g.T2[j % 2], g.psT[j % 2][:, 0, :], ACT.Copy).then_inc(s("t"), 1)
                over(act, body)

        if mode == "mean":
            @block.tensor
            def _(pe):
                pe.wait_ge(s("sum"), T)
                A.matmul(g.ps[6][:, 0:D], g.link_in[:], g.sums[:, (T - 1) * W:(T - 1) * W + D],
                         start=True, stop=True).then_inc(s("carry"), 1)

        @block.vector
        def _(dve):
            def copy_columns(dst, src, k):
                V.tensor_copy(dst, src).then_inc(s("cols"), 1)
                dve.wait_ge(s("cols"), k + 1)

            def body(k, first):
                if mode in ("conv", "mean"):
                    if not first:
                        dve.wait_ge(s("sum"), k * RING)
                    if mode == "conv":
                        V.tensor_copy(g.w_ring[:], g.w_slot[:, bass.ds(k * RING, RING), :])
                    copy_columns(g.same_ring[:], g.same[:, bass.ds(k * RING, RING)], k)
                for j in range(RING):
                    if mode == "conv":
                        after(dve, "prod", k, j)
                        for r in range(R):
                            p, w = g.psL[j % 2][:, r * D:(r + 1) * D], g.w_ring[:, j, r:r + 1]
                            if r == 0:
                                ins = V.tensor_scalar(g.acc[j % 2], p, w, None, ALU.mult)
                            else:
                                dve.wait_ge(s("part"), (k * RING + j) * R + r)
                                ins = V.scalar_tensor_tensor(g.acc[j % 2], p, w, g.acc[j % 2], ALU.mult, ALU.add)
                            ins.then_inc(s("part"), 1)
                        dve.wait_ge(s("part"), (k * RING + j) * R + R)
                        if not (first and j == 0):
                            after(dve, "sum", k, j, 1)
                        V.scalar_tensor_tensor(row_of(k, j, 1), row_of(k, j), g.same_ring[:, j:j + 1], g.acc[j % 2],
                                               ALU.mult, ALU.add).then_inc(s("sum"), 1)
                    if mode == "mean":
                        dve.wait_ge(s(f"row{j}"), k * 16 + 16)
                        if not (first and j == 0):
                            after(dve, "sum", k, j, 1)
                        V.scalar_tensor_tensor(row_of(k, j, 1), row_of(k, j), g.same_ring[:, j:j + 1], g.ring[j][:, 0:D],
                                               ALU.mult, ALU.add).then_inc(s("sum"), 1)
                    if mode == "rows":
                        dve.wait_ge(s(f"row{j}"), k * 16 + 16)
                        V.tensor_copy(row_of(k, j, 1, W), g.ring[j][:, 0:W]).then_inc(s("put"), 1)
                    if mode == "first":
                        after(dve, "prod", k, j)
                        V.tensor_copy(row_of(k, j, 1, W), g.psL[j % 2][:, 0:W]).then_inc(s("read"), 1)
                    if mode == "left":
                        after(dve, "prod", k, j)
                        V.tensor_copy(g.a_left[:, bass.ds(k * RING + j, 1), :], g.psL[j % 2][:, None, 0:H]).then_inc(s("read"), 1)
            if mode in ("conv", "mean"):
                V.memset(g.sums_all[:, 0:W], 0.0).then_inc(s("zero"), 1)
                dve.wait_ge(s("zero"), 1)
            over(dve, body)
            if mode in ("conv", "mean"):
                dve.wait_ge(s("carry"), 1)
                V.tensor_copy(g.carry[:], g.ps[6][:, 0:D]).then_inc(s("zero"), 1)
    ph.end()


RMAX = bass.bass_isa.ReduceOp.max


def attention(g, layer):
    nc, A, V, ACTE = g.nc, g.nc.tensor, g.nc.vector, g.nc.scalar
    final = layer == 3
    ph = Phase(nc, f"att{layer}")
    s_dve, s_pe, s_exp, s_max, s_mul, s_sum, s_col, s_zero = (
        ph.sem(n) for n in ("dve_steps", "pe_steps", "exp", "greatest", "weighed", "sum", "columns", "zero"))
    heads = lambda t: t.rearrange("p (h t) -> p h t", h=H)
    q = g.att
    reached = []
    with nc.Block() as block:
        @block.scalar
        def _(act):
            act.wait_ge(s_max, 2 if final else 1)
            ACTE.activation(q.e, q.e, ACT.Exp).then_inc(s_exp, 1)

        if final:
            @block.gpsimd
            def _(pool):
                pool.wait_ge(s_max, 1)
                nc.gpsimd.partition_all_reduce(q.gmax, q.pmax, P, RMAX).then_inc(s_mul, 1)

        @block.vector
        def _(dve):
            n = [0]

            def link(ins):
                n[0] += 1
                ins.then_inc(s_dve, 1)
                dve.wait_ge(s_dve, n[0])

            def wide(t):
                return t[:, None, :].to_broadcast([P, H, T])

            def segment_sum(v, out, pe_step):
                link(V.tensor_tensor_scan(q.fwd, q.same, v, 0.0, ALU.mult, ALU.add))
                link(V.tensor_tensor_scan(q.bwd[:, ::-1], q.next[:, ::-1], v[:, ::-1], 0.0, ALU.mult, ALU.add))
                link(V.tensor_copy(q.ends[:, 0:H], heads(q.fwd)[:, :, T - 1]))
                link(V.tensor_copy(q.ends[:, H:2 * H], heads(q.bwd)[:, :, 0]))
                reached.append(n[0])
                link(V.tensor_tensor(q.fwd, q.fwd, q.bwd, ALU.add))
                link(V.tensor_tensor(out, q.fwd, v, ALU.subtract))
                dve.wait_ge(s_pe, pe_step)
                link(V.tensor_copy(q.ends, g.ps[0][:, 0:2 * H]))
                for h in range(H):
                    oh = heads(out)[:, h, :]
                    link(V.scalar_tensor_tensor(oh, g.in_first[:], q.ends[:, h:h + 1], oh, ALU.mult, ALU.add))
                    link(V.scalar_tensor_tensor(oh, g.in_last[:], q.ends[:, H + h:H + h + 1], oh, ALU.mult, ALU.add))

            link(V.tensor_copy(heads(q.same), wide(g.same[:, 0:T])))
            link(V.tensor_copy(heads(q.next), wide(g.same[:, 1:T + 1])))
            link(V.tensor_tensor(heads(q.v), g.ad[:].rearrange("p t h -> p h t"), wide(g.is_last[:]), ALU.mult))
            segment_sum(q.v, q.e, 1)
            left = (g.a_left[:] if final else g.sums.rearrange("p (t w) -> p t w", w=W)[:, :, D:W]).rearrange("p t h -> p h t")
            link(V.tensor_tensor(heads(q.e), heads(q.e), left, ALU.add))
            link(V.scalar_tensor_tensor(q.e, q.e, 0.2, q.e, ALU.mult, ALU.max))
            if final:
                link(V.tensor_scalar(g.tmpT[:], g.dstf[:, 1:T + 1], float(N), -1e30, ALU.is_equal, ALU.mult))
                link(V.tensor_tensor(heads(q.e), heads(q.e), wide(g.tmpT[:]), ALU.add))
                link(V.tensor_reduce(q.pmax, q.e, AX_X, ALU.max))
                dve.sem_inc(s_max, 1)
                dve.wait_ge(s_mul, 1)
                V.tensor_scalar(q.e, q.e, q.gmax[:, 0:1], None, ALU.subtract).then_inc(s_max, 1)
                dve.wait_ge(s_exp, 1)
                link(V.tensor_copy(g.ad[:].rearrange("p t h -> p h t"), heads(q.e)))
                return
            link(V.tensor_scalar(q.same, q.same, 1e30, -1e30, ALU.mult, ALU.add))
            link(V.tensor_scalar(q.next, q.next, 1e30, -1e30, ALU.mult, ALU.add))
            link(V.tensor_tensor_scan(q.fwd, q.same, q.e, -1e30, ALU.add, ALU.max))
            link(V.tensor_tensor_scan(q.bwd[:, ::-1], q.next[:, ::-1], q.e[:, ::-1], -1e30, ALU.add, ALU.max))
            for h in range(H):
                c = slice(h * P, (h + 1) * P)
                link(V.tensor_scalar(q.diag_in[:, c], g.ident[:], heads(q.fwd)[:, h, T - 1:T], None, ALU.mult))
                link(V.tensor_scalar(q.diag_out[:, c], g.ident[:], heads(q.bwd)[:, h, 0:1], None, ALU.mult))
            reached.append(n[0])
            link(V.tensor_tensor(q.v, q.fwd, q.bwd, ALU.max))
            dve.wait_ge(s_pe, 2)
            for bank, mask, col in ((1, g.no_in, 0), (2, g.no_out, H)):
                both = q.diag_in.rearrange("p (h k) -> p h k", h=H)
                link(V.tensor_tensor(both, g.ps[bank].rearrange("p (h k) -> p h k", h=H),
                                     mask[:, None, :].to_broadcast([P, H, P]), ALU.add))
                link(V.tensor_reduce(q.ends[:, col:col + H], both, AX_X, ALU.max))
            link(V.tensor_scalar(g.tmpT[:], g.in_first[:], 1e30, -1e30, ALU.mult, ALU.add))
            link(V.tensor_scalar(g.tmpT2[:], g.in_last[:], 1e30, -1e30, ALU.mult, ALU.add))
            for h in range(H):
                vh = heads(q.v)[:, h, :]
                link(V.scalar_tensor_tensor(vh, g.tmpT[:], q.ends[:, h:h + 1], vh, ALU.add, ALU.max))
                link(V.scalar_tensor_tensor(vh, g.tmpT2[:], q.ends[:, H + h:H + h + 1], vh, ALU.add, ALU.max))
            V.tensor_tensor(q.e, q.e, q.v, ALU.subtract).then_inc(s_max, 1)
            link(V.tensor_copy(heads(q.same), wide(g.same[:, 0:T])))
            link(V.tensor_copy(heads(q.next), wide(g.same[:, 1:T + 1])))
            dve.wait_ge(s_exp, 1)
            segment_sum(q.e, q.v, 3)
            link(V.tensor_scalar(q.v, q.v, 1e-16, None, ALU.add))
            link(V.reciprocal(q.v, q.v))
            link(V.tensor_tensor(q.e, q.e, q.v, ALU.mult))
            link(V.memset(g.sums_all[:, 0:W], 0.0))
            alpha = q.e.rearrange("p (h t) -> p t h", h=H)

            def body(k, first):
                if not first:
                    dve.wait_ge(s_sum, k * RING)
                V.tensor_copy(g.same_ring[:], g.same[:, bass.ds(k * RING, RING)]).then_inc(s_col, 1)
                part = g.sums[:, bass.ds(k * (RING * W), RING * W)].rearrange("p (t w) -> p t w", w=W)[:, :, 0:D] \
                    .rearrange("p t (h c) -> p t h c", h=H)
                V.tensor_tensor(part, part, alpha[:, bass.ds(k * RING, RING), :, None].to_broadcast([P, RING, H, C]),
                                ALU.mult).then_inc(s_mul, 1)
                dve.wait_ge(s_col, k + 1)
                dve.wait_ge(s_mul, k + 1)
                for j in range(RING):
                    if not (first and j == 0):
                        dve.wait_ge(s_sum, k * RING + j)
                    at = lambda shift: g.sums_all[:, bass.ds((k * RING + j + shift) * W, D)]
                    V.scalar_tensor_tensor(at(1), at(0), g.same_ring[:, j:j + 1], at(1), ALU.mult, ALU.add).then_inc(s_sum, 1)
            body(0, True)
            with dve.Fori(1, T // RING) as k:
                body(k, False)
            dve.wait_ge(s_pe, 4)
            V.tensor_copy(g.carry[:], g.ps[6][:, 0:D]).then_inc(s_zero, 1)

        @block.tensor
        def _(pe):
            def links(n, sem_at):
                pe.wait_ge(s_dve, sem_at)
                A.matmul(g.ps[0][:, 0:H], g.link_in[:], q.ends[:, 0:H], start=True, stop=True)
                A.matmul(g.ps[0][:, H:2 * H], g.link_out[:], q.ends[:, H:2 * H], start=True, stop=True).then_inc(s_pe, 1)
            links(1, reached[0])
            if final:
                return
            pe.wait_ge(s_dve, reached[1])
            A.matmul(g.ps[1], g.ones[:], q.diag_in, start=True, stop=True)
            A.matmul(g.ps[2], g.ones[:], q.diag_out, start=True, stop=True).then_inc(s_pe, 1)
            links(3, reached[2])
            pe.wait_ge(s_sum, T)
            A.matmul(g.ps[6][:, 0:D], g.link_in[:], g.sums[:, (T - 1) * W:(T - 1) * W + D],
                     start=True, stop=True).then_inc(s_pe, 1)
    ph.end()


def by_source(g):
    nc, A, V, ACTE = g.nc, g.nc.tensor, g.nc.vector, g.nc.scalar
    ph = Phase(nc, "bysrc")
    sems = {}

    def s(name):
        if name not in sems:
            sems[name] = ph.sem(name)
        return sems[name]
    B = G4
    steps = T // B

    def over(eng, body):
        body(0, True)
        with eng.Fori(1, steps) as k:
            body(k, False)

    def after(eng, name, k, j, back=0):
        eng.wait_ge(s(name), k * B + j + 1 - back)
    with nc.Block() as block:
        @block.gpsimd
        def _(pool):
            def body(k, first):
                if first != "all":
                    for j in range(B):
                        pool.wait_ge(s(f"row{j}"), k * 16)
                nc.gpsimd.tensor_copy(g.idx_ring[:, 0:B], g.dst_slot_i[:, bass.ds(k * B, B)]).then_inc(s("index"), 1)
                pool.wait_ge(s("index"), k + 1)
                for j in range(B):
                    if first != "all":
                        after(pool, "msg", k, j, B)
                    pool.sem_inc(s("turn"), 1)
                    nc.gpsimd.indirect_dma_start(g.ring[j][:, 0:W], None, g.gat_dram,
                                                 bass.IndirectOffsetOnAxis(g.idx_ring[:, j:j + 1], 0)).then_inc(s(f"row{j}"), 16)
                    if first != "all":
                        add(k - 1, j, first)

            def add(k, j, first):
                after(pool, "sum", k, j)
                after(pool, "index_out", k, j)
                if not (first and j == 0):
                    pool.wait_ge(s("added"), (k * B + j) * 16)
                pool.sem_inc(s("turn"), 1)
                nc.gpsimd.indirect_dma_start(g.U_dram, bass.IndirectOffsetOnAxis(g.add_row[j][:, 0:1], 0), g.RS[j], None,
                                             compute_op=ALU.add).then_inc(s("added"), 16)
            body(0, "all")
            body(1, True)
            with pool.Fori(2, steps) as k:
                body(k, False)
            for j in range(B):
                add(steps - 1, j, False)
            pool.wait_ge(s("added"), 16 * T)

        @block.tensor
        def _(pe):
            def body(k, first):
                for j in range(B):
                    after(pe, "diag", k, j)
                    if not first or j >= 2:
                        after(pe, "same_src", k, j, 2)
                    A.matmul(g.ps[j % 2][:, 0:P], g.ones[:], g.diag[j % 2], start=True, stop=True).then_inc(s("srcrow"), 1)
                    after(pe, "same_src", k, j)
                    after(pe, "msg", k, j)
                    if not first or j >= 2:
                        after(pe, "sum", k, j, 2)
                    A.matmul(g.ps[2 + j % 2][:, 0:W], g.Sm[j % 2], g.msg[j % 2], start=True, stop=True).then_inc(s("sump"), 1)
            over(pe, body)

        @block.scalar
        def _(act):
            def body(k, first):
                for j in range(B):
                    after(act, "sump", k, j)
                    if not first:
                        act.wait_ge(s("added"), (k * B + (j + 1 - B)) * 16)
                    ACTE.activation(g.RS[j], g.ps[2 + j % 2][:, 0:W], ACT.Copy).then_inc(s("sum"), 1)
            over(act, body)

        @block.vector
        def _(dve):
            V.tensor_copy(g.tmpT[:], g.src_i[:]).then_inc(s("pre"), 1)
            V.tensor_copy(g.spare[:], g.spare_i[:]).then_inc(s("pre"), 1)
            dve.wait_ge(s("pre"), 2)
            V.tensor_scalar(g.tmpT2[:], g.dstf[:, 1:T + 1], float(N), g.spare[:, 0:1], ALU.is_equal, ALU.mult).then_inc(s("pre"), 1)
            dve.wait_ge(s("pre"), 3)
            V.tensor_tensor(g.tmpT[:], g.tmpT[:], g.tmpT2[:], ALU.add).then_inc(s("pre"), 1)
            dve.wait_ge(s("pre"), 4)

            def body(k, first):
                V.tensor_copy(g.src_cols[:], g.tmpT[:, bass.ds(k * B, B)])
                V.tensor_copy(g.ex_cols[:], g.ad[:, bass.ds(k * B, B), :]).then_inc(s("cols"), 1)
                dve.wait_ge(s("cols"), k + 1)
                for j in range(B):
                    src = g.src_cols[:, j:j + 1]
                    if not first or j >= 2:
                        after(dve, "srcrow", k, j, 2)
                    V.tensor_scalar(g.diag[j % 2], g.ident[:], src, None, ALU.mult).then_inc(s("diag"), 1)
                    dve.wait_ge(s(f"row{j}"), k * 16 + 16)
                    if not first or j >= 2:
                        after(dve, "sump", k, j, 2)
                    V.tensor_tensor(g.msg[j % 2][:, 0:D].rearrange("p (h c) -> p h c", h=H),
                                    g.ring[j][:, 0:D].rearrange("p (h c) -> p h c", h=H),
                                    g.ex_cols[:, j, :, None].to_broadcast([P, H, C]), ALU.mult)
                    V.tensor_copy(g.msg[j % 2][:, D:W], g.ex_cols[:, j, :]).then_inc(s("msg"), 1)
                    after(dve, "srcrow", k, j)
                    V.tensor_scalar(g.Sm[j % 2], g.ps[j % 2][:, 0:P], src, None, ALU.is_equal).then_inc(s("same_src"), 1)
                    after(dve, "same_src", k, j)
                    V.scalar_tensor_tensor(g.dup_tmp, g.Sm[j % 2], 1.0, g.below[:], ALU.mult, ALU.mult,
                                           accum_out=g.dup[:, 0:1]).then_inc(s("dup"), 1)
                    V.tensor_tensor(g.dup[:, 1:2], g.spare[:], src, ALU.subtract).then_inc(s("dup"), 1)
                    after_dup = (k * B + j) * 4
                    dve.wait_ge(s("dup"), after_dup + 2)
                    V.tensor_scalar(g.dup[:, 2:3], g.dup[:, 0:1], 0.5, g.dup[:, 1:2], ALU.is_gt, ALU.mult).then_inc(s("dup"), 1)
                    dve.wait_ge(s("dup"), after_dup + 3)
                    V.tensor_tensor(g.dup[:, 3:4], g.dup[:, 2:3], src, ALU.add).then_inc(s("dup"), 1)
                    dve.wait_ge(s("dup"), after_dup + 4)
                    if not first:
                        dve.wait_ge(s("added"), (k * B + (j + 1 - B)) * 16)
                    V.tensor_copy(g.add_row[j][:], g.dup[:, 3:4]).then_inc(s("index_out"), 1)
            over(dve, body)
    ph.end()


def last_layer(g):
    nc, A, V, ACTE = g.nc, g.nc.tensor, g.nc.vector, g.nc.scalar
    ph = Phase(nc, "last")
    sems = {}

    def s(name):
        if name not in sems:
            sems[name] = ph.sem(name)
        return sems[name]
    pairs = NCH // 2

    def over(eng, body):
        body(0, True, False)
        with eng.Fori(1, pairs - 1) as k:
            body(k, False, False)
        body(pairs - 1, False, True)

    def rows(table, k, h, last):
        start = N - CH if last and h == 1 else k * (2 * CH) + h * CH
        return table[bass.ds(start, CH), :].rearrange("(p j) f -> p j f", j=G4)

    def after(eng, name, k, h):
        eng.wait_ge(s(name), k * 2 + h + 1)

    def before(eng, name, k, h, first):
        if not first:
            eng.wait_ge(s(name), k * 2 + h - 1)
    with nc.Block() as block:
        @block.sync
        def _(sp):
            def body(k, first, last):
                for h in (0, 1):
                    before(sp, "y", k, h, first)
                    sp.sem_inc(s("turn_sp"), 1)
                    sp.dma_start(g.X[h][:], rows(g.x3_dram, k, h, last)).then_inc(s(f"load_x{h}"), 16)
                    sp.dma_start(g.UB[h][:], rows(g.U_dram, k, h, last)).then_inc(s(f"load_u{h}"), 16)
                for h in (0, 1):
                    after(sp, "o", k, h)
                    sp.sem_inc(s("turn_sp"), 1)
                    if last and h == 1:
                        sp.wait_ge(s("store0"), 16 * pairs)
                    sp.dma_start(rows(g.out, k, h, last), g.Y[h][:]).then_inc(s(f"store{h}"), 16)
            over(sp, body)
            for h in (0, 1):
                sp.wait_ge(s(f"store{h}"), 16 * pairs)

        @block.tensor
        def _(pe):
            def body(k, first, last):
                for h in (0, 1):
                    pe.wait_ge(s(f"load_x{h}"), k * 16 + 16)
                    for j in range(G4):
                        ins = A.transpose(g.psT[h][:, j, :], g.X[h][:, j, :], g.ident[:])
                    ins.then_inc(s("xTp"), 1)
                for h in (0, 1):
                    after(pe, "xT", k, h)
                    before(pe, "u", k, h, first)
                    for j in range(G4):
                        ins = A.matmul(g.psL[h][:, j * D:(j + 1) * D], g.XT[h][:, j, :], g.Wres[:], start=True, stop=True)
                    ins.then_inc(s("up"), 1)
            over(pe, body)

        @block.scalar
        def _(act):
            def body(k, first, last):
                for h in (0, 1):
                    after(act, "xTp", k, h)
                    ACTE.activation(g.XT[h][:], g.psT[h][:], ACT.Copy).then_inc(s("xT"), 1)
                for h in (0, 1):
                    after(act, "neg", k, h)
                    ACTE.activation(g.G[h][:], g.G[h][:], ACT.Exp).then_inc(s("e"), 1)
                for h in (0, 1):
                    after(act, "mv", k, h)
                    ACTE.activation(g.lnv[h][:], g.mv[h][:, :, 1], ACT.Ln, bias=g.eps[:, 0:1]).then_inc(s("ln"), 1)
                for h in (0, 1):
                    after(act, "ln", k, h)
                    ACTE.activation(g.rs[h][:], g.lnv[h][:], ACT.Exp, scale=-0.5).then_inc(s("rs"), 1)
            over(act, body)

        @block.vector
        def _(dve):
            def body(k, first, last):
                for h in (0, 1):
                    dve.wait_ge(s(f"load_u{h}"), k * 16 + 16)
                    V.tensor_scalar(g.den[h][:], g.UB[h][:, :, D:W], 1e-8, None, ALU.add).then_inc(s("d1"), 1)
                for h in (0, 1):
                    after(dve, "d1", k, h)
                    V.reciprocal(g.den[h][:], g.den[h][:]).then_inc(s("d2"), 1)
                for h in (0, 1):
                    after(dve, "d2", k, h)
                    V.tensor_tensor(g.V[h][:].rearrange("p j (h c) -> p j h c", h=H),
                                    g.UB[h][:, :, 0:D].rearrange("p j (h c) -> p j h c", h=H),
                                    g.den[h][:, :, :, None].to_broadcast([P, G4, H, C]), ALU.mult).then_inc(s("agg"), 1)
                for h in (0, 1):
                    after(dve, "agg", k, h)
                    after(dve, "up", k, h)
                    V.tensor_tensor(g.V[h][:].rearrange("p j f -> p (j f)"), g.V[h][:].rearrange("p j f -> p (j f)"),
                                    g.psL[h][:, 0:512], ALU.add).then_inc(s("u"), 1)
                for h in (0, 1):
                    after(dve, "u", k, h)
                    V.tensor_scalar(g.G[h][:], g.V[h][:], 0.0, None, ALU.min).then_inc(s("neg"), 1)
                for h in (0, 1):
                    if not first:
                        dve.wait_ge(s(f"store{h}"), k * 16)
                    V.scalar_tensor_tensor(g.Y[h][:], g.V[h][:], 0.0, g.X[h][:], ALU.max, ALU.add).then_inc(s("y"), 1)
                for h in (0, 1):
                    after(dve, "y", k, h)
                    after(dve, "e", k, h)
                    V.scalar_tensor_tensor(g.Y[h][:], g.G[h][:], -1.0, g.Y[h][:], ALU.add, ALU.add).then_inc(s("z"), 1)
                for h in (0, 1):
                    after(dve, "z", k, h)
                    for j in range(G4):
                        ins = V.bn_stats(g.st[h][:, j, :], g.Y[h][:, j, :])
                    ins.then_inc(s("st"), 1)
                for h in (0, 1):
                    after(dve, "st", k, h)
                    dve.sem_inc(s("turn_dve"), 1)
                    for j in range(G4):
                        ins = V.bn_aggr(g.mv[h][:, j, :], g.st[h][:, j, :])
                    ins.then_inc(s("mv"), 1)
                for h in (0, 1):
                    after(dve, "rs", k, h)
                    for j in range(G4):
                        ins = V.tensor_scalar(g.Y[h][:, j, :], g.Y[h][:, j, :], g.mv[h][:, j, 0:1], g.rs[h][:, j:j + 1],
                                              ALU.subtract, ALU.mult)
                    ins.then_inc(s("o"), 1)
            over(dve, body)
    ph.end()


def build(nc, args, out):
    with ExitStack() as ctx:
        g = Program()
        g.nc, g.args, g.out = nc, args, out

        def sb(name, shape, dt=F32):
            return ctx.enter_context(nc.sbuf_tensor(name, shape, dt))

        def each_slot(name, dt=F32):
            return sb(name, [P, T], dt)

        def dram(name, shape, dt=F32):
            return nc.dram_tensor(name, shape, dt).ap()
        g.tab_dram = dram("tab_dram", (N, 1), I32)
        g.z1_dram, g.x1_dram, g.x2_dram = (dram(n, (N + PAD, D)) for n in ("z1_dram", "x1_dram", "x2_dram"))
        g.xd_dram = dram("xd_dram", (PAD, D))
        g.x3_dram = dram("x3_dram", (N, D))
        g.x3s_dram = dram("x3s_dram", (PAD, D))
        g.gat_dram = dram("gat_dram", (PAD + 1, W))
        g.U_dram = dram("U_dram", (UROWS, W))
        g.ZB, g.ZW = 28, UROWS // P * W // 28
        g.src_i = each_slot("src_i", I32)
        g.dst_i = each_slot("dst_i", I32)
        g.type_i = each_slot("type_i", I32)
        g.slot_i = each_slot("slot_i", I32)
        g.last_node_i = each_slot("last_node_i", I32)
        g.tab_row_i = each_slot("tab_row_i", I32)
        g.src_row_i = each_slot("src_row_i", I32)
        g.src_slot_i = each_slot("src_slot_i", I32)
        g.dst_slot_i = each_slot("dst_slot_i", I32)
        g.own_i = each_slot("own_i", I32)
        g.dst_next_i = sb("dst_next_i", [P, 1], I32)
        g.spare_i = sb("spare_i", [P, 1], I32)
        g.spare = sb("spare", [P, 1])
        g.eps = sb("eps", [P, 1])
        g.idx_ring = sb("idx_ring", [P, RING], I32)
        g.row_ring = sb("row_ring", [P, RING], I32)
        g.dstf = sb("dstf", [P, T + 2])
        g.same = sb("same", [P, T + 1])
        g.typef = each_slot("typef")
        g.is_last = each_slot("is_last")
        g.in_first = each_slot("in_first")
        g.in_last = each_slot("in_last")
        g.tmpT = each_slot("tmpT")
        g.tmpT2 = each_slot("tmpT2")
        g.rcnt = each_slot("rcnt")
        g.w_slot = sb("w_slot", [P, T, R])
        g.ad = sb("ad", [P, T, H])
        g.a_left = sb("a_left", [P, T, H])
        g.ident = sb("ident", [P, P])
        g.ones = sb("ones", [P, P])
        g.below = sb("below", [P, P])
        g.above = sb("above", [P, P])
        g.link_in = sb("link_in", [P, P])
        g.link_out = sb("link_out", [P, P])
        g.no_in = sb("no_in", [P, P])
        g.no_out = sb("no_out", [P, P])
        g.carry = sb("carry", [P, P])
        g.root1 = sb("root1", [P, D])
        g.root2 = sb("root2", [P, D])
        g.Wres = sb("Wres", [P, D])
        g.gamma = sb("gamma", [P, D])
        g.beta = sb("beta", [P, D])
        g.gat_bias = [sb(f"gat_bias{i}", [P, D]) for i in range(3)]
        g.gat_bias_col = sb("gat_bias_col", [P, 2])
        g.Wrel = [sb(f"Wrel{i}", [P, R * D]) for i in range(2)]
        g.WG = [sb(f"WG{i}", [P, W + H]) for i in range(3)]
        g.vd = [g.WG[0][:, W:W + H]]
        g.WH = sb("WH", [P, W])
        g.vleft = sb("vleft", [P, H])
        g.b1_col, g.bself_col, g.bneigh_col = (sb(n, [P, 1]) for n in ("b1_col", "bself_col", "bneigh_col"))
        g.b1_row, g.b2_row = (sb(n, [1, D]) for n in ("b1_row", "b2_row"))
        g.A_gate, g.B_gate = (sb(n, [P, 2 * D]) for n in ("A_gate", "B_gate"))
        g.bias_gate, g.bias_gate_n = (sb(n, [1, 2 * D]) for n in ("bias_gate", "bias_gate_n"))
        g.const_row = [sb(f"const_row{i}", [1, W]) for i in range(2)]
        g.edge_ends = sb("edge_ends", [P, 2 * R1])
        two = lambda name, *shape: [sb(f"{name}{h}", [P, *shape]) for h in range(2)]
        g.st, g.mv, g.rs, g.lnv = two("st", G4, 6), two("mv", G4, 2), two("rs", G4), two("lnv", G4)
        g.den, g.RW = two("den", G4, H), two("RW", G4, W)
        g.own_ring = [sb(f"own_ring{h}", [P, G4], I32) for h in range(2)]
        g.add_row = [sb(f"add_row{j}", [P, 1], I32) for j in range(G4)]
        g.same_ring = sb("same_ring", [P, RING])
        g.w_ring = sb("w_ring", [P, RING, R])
        g.src_cols = sb("src_cols", [P, G4])
        g.ex_cols = sb("ex_cols", [P, G4, H])
        g.dup = sb("dup", [P, 4])
        psT = [ctx.enter_context(nc.psum_tensor(f"psT{h}", [P, G4, D], F32)) for h in range(2)]
        psM = [ctx.enter_context(nc.psum_tensor(f"psM{h}", [P, G4, D], F32)) for h in range(2)]
        psL = [ctx.enter_context(nc.psum_tensor(f"psL{h}", [P, 1024], F32)) for h in range(2)]
        g.psT, g.psM, g.psL = psT, psM, psL
        flat = lambda t: t[:].rearrange("p j f -> p (j f)")
        g.ps = [flat(psT[0]), flat(psT[1]), psL[0][:, 0:512], psL[0][:, 512:1024], psL[1][:, 0:512], psL[1][:, 512:1024],
                flat(psM[0]), flat(psM[1])]
        sums_all = sb("sums_all", [P, (T + 1) * W])
        g.sums_all, g.sums = sums_all, sums_all[:, W:]

        def carver(region):
            at = [0]

            def carve(*shape, dt=F32):
                n = int(np.prod(shape))
                v = region[:, at[0]:at[0] + n]
                at[0] += n
                assert at[0] <= region.shape[1]
                if dt is not F32:
                    v = v.bitcast(dt)
                names = " ".join(f"a{i}" for i in range(len(shape)))
                return v.rearrange(f"p ({names}) -> p {names}", **{f"a{i}": m for i, m in enumerate(shape)}) if len(shape) > 1 else v
            return carve
        carve = carver(sums_all)
        g.wrel, g.cnt_fwd, g.cnt_bwd = (carve(R1, T) for _ in range(3))
        g.diag_first, g.diag_last, g.bself_rep, g.bneigh_rep, g.att_tmp = (carve(D) for _ in range(5))
        g.WgaT, g.W_self, g.W_neigh, g.WselfT, g.WneighT, g.WgbT = (carve(D) for _ in range(6))
        g.bias_rep = [carve(D) for _ in range(2)]
        g.zero_row = carve(g.ZW)
        g.node_iota = carve(400, dt=I32)
        g.bself_row, g.bneigh_row, g.bgate_row = (carve(D)[0:1, :] for _ in range(3))
        g.att_rows = [carve(D) for _ in range(8)]
        g.Wd = [carve(D) for _ in range(3)]
        carve = carver(sums_all)
        g.UB = [carve(G4, W) for _ in range(2)]
        work = sb("work", [P, 2 * 12 * G4 * D])
        carve = carver(work)
        pair = lambda *shape: [carve(*shape) for _ in range(2)]
        g.X, g.XT, g.Z1T, g.Z1, g.Y, g.G = (pair(G4, D) for _ in range(6))
        g.V, g.X2, g.X3, g.M, g.MT = (pair(G4, D) for _ in range(5))
        carve = carver(work)
        q = g.att = Program()
        q.e, q.v, q.fwd, q.bwd, q.same, q.next = (carve(FT) for _ in range(6))
        q.diag_in, q.diag_out, q.ends, q.pmax, q.gmax = carve(H * P), carve(H * P), carve(2 * H), carve(1), carve(1)
        carve = carver(work)
        g.ring = [carve(W) for _ in range(RING)]
        g.T2 = [carve(D) for _ in range(2)]
        g.acc = [carve(D) for _ in range(2)]
        g.RS = [carve(W) for _ in range(G4)]
        g.diag, g.Sm, g.msg = pair(D), pair(D), pair(W)
        g.dup_tmp = carve(D)

        row = lambda ap: ap.rearrange("(a n) -> a n", a=1)
        col = lambda ap: ap.rearrange("(n a) -> n a", a=1)
        spread = lambda ap, at=0: bass.AP(ap.tensor, at, [[0, P], [1, D]])
        L2 = lambda n: args["L2_gnn_" + n]
        g.dst_next_view = bass.AP(args["dst"].tensor, T, [[T, P - 1], [1, 1]])
        g.weight_loads = [
            (g.W_self, args["L1_gnn_W_self"]), (g.W_neigh, args["L1_gnn_W_neigh"]),
            (g.WselfT, args["W_self_T"]), (g.WneighT, args["W_neigh_T"]),
            (g.WgaT, args["W_gate_T"][0:D, :]), (g.WgbT, args["W_gate_T"][D:2 * D, :]),
            (g.bself_col[:], col(args["L1_gnn_b_self"])), (g.bneigh_col[:], col(args["L1_gnn_b_neigh"])),
            (g.bself_row, row(args["L1_gnn_b_self"])), (g.bneigh_row, row(args["L1_gnn_b_neigh"])),
            (g.bgate_row, row(args["L1_gnn_b_gate"])), (g.b1_col[:], col(args["L0_gnn_b1"])),
            (g.b1_row[:], row(args["L0_gnn_b1"])), (g.b2_row[:], row(args["L0_gnn_b2"])),
            (g.root1[:], args["L0_gnn_root1"]), (g.root2[:], args["L0_gnn_root2"]),
            (g.Wres[:], args["L3_gnn_residual_projection"]), (g.WH[:, 0:D], args["L3_gnn_W"]),
            (g.gamma[:], spread(args["L1_gnn_ln_gamma"])), (g.beta[:], spread(args["L1_gnn_ln_beta"])),
            (g.Wrel[0][:].rearrange("p (r f) -> p r f", r=R), args["L0_gnn_W1"].rearrange("r i o -> i r o")),
            (g.Wrel[1][:].rearrange("p (r f) -> p r f", r=R), args["L0_gnn_W2"].rearrange("r i o -> i r o")),
            (g.att_rows[6], spread(args["L3_gnn_A_right"])), (g.att_rows[7], spread(args["L3_gnn_A_left"])),
        ]
        for i in range(3):
            g.weight_loads += [
                (g.WG[i][:, 0:D], L2("Ws")[i]), (g.Wd[i], L2("Wd")[i]), (g.gat_bias[i][:], spread(L2("b"), i * D)),
                (g.att_rows[i], spread(L2("att_s"), i * D)), (g.att_rows[3 + i], spread(L2("att_d"), i * D))]
        for i in range(2):
            g.weight_loads.append((g.gat_bias_col[:, i:i + 1], col(L2("b")[i])))
        g.att_products = []
        for i in range(3):
            g.att_products += [(g.WG[i][:, D:W], g.WG[i][:, 0:D], g.att_rows[i]), (g.WG[i][:, W:W + H], g.Wd[i], g.att_rows[3 + i])]
        g.att_products += [(g.WH[:, D:W], g.WH[:, 0:D], g.att_rows[6]), (g.vleft[:], g.WH[:, 0:D], g.att_rows[7])]
        nc.scalar.preload_act_table_set("natural_log_exp_and_others")
        steps = [
            lambda: setup(g),
            lambda: node_rows(g),
            lambda: chunks(g, "nodes"),
            lambda: gather(g, "conv", 0), lambda: chunks(g, "z1"),
            lambda: gather(g, "conv", 1), lambda: chunks(g, "x1"),
            lambda: gather(g, "mean"), lambda: chunks(g, "x2"),
            lambda: gather(g, "first"), lambda: attention(g, 0), lambda: chunks(g, "h", 0),
            lambda: gather(g, "rows", 1), lambda: attention(g, 1), lambda: chunks(g, "h", 1),
            lambda: gather(g, "rows", 2), lambda: attention(g, 2), lambda: chunks(g, "x3"),
            lambda: gather(g, "left"), lambda: attention(g, 3), lambda: by_source(g),
            lambda: last_layer(g),
        ]
        for step in steps:
            step()


_INS = ["x", "src", "dst", "edge_type_8", "L0_gnn_W1", "L0_gnn_root1", "L0_gnn_b1", "L0_gnn_W2", "L0_gnn_root2",
        "L0_gnn_b2", "L1_gnn_W_self", "L1_gnn_b_self", "L1_gnn_W_neigh", "L1_gnn_b_neigh", "L1_gnn_b_gate",
        "L1_gnn_ln_gamma", "L1_gnn_ln_beta", "L2_gnn_Ws", "L2_gnn_Wd", "L2_gnn_att_s", "L2_gnn_att_d", "L2_gnn_b",
        "L3_gnn_W", "L3_gnn_A_left", "L3_gnn_A_right", "L3_gnn_residual_projection"]
_TRANSPOSED = {"W_self_T": "L1_gnn_W_self", "W_neigh_T": "L1_gnn_W_neigh", "W_gate_T": "L1_gnn_W_gate"}


def kernel(**inputs):
    import numpy as _np
    import concourse.bacc as _bacc
    from concourse import mybir as _mybir
    from concourse.bass_utils import run_bass_kernel_spmd as _run

    nc = _bacc.Bacc("TRN2", target_bir_lowering=False, num_devices=1)
    laid_out = {name: _np.ascontiguousarray(inputs[name]) for name in _INS}
    for name, of in _TRANSPOSED.items():
        laid_out[name] = _np.ascontiguousarray(_np.asarray(inputs[of]).T)
    arrays = {f"in_{name}": a for name, a in laid_out.items()}
    args = {name: nc.dram_tensor(f"in_{name}", a.shape, _mybir.dt.from_np(a.dtype), kind="ExternalInput").ap()
            for name, a in laid_out.items()}
    out = nc.dram_tensor("out", (N, D), F32, kind="ExternalOutput").ap()
    build(nc, args, out)
    r = _run(nc, [arrays], core_ids=[0])
    return r.results[0]["out"]
```

```python
from contextlib import ExitStack

import numpy as np
import concourse.bass as bass
from concourse import mybir

F32 = mybir.dt.float32
I32 = mybir.dt.int32
BF16 = mybir.dt.bfloat16
ALU = mybir.AluOpType
ACT = mybir.ActivationFunctionType
AX_X = mybir.AxisListType.X

P = 128
N = 50000
E = 25000
D = 128
R = 8
H = 4
C = D // H
T = -(-E // P)
PAD = P * T
FULL = E // T
REST = E - FULL * T
R1 = R + 1
W = D + H
UROWS = 392 * P
SKIP = 1 << 20
LN_EPS = 1e-5
RING = 14


class Program:
    pass


class Phase:

    def __init__(self, nc, name):
        self.nc, self.name, self.sems = nc, name, []

    def sem(self, what):
        s = self.nc.alloc_semaphore(f"{self.name}_{what}")
        self.sems.append(s)
        return s

    def end(self):
        self.nc.clear_and_free_semaphores(self.sems)
        self.nc.all_engine_barrier()


def setup(g):
    nc, a = g.nc, g.args
    ph = Phase(nc, "setup")
    s_const, s_edges, s_w, s_dve, s_pe, s_iota, s_tab0, s_zero = (
        ph.sem(n) for n in ("const", "edges_loaded", "weights_loaded", "dve_steps", "pe_steps",
                            "iota", "table_filled", "zeros_stored"))
    src_r = a["src"].rearrange("(p t) -> p t", t=T) if E % T == 0 else None
    done = {}
    with nc.Block() as block:
        @block.sync
        def _(sp):
            sp.wait_ge(s_const, 1)
            for dram, tile in ((a["src"], g.src_i), (a["dst"], g.dst_i), (a["edge_type_8"], g.type_i)):
                sp.dma_start(tile[0:FULL, :], dram[0:FULL * T].rearrange("(p t) -> p t", t=T)).then_inc(s_edges, 16)
                sp.dma_start(tile[FULL:FULL + 1, 0:REST],
                             dram[FULL * T:E].rearrange("(p t) -> p t", t=REST)).then_inc(s_edges, 16)
            with nc.allow_non_contiguous_dma(reason="one value a partition"):
                sp.dma_start(g.dst_next_i[0:P - 1, :],
                             g.dst_next_view).then_inc(s_edges, 16)
            for tile, view in g.weight_loads:
                sp.dma_start(tile, view).then_inc(s_w, 16)
            sp.wait_ge(s_iota, 1)
            sp.dma_start(g.tab_dram.rearrange("(p t) o -> p (t o)", p=125), g.node_iota[0:125, :]).then_inc(s_tab0, 16)
            sp.wait_ge(s_const, 2)
            sp.dma_start(g.U_dram.rearrange("(p b r) w -> p b (r w)", p=P, b=g.ZB),
                         g.zero_row[:, None, :].to_broadcast([P, g.ZB, g.ZW])).then_inc(s_zero, 16)
            sp.wait_ge(s_w, 16 * len(g.weight_loads))
            sp.wait_ge(s_edges, 16 * 7)
            sp.wait_ge(s_tab0, 16)
            sp.wait_ge(s_zero, 16)

        @block.gpsimd
        def _(pool):
            nc.gpsimd.memset(g.src_i[:], 0)
            nc.gpsimd.memset(g.dst_i[:], N)
            nc.gpsimd.memset(g.type_i[:], 0)
            nc.gpsimd.memset(g.dst_next_i[:], -1).then_inc(s_const, 1)
            nc.gpsimd.memset(g.zero_row, 0.0).then_inc(s_const, 1)
            nc.gpsimd.memset(g.ones[:], 1.0)
            nc.gpsimd.memset(g.ident[:], 0.0).then_inc(s_const, 1)
            nc.gpsimd.iota(g.node_iota, [[1, 400]], base=0, channel_multiplier=400).then_inc(s_iota, 1)
            pool.wait_ge(s_const, 3)
            nc.gpsimd.affine_select(out=g.ident[:], in_=g.ident[:], compare_op=ALU.not_equal, fill=1.0,
                                    base=0, pattern=[[-1, P]], channel_multiplier=1).then_inc(s_const, 1)
            nc.gpsimd.affine_select(out=g.below[:], in_=g.ones[:], compare_op=ALU.is_gt, fill=0.0,
                                    base=0, pattern=[[-1, P]], channel_multiplier=1).then_inc(s_const, 1)
            nc.gpsimd.affine_select(out=g.above[:], in_=g.ones[:], compare_op=ALU.is_gt, fill=0.0,
                                    base=0, pattern=[[1, P]], channel_multiplier=-1).then_inc(s_const, 1)
            nc.gpsimd.iota(g.spare_i[:], [[1, 1]], base=N, channel_multiplier=1).then_inc(s_const, 1)
            nc.gpsimd.iota(g.slot_i[:], [[1, T]], base=0, channel_multiplier=T).then_inc(s_const, 1)

        @block.vector
        def _(dve):
            n = [0]

            def link(ins):
                n[0] += 1
                ins.then_inc(s_dve, 1)
                dve.wait_ge(s_dve, n[0])

            def mark(what):
                done[what] = n[0]
            V = nc.vector
            dve.wait_ge(s_const, 8)
            dve.wait_ge(s_w, 16 * len(g.weight_loads))
            link(V.tensor_scalar(g.bself_rep, g.ones[:], g.bself_col[:, 0:1], None, ALU.mult))
            link(V.tensor_scalar(g.bneigh_rep, g.ones[:], g.bneigh_col[:, 0:1], None, ALU.mult))
            mark("biases")
            dve.wait_ge(s_edges, 16 * 7)
            link(V.tensor_copy(g.dstf[:, 1:T + 1], g.dst_i[:]))
            link(V.tensor_copy(g.dstf[:, T + 1:T + 2], g.dst_next_i[:]))
            link(V.tensor_copy(g.typef[:], g.type_i[:]))
            link(V.memset(g.eps[:], LN_EPS))
            link(V.memset(g.ones3[:], 1.0))
            link(V.tensor_scalar(g.own_i[:], g.dst_i[:], float(N - 1), None, ALU.min))
            dst = g.dstf[:, 1:T + 1]
            first, last = g.dstf[:, 1:2], g.dstf[:, T:T + 1]
            link(V.tensor_scalar(g.diag_first, g.ident[:], first, None, ALU.mult))
            link(V.tensor_scalar(g.diag_last, g.ident[:], last, None, ALU.mult))
            mark("ends")
            link(V.memset(g.same[:], 0.0))
            link(V.tensor_tensor(g.same[:, 1:T], g.dstf[:, 2:T + 1], g.dstf[:, 1:T], ALU.is_equal))
            link(V.tensor_tensor(g.is_last[:], dst, g.dstf[:, 2:T + 2], ALU.not_equal))
            link(V.scalar_tensor_tensor(g.is_last[:], dst, float(N), g.is_last[:], ALU.is_lt, ALU.mult))
            link(V.tensor_scalar(g.in_first[:], dst, first, None, ALU.is_equal))
            link(V.tensor_scalar(g.in_last[:], dst, last, None, ALU.is_equal))
            link(V.tensor_scalar(g.tmpT[:], g.is_last[:], -float(SKIP), float(SKIP), ALU.mult, ALU.add))
            link(V.tensor_tensor(g.tmpT[:], g.tmpT[:], dst, ALU.add))
            link(V.tensor_copy(g.last_node_i[:], g.tmpT[:]))
            link(V.tensor_scalar(g.tab_row_i[:], g.slot_i[:], float(N), None, ALU.add))
            dve.wait_ge(s_pe, 6)
            rowF, rowL = g.ps[1][:, 0:P], g.ps[1][:, P:2 * P]
            link(V.scalar_tensor_tensor(g.link_in[:], rowF, last, g.above[:], ALU.is_equal, ALU.mult))
            link(V.scalar_tensor_tensor(g.link_out[:], rowL, first, g.below[:], ALU.is_equal, ALU.mult))
            link(V.scalar_tensor_tensor(g.no_in[:], rowL, first, g.below[:], ALU.is_equal, ALU.mult))
            link(V.scalar_tensor_tensor(g.no_out[:], rowF, last, g.above[:], ALU.is_equal, ALU.mult))
            link(V.tensor_scalar(g.no_in[:], g.no_in[:], 1e30, -1e30, ALU.mult, ALU.add))
            link(V.tensor_scalar(g.no_out[:], g.no_out[:], 1e30, -1e30, ALU.mult, ALU.add))
            link(V.tensor_copy(g.tmpT[:], g.slot_i[:]))
            for r in range(R1):
                oh, fwd, bwd = g.wrel[:, r, :], g.cnt_fwd[:, r, :], g.cnt_bwd[:, r, :]
                if r < R:
                    link(V.tensor_scalar(oh, g.typef[:], float(r), None, ALU.is_equal))
                else:
                    link(V.tensor_tensor(oh, g.tmpT[:], g.is_last[:], ALU.mult))
                link(V.tensor_tensor_scan(fwd, g.same[:, 0:T], oh, 0.0, ALU.mult, ALU.add))
                link(V.tensor_tensor_scan(bwd[:, ::-1], g.same[:, 1:T + 1][:, ::-1], oh[:, ::-1], 0.0, ALU.mult, ALU.add))
            link(V.tensor_copy(g.edge_ends[:, 0:R1], g.cnt_fwd[:, :, T - 1]))
            link(V.tensor_copy(g.edge_ends[:, R1:2 * R1], g.cnt_bwd[:, :, 0]))
            mark("counts")
            dve.wait_ge(s_pe, 8)
            link(V.tensor_copy(g.edge_ends[:], g.ps[2][:, 0:2 * R1]))
            link(V.memset(g.rcnt[:], 0.0))
            for r in range(R1):
                oh, fwd, bwd = g.wrel[:, r, :], g.cnt_fwd[:, r, :], g.cnt_bwd[:, r, :]
                link(V.tensor_tensor(fwd, fwd, bwd, ALU.add))
                link(V.tensor_tensor(fwd, fwd, oh, ALU.subtract))
                link(V.scalar_tensor_tensor(fwd, g.in_first[:], g.edge_ends[:, r:r + 1], fwd, ALU.mult, ALU.add))
                link(V.scalar_tensor_tensor(fwd, g.in_last[:], g.edge_ends[:, R1 + r:R1 + r + 1], fwd, ALU.mult, ALU.add))
                if r == R:
                    link(V.tensor_copy(g.dst_slot_i[:], fwd))
                    continue
                link(V.tensor_tensor(g.rcnt[:], g.rcnt[:], fwd, ALU.add))
                link(V.tensor_scalar(fwd, fwd, 1.0, None, ALU.max))
                link(V.reciprocal(fwd, fwd))
                link(V.tensor_tensor(oh, oh, fwd, ALU.mult))
            link(V.reciprocal(g.rcnt[:], g.rcnt[:]))
            link(V.tensor_copy(g.w_slot[:].rearrange("p t r -> p r t"), g.wrel[:, 0:R, :]))
            dve.wait_ge(s_pe, 4)
            link(V.tensor_tensor(g.A_gate[:, 0:D], g.WselfT, g.ident[:], ALU.subtract))
            link(V.tensor_tensor(g.A_gate[:, D:2 * D], g.WgaT, g.ps[0][:, 0:D], ALU.add))
            link(V.tensor_copy(g.B_gate[:, 0:D], g.WneighT))
            link(V.tensor_copy(g.B_gate[:, D:2 * D], g.ps[0][:, D:2 * D]))
            link(V.tensor_tensor(g.bias_gate[:, D:2 * D], g.bgate_row[:], g.ps[0][0:3, 2 * D:3 * D], ALU.add))
            link(V.tensor_copy(g.bias_gate[:, 0:D], g.bself_row[:]))
            link(V.tensor_tensor(g.bias_gate_n[:, 0:D], g.bself_row[:], g.bneigh_row[:], ALU.add))
            link(V.tensor_tensor(g.bias_gate_n[:, D:2 * D], g.bias_gate[:, D:2 * D], g.ps[0][0:3, 3 * D:4 * D], ALU.add))
            for row, parts, width in ((g.b1_row, g.b1_parts, D), (g.b2_row, g.b2_parts, D),
                                      (g.bias_gate, g.gate_parts, 2 * D), (g.bias_gate_n, g.gate_parts_n, 2 * D)):
                rest, total, piece = g.split_rest[:, 0:width], g.split_sum[:, 0:width], g.split_part[:, 0:width]
                link(V.tensor_copy(rest, row))
                for i in range(3):
                    link(V.tensor_copy(piece, rest))
                    link(V.tensor_tensor(rest, rest, piece, ALU.subtract))
                    pick = g.ident[0:3, i:i + 1]
                    if i == 0:
                        link(V.tensor_scalar(total, piece, pick, None, ALU.mult))
                    else:
                        link(V.scalar_tensor_tensor(total, piece, pick, total, ALU.mult, ALU.add))
                link(V.tensor_copy(parts[:], total))
            for out, w, row in g.att_products:
                link(V.tensor_tensor(g.att_tmp, w, row, ALU.mult))
                link(V.tensor_reduce(out, g.att_tmp[:].rearrange("p (h c) -> p h c", h=H), AX_X, ALU.add))
            for i in range(2):
                link(V.tensor_scalar(g.bias_rep[i], g.ones[:], g.gat_bias_col[:, i:i + 1], 0.0, ALU.mult, ALU.max))
            mark("weights")
            dve.wait_ge(s_pe, 10)
            for i in range(2):
                link(V.tensor_copy(g.const_row[i][:], g.ps[3 + i][0:1, 0:W]))

        @block.tensor
        def _(pe):
            def step(n, ins):
                ins.then_inc(s_pe, 1)
            pe.wait_ge(s_w, 16 * len(g.weight_loads))
            step(1, nc.tensor.matmul(g.ps[0][:, 0:D], g.W_self, g.WgbT, start=True, stop=True))
            step(2, nc.tensor.matmul(g.ps[0][:, D:2 * D], g.W_neigh, g.WgbT, start=True, stop=True))
            pe.wait_ge(s_dve, done["biases"])
            step(3, nc.tensor.matmul(g.ps[0][:, 2 * D:3 * D], g.bself_rep, g.WgbT, start=True, stop=True))
            step(4, nc.tensor.matmul(g.ps[0][:, 3 * D:4 * D], g.bneigh_rep, g.WgbT, start=True, stop=True))
            pe.wait_ge(s_dve, done["ends"])
            step(5, nc.tensor.matmul(g.ps[1][:, 0:P], g.ones[:], g.diag_first, start=True, stop=True))
            step(6, nc.tensor.matmul(g.ps[1][:, P:2 * P], g.ones[:], g.diag_last, start=True, stop=True))
            pe.wait_ge(s_dve, done["counts"])
            step(7, nc.tensor.matmul(g.ps[2][:, 0:R1], g.link_in[:], g.edge_ends[:, 0:R1], start=True, stop=True))
            step(8, nc.tensor.matmul(g.ps[2][:, R1:2 * R1], g.link_out[:], g.edge_ends[:, R1:2 * R1], start=True, stop=True))
            pe.wait_ge(s_dve, done["weights"])
            for i in range(2):
                step(9 + i, nc.tensor.matmul(g.ps[3 + i][:, 0:W], g.bias_rep[i], g.WG[i + 1][:, 0:W], start=True, stop=True))
    ph.end()


G4 = 4
CH = G4 * P
NCH = -(-N // CH)
SCH = T // G4
AHEAD, BEHIND = 3, 1


class Chunk:

    def __init__(self, k, h, first, last):
        self.k, self.h, self.first, self.last = k, h, first, last


def rounds(eng, n, turn):
    def step(k, e, number):
        def at(d):
            if number is not None and not 0 <= number + d < n:
                return None
            c = None if number is None else number + d
            return Chunk(k + (e + d) // 2, (e + d) % 2, c is not None and c < 2, c == n - 1)
        turn(at)
    pairs = (n - 2 - AHEAD) // 2
    for i in range(-AHEAD, 2):
        step(i // 2, i % 2, i)
    with eng.Fori(1, pairs + 1) as k:
        step(k, 0, None)
        step(k, 1, None)
    for i in range(2 + 2 * pairs, n + BEHIND):
        step(i // 2, i % 2, i)


def alternate(*parts):
    parts = [p for p in parts if p is not None]
    while parts:
        for p in list(parts):
            try:
                next(p)
            except StopIteration:
                parts.remove(p)


def opt(part, c):
    return part(c) if c is not None else None


class Signals:

    def __init__(self, ph):
        self.ph, self.of = ph, {}

    def __call__(self, name):
        if name not in self.of:
            self.of[name] = self.ph.sem(name)
        return self.of[name]

    def after(self, eng, name, c):
        eng.wait_ge(self(name), c.k * 2 + c.h + 1)

    def before(self, eng, name, c):
        if not c.first:
            eng.wait_ge(self(name), c.k * 2 + c.h - 1)

    def loaded(self, eng, which, c, dmas=1):
        eng.wait_ge(self(f"load_{which}{c.h}"), c.k * (16 * dmas) + 16 * dmas)

    def stored(self, eng, name, c, dmas=1):
        if not c.first:
            eng.wait_ge(self(f"store_{name}{c.h}"), c.k * (16 * dmas))


def node_rows(g, ph, block):
    nc = g.nc
    s_idx, s_scattered, s_gathered, s_moved, s_slots, s_turn = (
        ph.sem(n) for n in ("tab_index_copied", "tab_scattered", "tab_gathered", "tab_moved", "tab_slots", "tab_turn"))
    steps = T // RING

    @block.gpsimd
    def _(pool):
        def scatter(k, first):
            if not first:
                pool.wait_ge(s_scattered, k * (16 * RING))
            nc.gpsimd.tensor_copy(g.idx_ring[:], g.last_node_i[:, bass.ds(k * RING, RING)])
            nc.gpsimd.tensor_copy(g.row_ring[:], g.tab_row_i[:, bass.ds(k * RING, RING)]).then_inc(s_idx, 1)
            pool.wait_ge(s_idx, k + 1)
            pool.sem_inc(s_turn, 1)
            for j in range(RING):
                nc.gpsimd.indirect_dma_start(g.tab_dram, bass.IndirectOffsetOnAxis(g.idx_ring[:, j:j + 1], 0),
                                             g.row_ring[:, j:j + 1], None, bounds_check=N - 1,
                                             oob_is_err=False).then_inc(s_scattered, 16)
        scatter(0, True)
        with pool.Fori(1, steps) as k:
            scatter(k, False)
        pool.wait_ge(s_scattered, 16 * T)

        def gather(k, first):
            if not first:
                pool.wait_ge(s_moved, k)
            nc.gpsimd.tensor_copy(g.idx_ring[:], g.src_i[:, bass.ds(k * RING, RING)]).then_inc(s_idx, 1)
            pool.wait_ge(s_idx, k + steps + 1)
            pool.sem_inc(s_turn, 1)
            for j in range(RING):
                nc.gpsimd.indirect_dma_start(g.row_ring[:, j:j + 1], None, g.tab_dram,
                                             bass.IndirectOffsetOnAxis(g.idx_ring[:, j:j + 1], 0)).then_inc(s_gathered, 16)
            pool.wait_ge(s_gathered, k * (16 * RING) + 16 * RING)
            nc.gpsimd.tensor_copy(g.src_row_i[:, bass.ds(k * RING, RING)], g.row_ring[:]).then_inc(s_moved, 1)
        gather(0, True)
        with pool.Fori(1, steps) as k:
            gather(k, False)
        pool.wait_ge(s_moved, steps)
        nc.gpsimd.tensor_scalar(g.tmpT[:], g.src_row_i[:], -float(N), None, ALU.add).then_inc(s_slots, 1)
        pool.wait_ge(s_slots, 1)
        nc.gpsimd.tensor_scalar(g.tmpT2[:], g.tmpT[:], 0.0, float(PAD), ALU.is_lt, ALU.mult).then_inc(s_slots, 1)
        pool.wait_ge(s_slots, 2)
        nc.gpsimd.tensor_scalar(g.tmpT[:], g.tmpT[:], 0.0, None, ALU.max).then_inc(s_slots, 1)
        pool.wait_ge(s_slots, 3)
        nc.gpsimd.tensor_tensor(g.tmpT[:], g.tmpT[:], g.tmpT2[:], ALU.add).then_inc(s_slots, 1)
        pool.wait_ge(s_slots, 4)
        nc.gpsimd.tensor_copy(g.src_slot_i[:], g.tmpT[:]).then_inc(s_slots, 1)


def chunks(g, mode, layer=0):
    nc = g.nc
    dense = mode == "nodes"
    ph = Phase(nc, f"{mode}{layer}")
    s = Signals(ph)
    after, before, loaded, stored = s.after, s.before, s.loaded, s.stored
    A, V, ACTE = nc.tensor, nc.vector, nc.scalar
    n_chunks = NCH if dense else SCH

    def rows(table, c):
        if dense:
            start = N - CH if c.last else c.k * (2 * CH) + c.h * CH
            return table[bass.ds(start, CH), :].rearrange("(p j) f -> p j f", j=G4)
        return table.rearrange("(p t) f -> p t f", t=T)[:, bass.ds(c.k * (2 * G4) + c.h * G4, G4), :]

    def slots(t, c):
        return t[:, bass.ds(c.k * (2 * G4) + c.h * G4, G4)]

    part = (lambda t: t[0:N, :]) if dense else (lambda t: t[N:N + PAD, :])
    loads = {"nodes": [("a", g.X, g.args["x"], "y")],
             "x1": [("a", g.X, g.z1_dram[N:N + PAD, :], "xT"), ("b", g.G, g.xd_dram, "y")],
             "x2": [("a", g.Y, g.x1_dram[N:N + PAD, :], "w")],
             "x3": [("a", g.X2, g.x2_dram[N:N + PAD, :], "x3p")]}.get(mode, [])
    stores = {"nodes": [("z1", g.Z1, part(g.z1_dram), "z1r", 2), ("x1", g.Y, part(g.x1_dram), "x1", 1),
                        ("x2", g.X2, part(g.x2_dram), "x2", 0), ("x3", g.X3, g.x3_dram, "x3", 0)],
              "z1": [("xd", g.X, g.xd_dram, "xT", 1), ("z1", g.Z1, part(g.z1_dram), "z1r", 0)],
              "x1": [("x1", g.Y, part(g.x1_dram), "x1", 0)],
              "x2": [("x2", g.X2, part(g.x2_dram), "x2", 0)],
              "h": [("rows", g.RW, g.gat_dram[0:PAD, :], "rw", 0)],
              "x3": [("x3", g.X3, g.x3s_dram, "x3", 0), ("rows", g.RW, g.gat_dram[0:PAD, :], "rw", -1)]}[mode]

    def gate_view(c):
        return g.psL[c.h][:].rearrange("p (j w) -> p j w", j=G4)

    def first_half(c):
        return g.psL[c.h][:, 0:512].rearrange("p (j f) -> p j f", j=G4)

    def second_half(c):
        return g.psL[c.h][:, 512:1024].rearrange("p (j f) -> p j f", j=G4)

    with nc.Block() as block:
        @block.sync
        def _(sp):
            if mode == "h":
                sp.dma_start(g.gat_dram[PAD:PAD + 1, :], g.const_row[layer][:]).then_inc(s("const_row"), 16)

            def turn(at):
                c = at(3)
                if c is not None:
                    for which, buf, table, free in loads:
                        before(sp, free, c)
                        sp.sem_inc(s("turn_sp"), 1)
                        sp.dma_start(buf[c.h][:], rows(table, c)).then_inc(s(f"load_{which}{c.h}"), 16)
                for name, buf, table, ready, ahead in sorted(stores, key=lambda st: st[4] == 2):
                    c = at(ahead)
                    if c is not None:
                        after(sp, ready, c)
                        sp.sem_inc(s("turn_sp"), 1)
                        if dense and c.last:
                            sp.wait_ge(s(f"store_{name}{1 - c.h}"), 16 * (n_chunks // 2))
                        sp.dma_start(rows(table, c), buf[c.h][:]).then_inc(s(f"store_{name}{c.h}"), 16)
            rounds(sp, n_chunks, turn)
            if mode == "h":
                sp.wait_ge(s("const_row"), 16)
            for name, *_ in stores:
                for h in (0, 1):
                    sp.wait_ge(s(f"store_{name}{h}"), 16 * ((n_chunks + 1 - h) // 2))

        if dense:
            node_rows(g, ph, block)

        if mode == "z1":
            @block.gpsimd
            def _(pool):
                def turn(at):
                    c = at(3)
                    if c is None:
                        return
                    stored(pool, "xd", c)
                    before(pool, "xT", c)
                    nc.gpsimd.tensor_copy(g.own_ring[c.h][:], slots(g.own_i, c)).then_inc(s("own"), 1)
                    after(pool, "own", c)
                    pool.sem_inc(s("turn"), 1)
                    for j in range(G4):
                        nc.gpsimd.indirect_dma_start(
                            g.X[c.h][:, j, :], None, g.args["x"],
                            bass.IndirectOffsetOnAxis(g.own_ring[c.h][:, j:j + 1], 0)).then_inc(s(f"load_a{c.h}"), 16)
                rounds(pool, n_chunks, turn)

        if mode == "x3":
            @block.gpsimd
            def _(pool):
                def turn(at):
                    c = at(0)
                    if c is None:
                        return
                    if not c.first:
                        pool.wait_ge(s(f"scatter{c.h}"), c.k * (16 * G4))
                    nc.gpsimd.tensor_copy(g.own_ring[c.h][:], slots(g.last_node_i, c)).then_inc(s("own"), 1)
                    after(pool, "own", c)
                    after(pool, "x3", c)
                    pool.sem_inc(s("turn"), 1)
                    for j in range(G4):
                        nc.gpsimd.indirect_dma_start(
                            g.x3_dram, bass.IndirectOffsetOnAxis(g.own_ring[c.h][:, j:j + 1], 0),
                            g.X3[c.h][:, j, :], None, bounds_check=N - 1, oob_is_err=False
                        ).then_inc(s(f"scatter{c.h}"), 16)
                rounds(pool, n_chunks, turn)
                for h in (0, 1):
                    pool.wait_ge(s(f"scatter{h}"), 16 * G4 * ((n_chunks + 1 - h) // 2))

        @block.tensor
        def _(pe):
            def transposes(out, src):
                for j in range(G4):
                    ins = A.transpose(out[:, j, :], src[:, j, :], g.ident[:])
                return ins

            def product(out, lhs, weights, bias=None):
                for j in range(G4):
                    if bias is not None:
                        A.matmul(out[:, j, :], g.ones3[:], bias[:], start=True, stop=False)
                    ins = A.matmul(out[:, j, :], lhs[:, j, :], weights, start=bias is None, stop=True)
                return ins

            def x_products(c):
                loaded(pe, "a", c, G4 if mode == "z1" else 1)
                before(pe, "z1r" if mode == "z1" else "y", c)
                transposes(g.psT[c.h], g.X[c.h]).then_inc(s("xTp"), 1)
                yield
                after(pe, "xT", c)
                if mode == "z1":
                    product(second_half(c), g.XT[c.h], g.root1[:], g.b1_parts).then_inc(s("z1p"), 1)
                if dense:
                    before(pe, "v", c)
                    A.matmul(g.psL[c.h][:, 0:512], g.root1[:], g.XT[c.h][:].rearrange("p j f -> p (j f)"),
                             start=True, stop=True).then_inc(s("z1Tp"), 1)
                yield
                if dense:
                    after(pe, "z1T", c)
                if mode != "z1":
                    product(g.psT[c.h], g.Z1T[c.h] if dense else g.XT[c.h], g.root2[:], g.b2_parts).then_inc(s("z2p"), 1)
                if dense:
                    transposes(second_half(c), g.Z1T[c.h]).then_inc(s("z1p"), 1)
                yield

            def gate_inputs(c):
                if dense:
                    after(pe, "x1", c)
                else:
                    loaded(pe, "a", c)
                transposes(g.psT[c.h], g.Y[c.h]).then_inc(s("x1Tp"), 1)
                yield
                if not dense:
                    after(pe, "mean", c)
                    transposes(g.psM[c.h], g.M[c.h]).then_inc(s("mTp"), 1)
                yield

            def gate_products(c):
                after(pe, "x1T", c)
                if not dense:
                    after(pe, "mT", c)
                    before(pe, "ad", c)
                L = gate_view(c)
                for j in range(G4):
                    A.matmul(L[:, j, :], g.ones3[:], (g.gate_parts if dense else g.gate_parts_n)[:], start=True, stop=False)
                    ins = A.matmul(L[:, j, :], g.XT[c.h][:, j, :], g.A_gate[:], start=False, stop=dense)
                    if not dense:
                        ins = A.matmul(L[:, j, :], g.MT[c.h][:, j, :], g.B_gate[:], start=False, stop=True)
                ins.then_inc(s("Lp"), 1)
                yield

            def right_values(c):
                after(pe, "x2", c)
                transposes(first_half(c), g.X2[c.h]).then_inc(s("adTp"), 1)
                yield
                after(pe, "adT", c)
                for j in range(G4):
                    ins = A.matmul(second_half(c)[:, j, 0:H], g.X[c.h][:, j, :], g.vd[0], start=True, stop=True)
                ins.then_inc(s("adp"), 1)
                yield

            def next_rows(c):
                src, wts, wd = (g.Y, g.WG[layer + 1], W + H) if mode == "h" else (g.X3, g.WH, W)
                after(pe, "hr" if mode == "h" else "x3", c)
                transposes(g.psT[c.h], src[c.h]).then_inc(s("hTp"), 1)
                yield
                after(pe, "hT", c)
                before(pe, "rw", c)
                L = gate_view(c)
                for j in range(G4):
                    ins = A.matmul(L[:, j, 0:wd], g.XT[c.h][:, j, :], wts[:], start=True, stop=True)
                ins.then_inc(s("rwp"), 1)
                yield

            def turn(at):
                if dense:
                    alternate(opt(gate_inputs, at(1)))
                    alternate(opt(gate_products, at(1)))
                    alternate(opt(x_products, at(2)))
                elif mode in ("z1", "x1"):
                    alternate(opt(x_products, at(2)))
                elif mode == "x2":
                    alternate(opt(gate_inputs, at(2)))
                    alternate(opt(right_values, at(-1)))
                    alternate(opt(gate_products, at(1)))
                elif mode == "h":
                    alternate(opt(next_rows, at(0)))
                else:
                    alternate(opt(next_rows, at(-1)))
            rounds(pe, n_chunks, turn)

        @block.scalar
        def _(act):
            def copy(out, src, name):
                ACTE.activation(out, src, ACT.Copy).then_inc(s(name), 1)

            def rstd(c, t):
                after(act, f"mv{t}", c)
                ACTE.activation(g.lnv[c.h][:], g.mv[t][c.h][:, :, 1], ACT.Ln, bias=g.eps[:, 0:1]).then_inc(s(f"ln{t}"), 1)
                yield
                after(act, f"ln{t}", c)
                ACTE.activation(g.rs[t][c.h][:], g.lnv[c.h][:], ACT.Exp, scale=-0.5).then_inc(s(f"rs{t}"), 1)
                yield

            def x_transposed(c):
                after(act, "xTp", c)
                copy(g.XT[c.h][:], g.psT[c.h][:], "xT")
                yield
                if dense:
                    after(act, "z1Tp", c)
                    ACTE.activation(g.Z1T[c.h][:].rearrange("p j f -> p (j f)"), g.psL[c.h][:, 0:512], ACT.Relu,
                                    bias=g.b1_col[:, 0:1]).then_inc(s("z1T"), 1)
                    yield
                    after(act, "z1p", c)
                    stored(act, "z1", c)
                    copy(g.Z1[c.h][:], second_half(c), "z1r")
                    yield

            def gate_transposed(c):
                after(act, "x1Tp", c)
                copy(g.XT[c.h][:], g.psT[c.h][:], "x1T")
                yield
                if mode == "x2":
                    after(act, "mTp", c)
                    copy(g.MT[c.h][:], g.psM[c.h][:], "mT")
                yield

            def gate(c):
                after(act, "Lp", c)
                ACTE.activation(g.G[c.h][:], gate_view(c)[:, :, D:2 * D], ACT.Exp, scale=-1.0).then_inc(s("g1"), 1)
                yield
                after(act, "g1", c)
                ACTE.activation(g.G[c.h][:], g.G[c.h][:], ACT.Ln, bias=g.ones[:, 0:1]).then_inc(s("g2"), 1)
                yield
                after(act, "g2", c)
                ACTE.activation(g.G[c.h][:], g.G[c.h][:], ACT.Exp, scale=-1.0).then_inc(s("g"), 1)
                yield

            def right_values(c):
                after(act, "adTp", c)
                copy(g.X[c.h][:], first_half(c), "adT")
                yield
                after(act, "adp", c)
                copy(slots(g.ad, c), second_half(c)[:, :, 0:H], "ad")
                yield

            def next_rows(c):
                after(act, "hTp", c)
                copy(g.XT[c.h][:], g.psT[c.h][:], "hT")
                yield
                after(act, "rwp", c)
                stored(act, "rows", c)
                L = gate_view(c)
                ACTE.activation(g.RW[c.h][:], L[:, :, 0:W], ACT.Copy)
                copy(slots(g.ad, c), L[:, :, W:W + H] if mode == "h" else L[:, :, D:W], "rw")
                yield

            def turn(at):
                if dense:
                    if at(1):
                        alternate(rstd(at(1), "a"))
                    if at(0):
                        alternate(rstd(at(0), "b"))
                    alternate(opt(gate_transposed, at(1)))
                    if at(0):
                        alternate(rstd(at(0), "c"))
                    alternate(opt(gate, at(1)), opt(x_transposed, at(2)))
                    if at(0):
                        alternate(rstd(at(0), "d"))
                elif mode == "z1":
                    alternate(opt(x_transposed, at(2)))
                elif mode == "x1":
                    if at(1):
                        alternate(rstd(at(1), "a"))
                    alternate(opt(x_transposed, at(2)))
                elif mode == "x2":
                    if at(0):
                        alternate(rstd(at(0), "b"))
                    alternate(opt(gate_transposed, at(2)))
                    alternate(opt(right_values, at(-1)))
                    if at(0):
                        alternate(rstd(at(0), "c"), opt(gate, at(1)))
                    else:
                        alternate(opt(gate, at(1)))
                elif mode == "h":
                    alternate(opt(next_rows, at(0)))
                else:
                    alternate(opt(next_rows, at(-1)))
                    if at(1):
                        alternate(rstd(at(1), "d"))
            rounds(act, n_chunks, turn)

        @block.vector
        def _(dve):
            def stats(c, t, src):
                for j in range(G4):
                    ins = V.bn_stats(g.st[t][c.h][:, j, :], src[c.h][:, j, :])
                ins.then_inc(s(f"st{t}"), 1)
                yield
                after(dve, f"st{t}", c)
                dve.sem_inc(s("turn_dve"), 1)
                for j in range(G4):
                    ins = V.bn_aggr(g.mv[t][c.h][:, j, :], g.st[t][c.h][:, j, :])
                ins.then_inc(s(f"mv{t}"), 1)
                yield

            def normed(c, t, src, dst, name):
                after(dve, f"rs{t}", c)
                for j in range(G4):
                    ins = V.tensor_scalar(dst[c.h][:, j, :], src[c.h][:, j, :], g.mv[t][c.h][:, j, 0:1],
                                          g.rs[t][c.h][:, j:j + 1], ALU.subtract, ALU.mult)
                ins.then_inc(s(name), 1)

            def sums_with_carry(dst, c):
                for j in range(G4):
                    t = c.k * (2 * G4) + c.h * G4 + j
                    ins = V.scalar_tensor_tensor(dst[c.h][:, j, :], g.carry[:], g.in_first[:, bass.ds(t, 1)],
                                                 g.sums[:, bass.ds(t * W, D)], ALU.mult, ALU.add)
                return ins

            def spread(row):
                return row[:, None, :].to_broadcast([P, G4, D])

            def sums(c):
                if mode == "z1":
                    before(dve, "z1r", c)
                elif mode == "x1":
                    before(dve, "y", c)
                elif mode == "x2":
                    before(dve, "mTp", c)
                elif mode == "h":
                    before(dve, "hTp", c)
                else:
                    before(dve, "hp", c)
                sums_with_carry(g.Y if mode == "h" else g.M, c).then_inc(s("agg"), 1)
                yield
                if mode == "x2":
                    after(dve, "agg", c)
                    V.tensor_tensor(g.M[c.h][:], g.M[c.h][:], slots(g.rcnt, c)[:, :, None].to_broadcast([P, G4, D]),
                                    ALU.mult).then_inc(s("mean"), 1)
                yield

            def z1(c):
                after(dve, "agg", c)
                after(dve, "z1p", c)
                V.tensor_tensor(g.M[c.h][:], g.M[c.h][:], second_half(c), ALU.add).then_inc(s("z1q"), 1)
                yield
                after(dve, "z1q", c)
                stored(dve, "z1", c)
                V.tensor_scalar(g.Z1[c.h][:], g.M[c.h][:], 0.0, None, ALU.max).then_inc(s("z1r"), 1)
                yield

            def x1(c):
                if not dense:
                    after(dve, "agg", c)
                    after(dve, "z2p", c)
                    V.tensor_tensor(g.M[c.h][:], g.M[c.h][:], g.psT[c.h][:], ALU.add).then_inc(s("z2q"), 1)
                    yield
                    after(dve, "z2q", c)
                    loaded(dve, "b", c)
                    z2, x = g.M, g.G
                else:
                    after(dve, "z2p", c)
                    z2, x = g.psT, g.X
                stored(dve, "x1", c)
                V.scalar_tensor_tensor(g.Y[c.h][:], z2[c.h][:], 0.0, x[c.h][:], ALU.max, ALU.add).then_inc(s("y"), 1)
                yield
                after(dve, "y", c)
                yield from stats(c, "a", g.Y)
                if dense:
                    yield from x1_norm(c)

            def x1_norm(c):
                normed(c, "a", g.Y, g.Y, "x1")
                yield

            def x2(c):
                after(dve, "g", c)
                V.tensor_tensor(g.V[c.h][:], g.G[c.h][:], gate_view(c)[:, :, 0:D], ALU.mult).then_inc(s("v"), 1)
                yield
                after(dve, "v", c)
                V.tensor_tensor(g.V[c.h][:], g.V[c.h][:], g.Y[c.h][:], ALU.add).then_inc(s("v2"), 1)
                yield
                after(dve, "v2", c)
                yield from stats(c, "b", g.V)
                normed(c, "b", g.V, g.V, "vn")
                yield
                after(dve, "vn", c)
                V.tensor_tensor(g.V[c.h][:], g.V[c.h][:], spread(g.gamma), ALU.mult).then_inc(s("vg"), 1)
                yield
                after(dve, "vg", c)
                V.tensor_tensor(g.V[c.h][:], g.V[c.h][:], spread(g.beta), ALU.add).then_inc(s("vb"), 1)
                yield
                after(dve, "vb", c)
                V.scalar_tensor_tensor(g.V[c.h][:], g.V[c.h][:], 0.0, g.Y[c.h][:], ALU.max, ALU.add).then_inc(s("w"), 1)
                yield
                after(dve, "w", c)
                yield from stats(c, "c", g.V)
                stored(dve, "x2", c)
                normed(c, "c", g.V, g.X2, "x2")
                yield
                if dense:
                    after(dve, "x2", c)
                    stored(dve, "x3", c)
                    V.tensor_tensor(g.X3[c.h][:], g.X2[c.h][:], spread(g.gat_bias[2]), ALU.add).then_inc(s("x3p"), 1)
                    yield
                    after(dve, "x3p", c)
                    yield from stats(c, "d", g.X3)
                    normed(c, "d", g.X3, g.X3, "x3")
                    yield

            def layer_out(c):
                X = g.Y if mode == "h" else g.X3
                if mode == "x3":
                    stored(dve, "x3", c)
                    before(dve, "hTp", c)
                    if not c.first:
                        dve.wait_ge(s(f"scatter{c.h}"), c.k * (16 * G4))
                after(dve, "agg", c)
                V.tensor_tensor(X[c.h][:], (g.Y if mode == "h" else g.M)[c.h][:], spread(g.gat_bias[layer if mode == "h" else 2]), ALU.add).then_inc(s("hp"), 1)
                yield
                after(dve, "hp", c)
                if mode == "h":
                    V.tensor_scalar(X[c.h][:], X[c.h][:], 0.0, None, ALU.max).then_inc(s("hr"), 1)
                    yield
                    return
                loaded(dve, "a", c)
                V.tensor_tensor(X[c.h][:], X[c.h][:], g.X2[c.h][:], ALU.add).then_inc(s("x3p"), 1)
                yield
                after(dve, "x3p", c)
                yield from stats(c, "d", X)

            def x3_norm(c):
                normed(c, "d", g.X3, g.X3, "x3")
                yield

            def turn(at):
                if dense:
                    alternate(opt(x1, at(1)), opt(x2, at(0)))
                elif mode == "z1":
                    alternate(opt(sums, at(2)), opt(z1, at(1)))
                elif mode == "x1":
                    alternate(opt(x1_norm, at(0)), opt(x1, at(1)), opt(sums, at(2)))
                elif mode == "x2":
                    alternate(opt(x2, at(0)), opt(sums, at(2)))
                elif mode == "h":
                    alternate(opt(layer_out, at(1)), opt(sums, at(2)))
                else:
                    alternate(opt(x3_norm, at(0)), opt(layer_out, at(1)), opt(sums, at(2)))
            rounds(dve, n_chunks, turn)
    ph.end()


FT = H * T


def gather(g, mode, layer=0):
    nc, A, V, ACTE = g.nc, g.nc.tensor, g.nc.vector, g.nc.scalar
    ph = Phase(nc, f"{mode}{layer}g")
    sems = {}

    def s(name):
        if name not in sems:
            sems[name] = ph.sem(name)
        return sems[name]
    table, index, width = {
        "conv": (g.z1_dram if layer else g.args["x"], g.src_row_i if layer else g.src_i, D),
        "mean": (g.x1_dram, g.src_row_i, D), "first": (g.x2_dram, g.src_row_i, D),
        "rows": (g.gat_dram, g.src_slot_i, W), "left": (g.x3_dram, g.src_i, D)}[mode]
    steps = T // RING
    used = {"conv": "tp", "mean": "sum", "first": "tp", "rows": "put", "left": "tp"}[mode]

    def over(eng, body):
        body(0, True)
        with eng.Fori(1, steps) as k:
            body(k, False)

    def after(eng, name, k, j, back=0):
        eng.wait_ge(s(name), k * RING + j + 1 - back)

    def row_of(k, j, shift=0, width=D):
        return g.sums_all[:, bass.ds((k * RING + j + shift) * W, width)]

    with nc.Block() as block:
        @block.gpsimd
        def _(pool):
            def body(k, first):
                if not first:
                    for j in range(RING):
                        pool.wait_ge(s(f"row{j}"), k * 16)
                nc.gpsimd.tensor_copy(g.idx_ring[:, 0:RING], index[:, bass.ds(k * RING, RING)]).then_inc(s("index"), 1)
                pool.wait_ge(s("index"), k + 1)
                for j in range(RING):
                    if not first:
                        pool.wait_ge(s(used), k * RING + (j + 1 - RING))
                    pool.sem_inc(s("turn"), 1)
                    nc.gpsimd.indirect_dma_start(g.ring[j][:, 0:width], None, table,
                                                 bass.IndirectOffsetOnAxis(g.idx_ring[:, j:j + 1], 0)).then_inc(s(f"row{j}"), 16)
            over(pool, body)

        if mode in ("conv", "first", "left"):
            @block.tensor
            def _(pe):
                def turn(k, first, j):
                    pe.wait_ge(s(f"row{j}"), k * 16 + 16)
                    if not (first and j < 2):
                        after(pe, "t", k, j, 2)
                    A.transpose(g.psT[j % 2][:, 0, :], g.ring[j][:, 0:D], g.ident[:]).then_inc(s("tp"), 1)

                def product(k, first, j):
                    after(pe, "t", k, j)
                    if not (first and j < 2):
                        if mode == "conv":
                            pe.wait_ge(s("part"), (k * RING + (j - 1)) * R)
                        else:
                            after(pe, "read", k, j, 2)
                    out = g.psL[j % 2]
                    if mode == "conv":
                        A.matmul(out[:, 0:512], g.T2[j % 2], g.Wrel[layer][:, 0:512], start=True, stop=True)
                        ins = A.matmul(out[:, 512:1024], g.T2[j % 2], g.Wrel[layer][:, 512:1024], start=True, stop=True)
                    elif mode == "first":
                        ins = A.matmul(out[:, 0:W], g.T2[j % 2], g.WG[0][:, 0:W], start=True, stop=True)
                    else:
                        ins = A.matmul(out[:, 0:H], g.T2[j % 2], g.vleft[:], start=True, stop=True)
                    ins.then_inc(s("prod"), 1)

                def body(k, first):
                    turn(k, first, 0)
                    for j in range(1, RING):
                        turn(k, first, j)
                        product(k, first, j - 1)
                    product(k, first, RING - 1)
                over(pe, body)
                if mode == "conv":
                    pe.wait_ge(s("sum"), T)
                    A.matmul(g.ps[6][:, 0:D], g.link_in[:], g.sums[:, (T - 1) * W:(T - 1) * W + D],
                             start=True, stop=True).then_inc(s("carry"), 1)

            @block.scalar
            def _(act):
                def body(k, first):
                    for j in range(RING):
                        after(act, "tp", k, j)
                        if not (first and j < 2):
                            after(act, "prod", k, j, 2)
                        ACTE.activation(g.T2[j % 2], g.psT[j % 2][:, 0, :], ACT.Copy).then_inc(s("t"), 1)
                over(act, body)

        if mode == "mean":
            @block.tensor
            def _(pe):
                pe.wait_ge(s("sum"), T)
                A.matmul(g.ps[6][:, 0:D], g.link_in[:], g.sums[:, (T - 1) * W:(T - 1) * W + D],
                         start=True, stop=True).then_inc(s("carry"), 1)

        @block.vector
        def _(dve):
            def copy_columns(dst, src, k):
                V.tensor_copy(dst, src).then_inc(s("cols"), 1)
                dve.wait_ge(s("cols"), k + 1)

            def body(k, first):
                if mode in ("conv", "mean"):
                    if not first:
                        dve.wait_ge(s("sum"), k * RING)
                    if mode == "conv":
                        V.tensor_copy(g.w_ring[:], g.w_slot[:, bass.ds(k * RING, RING), :])
                    copy_columns(g.same_ring[:], g.same[:, bass.ds(k * RING, RING)], k)
                for j in range(RING):
                    if mode == "conv":
                        after(dve, "prod", k, j)
                        for r in range(R):
                            p, w = g.psL[j % 2][:, r * D:(r + 1) * D], g.w_ring[:, j, r:r + 1]
                            if r == 0:
                                ins = V.tensor_scalar(g.acc[j % 2], p, w, None, ALU.mult)
                            else:
                                dve.wait_ge(s("part"), (k * RING + j) * R + r)
                                ins = V.scalar_tensor_tensor(g.acc[j % 2], p, w, g.acc[j % 2], ALU.mult, ALU.add)
                            ins.then_inc(s("part"), 1)
                        dve.wait_ge(s("part"), (k * RING + j) * R + R)
                        if not (first and j == 0):
                            after(dve, "sum", k, j, 1)
                        V.scalar_tensor_tensor(row_of(k, j, 1), row_of(k, j), g.same_ring[:, j:j + 1], g.acc[j % 2],
                                               ALU.mult, ALU.add).then_inc(s("sum"), 1)
                    if mode == "mean":
                        dve.wait_ge(s(f"row{j}"), k * 16 + 16)
                        if not (first and j == 0):
                            after(dve, "sum", k, j, 1)
                        V.scalar_tensor_tensor(row_of(k, j, 1), row_of(k, j), g.same_ring[:, j:j + 1], g.ring[j][:, 0:D],
                                               ALU.mult, ALU.add).then_inc(s("sum"), 1)
                    if mode == "rows":
                        dve.wait_ge(s(f"row{j}"), k * 16 + 16)
                        V.tensor_copy(row_of(k, j, 1, W), g.ring[j][:, 0:W]).then_inc(s("put"), 1)
                    if mode == "first":
                        after(dve, "prod", k, j)
                        V.tensor_copy(row_of(k, j, 1, W), g.psL[j % 2][:, 0:W]).then_inc(s("read"), 1)
                    if mode == "left":
                        after(dve, "prod", k, j)
                        V.tensor_copy(g.a_left[:, bass.ds(k * RING + j, 1), :], g.psL[j % 2][:, None, 0:H]).then_inc(s("read"), 1)
            if mode in ("conv", "mean"):
                V.memset(g.sums_all[:, 0:W], 0.0).then_inc(s("zero"), 1)
                dve.wait_ge(s("zero"), 1)
            over(dve, body)
            if mode in ("conv", "mean"):
                dve.wait_ge(s("carry"), 1)
                V.tensor_copy(g.carry[:], g.ps[6][:, 0:D]).then_inc(s("zero"), 1)
    ph.end()


RMAX = bass.bass_isa.ReduceOp.max


def attention(g, layer):
    nc, A, V, ACTE = g.nc, g.nc.tensor, g.nc.vector, g.nc.scalar
    final = layer == 3
    ph = Phase(nc, f"att{layer}")
    s_dve, s_pe, s_exp, s_max, s_mul, s_sum, s_col, s_zero = (
        ph.sem(n) for n in ("dve_steps", "pe_steps", "exp", "greatest", "weighed", "sum", "columns", "zero"))
    heads = lambda t: t.rearrange("p (h t) -> p h t", h=H)
    q = g.att
    reached = []
    with nc.Block() as block:
        @block.scalar
        def _(act):
            act.wait_ge(s_max, 2 if final else 1)
            ACTE.activation(q.e, q.e, ACT.Exp).then_inc(s_exp, 1)

        if final:
            @block.gpsimd
            def _(pool):
                pool.wait_ge(s_max, 1)
                nc.gpsimd.partition_all_reduce(q.gmax, q.pmax, P, RMAX).then_inc(s_mul, 1)

        @block.vector
        def _(dve):
            n = [0]

            def link(ins):
                n[0] += 1
                ins.then_inc(s_dve, 1)
                dve.wait_ge(s_dve, n[0])

            def wide(t):
                return t[:, None, :].to_broadcast([P, H, T])

            def segment_sum(v, out, pe_step):
                link(V.tensor_tensor_scan(q.fwd, q.same, v, 0.0, ALU.mult, ALU.add))
                link(V.tensor_tensor_scan(q.bwd[:, ::-1], q.next[:, ::-1], v[:, ::-1], 0.0, ALU.mult, ALU.add))
                link(V.tensor_copy(q.ends[:, 0:H], heads(q.fwd)[:, :, T - 1]))
                link(V.tensor_copy(q.ends[:, H:2 * H], heads(q.bwd)[:, :, 0]))
                reached.append(n[0])
                link(V.tensor_tensor(q.fwd, q.fwd, q.bwd, ALU.add))
                link(V.tensor_tensor(out, q.fwd, v, ALU.subtract))
                dve.wait_ge(s_pe, pe_step)
                link(V.tensor_copy(q.ends, g.ps[0][:, 0:2 * H]))
                for h in range(H):
                    oh = heads(out)[:, h, :]
                    link(V.scalar_tensor_tensor(oh, g.in_first[:], q.ends[:, h:h + 1], oh, ALU.mult, ALU.add))
                    link(V.scalar_tensor_tensor(oh, g.in_last[:], q.ends[:, H + h:H + h + 1], oh, ALU.mult, ALU.add))

            link(V.tensor_copy(heads(q.same), wide(g.same[:, 0:T])))
            link(V.tensor_copy(heads(q.next), wide(g.same[:, 1:T + 1])))
            link(V.tensor_tensor(heads(q.v), g.ad[:].rearrange("p t h -> p h t"), wide(g.is_last[:]), ALU.mult))
            segment_sum(q.v, q.e, 1)
            left = (g.a_left[:] if final else g.sums.rearrange("p (t w) -> p t w", w=W)[:, :, D:W]).rearrange("p t h -> p h t")
            link(V.tensor_tensor(heads(q.e), heads(q.e), left, ALU.add))
            link(V.scalar_tensor_tensor(q.e, q.e, 0.2, q.e, ALU.mult, ALU.max))
            if final:
                link(V.tensor_scalar(g.tmpT[:], g.dstf[:, 1:T + 1], float(N), -1e30, ALU.is_equal, ALU.mult))
                link(V.tensor_tensor(heads(q.e), heads(q.e), wide(g.tmpT[:]), ALU.add))
                link(V.tensor_reduce(q.pmax, q.e, AX_X, ALU.max))
                dve.sem_inc(s_max, 1)
                dve.wait_ge(s_mul, 1)
                V.tensor_scalar(q.e, q.e, q.gmax[:, 0:1], None, ALU.subtract).then_inc(s_max, 1)
                dve.wait_ge(s_exp, 1)
                link(V.tensor_copy(g.ad[:].rearrange("p t h -> p h t"), heads(q.e)))
                return
            link(V.tensor_scalar(q.same, q.same, 1e30, -1e30, ALU.mult, ALU.add))
            link(V.tensor_scalar(q.next, q.next, 1e30, -1e30, ALU.mult, ALU.add))
            link(V.tensor_tensor_scan(q.fwd, q.same, q.e, -1e30, ALU.add, ALU.max))
            link(V.tensor_tensor_scan(q.bwd[:, ::-1], q.next[:, ::-1], q.e[:, ::-1], -1e30, ALU.add, ALU.max))
            for h in range(H):
                c = slice(h * P, (h + 1) * P)
                link(V.tensor_scalar(q.diag_in[:, c], g.ident[:], heads(q.fwd)[:, h, T - 1:T], None, ALU.mult))
                link(V.tensor_scalar(q.diag_out[:, c], g.ident[:], heads(q.bwd)[:, h, 0:1], None, ALU.mult))
            reached.append(n[0])
            link(V.tensor_tensor(q.v, q.fwd, q.bwd, ALU.max))
            dve.wait_ge(s_pe, 2)
            for bank, mask, col in ((1, g.no_in, 0), (2, g.no_out, H)):
                both = q.diag_in.rearrange("p (h k) -> p h k", h=H)
                link(V.tensor_tensor(both, g.ps[bank].rearrange("p (h k) -> p h k", h=H),
                                     mask[:, None, :].to_broadcast([P, H, P]), ALU.add))
                link(V.tensor_reduce(q.ends[:, col:col + H], both, AX_X, ALU.max))
            link(V.tensor_scalar(g.tmpT[:], g.in_first[:], 1e30, -1e30, ALU.mult, ALU.add))
            link(V.tensor_scalar(g.tmpT2[:], g.in_last[:], 1e30, -1e30, ALU.mult, ALU.add))
            for h in range(H):
                vh = heads(q.v)[:, h, :]
                link(V.scalar_tensor_tensor(vh, g.tmpT[:], q.ends[:, h:h + 1], vh, ALU.add, ALU.max))
                link(V.scalar_tensor_tensor(vh, g.tmpT2[:], q.ends[:, H + h:H + h + 1], vh, ALU.add, ALU.max))
            V.tensor_tensor(q.e, q.e, q.v, ALU.subtract).then_inc(s_max, 1)
            link(V.tensor_copy(heads(q.same), wide(g.same[:, 0:T])))
            link(V.tensor_copy(heads(q.next), wide(g.same[:, 1:T + 1])))
            dve.wait_ge(s_exp, 1)
            segment_sum(q.e, q.v, 3)
            link(V.tensor_scalar(q.v, q.v, 1e-16, None, ALU.add))
            link(V.reciprocal(q.v, q.v))
            link(V.tensor_tensor(q.e, q.e, q.v, ALU.mult))
            link(V.memset(g.sums_all[:, 0:W], 0.0))
            alpha = q.e.rearrange("p (h t) -> p t h", h=H)

            def body(k, first):
                if not first:
                    dve.wait_ge(s_sum, k * RING)
                V.tensor_copy(g.same_ring[:], g.same[:, bass.ds(k * RING, RING)]).then_inc(s_col, 1)
                part = g.sums[:, bass.ds(k * (RING * W), RING * W)].rearrange("p (t w) -> p t w", w=W)[:, :, 0:D] \
                    .rearrange("p t (h c) -> p t h c", h=H)
                V.tensor_tensor(part, part, alpha[:, bass.ds(k * RING, RING), :, None].to_broadcast([P, RING, H, C]),
                                ALU.mult).then_inc(s_mul, 1)
                dve.wait_ge(s_col, k + 1)
                dve.wait_ge(s_mul, k + 1)
                for j in range(RING):
                    if not (first and j == 0):
                        dve.wait_ge(s_sum, k * RING + j)
                    at = lambda shift: g.sums_all[:, bass.ds((k * RING + j + shift) * W, D)]
                    V.scalar_tensor_tensor(at(1), at(0), g.same_ring[:, j:j + 1], at(1), ALU.mult, ALU.add).then_inc(s_sum, 1)
            body(0, True)
            with dve.Fori(1, T // RING) as k:
                body(k, False)
            dve.wait_ge(s_pe, 4)
            V.tensor_copy(g.carry[:], g.ps[6][:, 0:D]).then_inc(s_zero, 1)

        @block.tensor
        def _(pe):
            def links(n, sem_at):
                pe.wait_ge(s_dve, sem_at)
                A.matmul(g.ps[0][:, 0:H], g.link_in[:], q.ends[:, 0:H], start=True, stop=True)
                A.matmul(g.ps[0][:, H:2 * H], g.link_out[:], q.ends[:, H:2 * H], start=True, stop=True).then_inc(s_pe, 1)
            links(1, reached[0])
            if final:
                return
            pe.wait_ge(s_dve, reached[1])
            A.matmul(g.ps[1], g.ones[:], q.diag_in, start=True, stop=True)
            A.matmul(g.ps[2], g.ones[:], q.diag_out, start=True, stop=True).then_inc(s_pe, 1)
            links(3, reached[2])
            pe.wait_ge(s_sum, T)
            A.matmul(g.ps[6][:, 0:D], g.link_in[:], g.sums[:, (T - 1) * W:(T - 1) * W + D],
                     start=True, stop=True).then_inc(s_pe, 1)
    ph.end()


def by_source(g):
    nc, A, V, ACTE = g.nc, g.nc.tensor, g.nc.vector, g.nc.scalar
    ph = Phase(nc, "bysrc")
    sems = {}

    def s(name):
        if name not in sems:
            sems[name] = ph.sem(name)
        return sems[name]
    B = G4
    steps = T // B

    def over(eng, body):
        body(0, True)
        with eng.Fori(1, steps) as k:
            body(k, False)

    def after(eng, name, k, j, back=0):
        eng.wait_ge(s(name), k * B + j + 1 - back)
    with nc.Block() as block:
        @block.gpsimd
        def _(pool):
            def body(k, first):
                if first != "all":
                    for j in range(B):
                        pool.wait_ge(s(f"row{j}"), k * 16)
                nc.gpsimd.tensor_copy(g.idx_ring[:, 0:B], g.dst_slot_i[:, bass.ds(k * B, B)]).then_inc(s("index"), 1)
                pool.wait_ge(s("index"), k + 1)
                for j in range(B):
                    if first != "all":
                        after(pool, "msg", k, j, B)
                    pool.sem_inc(s("turn"), 1)
                    nc.gpsimd.indirect_dma_start(g.ring[j][:, 0:W], None, g.gat_dram,
                                                 bass.IndirectOffsetOnAxis(g.idx_ring[:, j:j + 1], 0)).then_inc(s(f"row{j}"), 16)
                    if first != "all":
                        add(k - 1, j, first)

            def add(k, j, first):
                after(pool, "sum", k, j)
                after(pool, "index_out", k, j)
                if not (first and j == 0):
                    pool.wait_ge(s("added"), (k * B + j) * 16)
                pool.sem_inc(s("turn"), 1)
                nc.gpsimd.indirect_dma_start(g.U_dram, bass.IndirectOffsetOnAxis(g.add_row[j][:, 0:1], 0), g.RS[j], None,
                                             compute_op=ALU.add).then_inc(s("added"), 16)
            body(0, "all")
            body(1, True)
            with pool.Fori(2, steps) as k:
                body(k, False)
            for j in range(B):
                add(steps - 1, j, False)
            pool.wait_ge(s("added"), 16 * T)

        @block.tensor
        def _(pe):
            def body(k, first):
                for j in range(B):
                    after(pe, "diag", k, j)
                    if not first or j >= 2:
                        after(pe, "same_src", k, j, 2)
                    A.matmul(g.ps[j % 2][:, 0:P], g.ones[:], g.diag[j % 2], start=True, stop=True).then_inc(s("srcrow"), 1)
                    after(pe, "same_src", k, j)
                    after(pe, "msg", k, j)
                    if not first or j >= 2:
                        after(pe, "sum", k, j, 2)
                    A.matmul(g.ps[2 + j % 2][:, 0:W], g.Sm[j % 2], g.msg[j % 2], start=True, stop=True).then_inc(s("sump"), 1)
            over(pe, body)

        @block.scalar
        def _(act):
            def body(k, first):
                for j in range(B):
                    after(act, "sump", k, j)
                    if not first:
                        act.wait_ge(s("added"), (k * B + (j + 1 - B)) * 16)
                    ACTE.activation(g.RS[j], g.ps[2 + j % 2][:, 0:W], ACT.Copy).then_inc(s("sum"), 1)
            over(act, body)

        @block.vector
        def _(dve):
            V.tensor_copy(g.tmpT[:], g.src_i[:]).then_inc(s("pre"), 1)
            V.tensor_copy(g.spare[:], g.spare_i[:]).then_inc(s("pre"), 1)
            dve.wait_ge(s("pre"), 2)
            V.tensor_scalar(g.tmpT2[:], g.dstf[:, 1:T + 1], float(N), g.spare[:, 0:1], ALU.is_equal, ALU.mult).then_inc(s("pre"), 1)
            dve.wait_ge(s("pre"), 3)
            V.tensor_tensor(g.tmpT[:], g.tmpT[:], g.tmpT2[:], ALU.add).then_inc(s("pre"), 1)
            dve.wait_ge(s("pre"), 4)

            def body(k, first):
                V.tensor_copy(g.src_cols[:], g.tmpT[:, bass.ds(k * B, B)])
                V.tensor_copy(g.ex_cols[:], g.ad[:, bass.ds(k * B, B), :]).then_inc(s("cols"), 1)
                dve.wait_ge(s("cols"), k + 1)
                for j in range(B):
                    src = g.src_cols[:, j:j + 1]
                    if not first or j >= 2:
                        after(dve, "srcrow", k, j, 2)
                    V.tensor_scalar(g.diag[j % 2], g.ident[:], src, None, ALU.mult).then_inc(s("diag"), 1)
                    dve.wait_ge(s(f"row{j}"), k * 16 + 16)
                    if not first or j >= 2:
                        after(dve, "sump", k, j, 2)
                    V.tensor_tensor(g.msg[j % 2][:, 0:D].rearrange("p (h c) -> p h c", h=H),
                                    g.ring[j][:, 0:D].rearrange("p (h c) -> p h c", h=H),
                                    g.ex_cols[:, j, :, None].to_broadcast([P, H, C]), ALU.mult)
                    V.tensor_copy(g.msg[j % 2][:, D:W], g.ex_cols[:, j, :]).then_inc(s("msg"), 1)
                    after(dve, "srcrow", k, j)
                    V.tensor_scalar(g.Sm[j % 2], g.ps[j % 2][:, 0:P], src, None, ALU.is_equal).then_inc(s("same_src"), 1)
                    after(dve, "same_src", k, j)
                    V.scalar_tensor_tensor(g.dup_tmp, g.Sm[j % 2], 1.0, g.below[:], ALU.mult, ALU.mult,
                                           accum_out=g.dup[:, 0:1]).then_inc(s("dup"), 1)
                    V.tensor_tensor(g.dup[:, 1:2], g.spare[:], src, ALU.subtract).then_inc(s("dup"), 1)
                    after_dup = (k * B + j) * 4
                    dve.wait_ge(s("dup"), after_dup + 2)
                    V.tensor_scalar(g.dup[:, 2:3], g.dup[:, 0:1], 0.5, g.dup[:, 1:2], ALU.is_gt, ALU.mult).then_inc(s("dup"), 1)
                    dve.wait_ge(s("dup"), after_dup + 3)
                    V.tensor_tensor(g.dup[:, 3:4], g.dup[:, 2:3], src, ALU.add).then_inc(s("dup"), 1)
                    dve.wait_ge(s("dup"), after_dup + 4)
                    if not first:
                        dve.wait_ge(s("added"), (k * B + (j + 1 - B)) * 16)
                    V.tensor_copy(g.add_row[j][:], g.dup[:, 3:4]).then_inc(s("index_out"), 1)
            over(dve, body)
    ph.end()


def last_layer(g):
    nc, A, V, ACTE = g.nc, g.nc.tensor, g.nc.vector, g.nc.scalar
    ph = Phase(nc, "last")
    sems = {}

    def s(name):
        if name not in sems:
            sems[name] = ph.sem(name)
        return sems[name]
    pairs = NCH // 2

    def over(eng, body):
        body(0, True, False)
        with eng.Fori(1, pairs - 1) as k:
            body(k, False, False)
        body(pairs - 1, False, True)

    def rows(table, k, h, last):
        start = N - CH if last and h == 1 else k * (2 * CH) + h * CH
        return table[bass.ds(start, CH), :].rearrange("(p j) f -> p j f", j=G4)

    def after(eng, name, k, h):
        eng.wait_ge(s(name), k * 2 + h + 1)

    def before(eng, name, k, h, first):
        if not first:
            eng.wait_ge(s(name), k * 2 + h - 1)
    with nc.Block() as block:
        @block.sync
        def _(sp):
            def body(k, first, last):
                for h in (0, 1):
                    before(sp, "y", k, h, first)
                    sp.sem_inc(s("turn_sp"), 1)
                    sp.dma_start(g.X[h][:], rows(g.x3_dram, k, h, last)).then_inc(s(f"load_x{h}"), 16)
                    sp.dma_start(g.UB[h][:], rows(g.U_dram, k, h, last)).then_inc(s(f"load_u{h}"), 16)
                for h in (0, 1):
                    after(sp, "o", k, h)
                    sp.sem_inc(s("turn_sp"), 1)
                    if last and h == 1:
                        sp.wait_ge(s("store0"), 16 * pairs)
                    sp.dma_start(rows(g.out, k, h, last), g.Y[h][:]).then_inc(s(f"store{h}"), 16)
            over(sp, body)
            for h in (0, 1):
                sp.wait_ge(s(f"store{h}"), 16 * pairs)

        @block.tensor
        def _(pe):
            def body(k, first, last):
                for h in (0, 1):
                    pe.wait_ge(s(f"load_x{h}"), k * 16 + 16)
                    for j in range(G4):
                        ins = A.transpose(g.psT[h][:, j, :], g.X[h][:, j, :], g.ident[:])
                    ins.then_inc(s("xTp"), 1)
                for h in (0, 1):
                    after(pe, "xT", k, h)
                    before(pe, "u", k, h, first)
                    for j in range(G4):
                        ins = A.matmul(g.psL[h][:, j * D:(j + 1) * D], g.XT[h][:, j, :], g.Wres[:], start=True, stop=True)
                    ins.then_inc(s("up"), 1)
            over(pe, body)

        @block.scalar
        def _(act):
            def body(k, first, last):
                for h in (0, 1):
                    after(act, "xTp", k, h)
                    ACTE.activation(g.XT[h][:], g.psT[h][:], ACT.Copy).then_inc(s("xT"), 1)
                for h in (0, 1):
                    after(act, "neg", k, h)
                    ACTE.activation(g.G[h][:], g.G[h][:], ACT.Exp).then_inc(s("e"), 1)
                for h in (0, 1):
                    after(act, "mv", k, h)
                    ACTE.activation(g.lnv[h][:], g.mv["a"][h][:, :, 1], ACT.Ln, bias=g.eps[:, 0:1]).then_inc(s("ln"), 1)
                for h in (0, 1):
                    after(act, "ln", k, h)
                    ACTE.activation(g.rs["a"][h][:], g.lnv[h][:], ACT.Exp, scale=-0.5).then_inc(s("rs"), 1)
            over(act, body)

        @block.vector
        def _(dve):
            def body(k, first, last):
                for h in (0, 1):
                    dve.wait_ge(s(f"load_u{h}"), k * 16 + 16)
                    V.tensor_scalar(g.den[h][:], g.UB[h][:, :, D:W], 1e-8, None, ALU.add).then_inc(s("d1"), 1)
                for h in (0, 1):
                    after(dve, "d1", k, h)
                    V.reciprocal(g.den[h][:], g.den[h][:]).then_inc(s("d2"), 1)
                for h in (0, 1):
                    after(dve, "d2", k, h)
                    V.tensor_tensor(g.V[h][:].rearrange("p j (h c) -> p j h c", h=H),
                                    g.UB[h][:, :, 0:D].rearrange("p j (h c) -> p j h c", h=H),
                                    g.den[h][:, :, :, None].to_broadcast([P, G4, H, C]), ALU.mult).then_inc(s("agg"), 1)
                for h in (0, 1):
                    after(dve, "agg", k, h)
                    after(dve, "up", k, h)
                    V.tensor_tensor(g.V[h][:].rearrange("p j f -> p (j f)"), g.V[h][:].rearrange("p j f -> p (j f)"),
                                    g.psL[h][:, 0:512], ALU.add).then_inc(s("u"), 1)
                for h in (0, 1):
                    after(dve, "u", k, h)
                    V.tensor_scalar(g.G[h][:], g.V[h][:], 0.0, None, ALU.min).then_inc(s("neg"), 1)
                for h in (0, 1):
                    if not first:
                        dve.wait_ge(s(f"store{h}"), k * 16)
                    V.scalar_tensor_tensor(g.Y[h][:], g.V[h][:], 0.0, g.X[h][:], ALU.max, ALU.add).then_inc(s("y"), 1)
                for h in (0, 1):
                    after(dve, "y", k, h)
                    after(dve, "e", k, h)
                    V.scalar_tensor_tensor(g.Y[h][:], g.G[h][:], -1.0, g.Y[h][:], ALU.add, ALU.add).then_inc(s("z"), 1)
                for h in (0, 1):
                    after(dve, "z", k, h)
                    for j in range(G4):
                        ins = V.bn_stats(g.st["a"][h][:, j, :], g.Y[h][:, j, :])
                    ins.then_inc(s("st"), 1)
                for h in (0, 1):
                    after(dve, "st", k, h)
                    dve.sem_inc(s("turn_dve"), 1)
                    for j in range(G4):
                        ins = V.bn_aggr(g.mv["a"][h][:, j, :], g.st["a"][h][:, j, :])
                    ins.then_inc(s("mv"), 1)
                for h in (0, 1):
                    after(dve, "rs", k, h)
                    for j in range(G4):
                        ins = V.tensor_scalar(g.Y[h][:, j, :], g.Y[h][:, j, :], g.mv["a"][h][:, j, 0:1], g.rs["a"][h][:, j:j + 1],
                                              ALU.subtract, ALU.mult)
                    ins.then_inc(s("o"), 1)
            over(dve, body)
    ph.end()


def build(nc, args, out):
    with ExitStack() as ctx:
        g = Program()
        g.nc, g.args, g.out = nc, args, out

        def sb(name, shape, dt=F32):
            return ctx.enter_context(nc.sbuf_tensor(name, shape, dt))

        def each_slot(name, dt=F32):
            return sb(name, [P, T], dt)

        def dram(name, shape, dt=F32):
            return nc.dram_tensor(name, shape, dt).ap()
        g.tab_dram = dram("tab_dram", (N, 1), I32)
        g.z1_dram, g.x1_dram, g.x2_dram = (dram(n, (N + PAD, D)) for n in ("z1_dram", "x1_dram", "x2_dram"))
        g.xd_dram = dram("xd_dram", (PAD, D))
        g.x3_dram = dram("x3_dram", (N, D))
        g.x3s_dram = dram("x3s_dram", (PAD, D))
        g.gat_dram = dram("gat_dram", (PAD + 1, W))
        g.U_dram = dram("U_dram", (UROWS, W))
        g.ZB, g.ZW = 28, UROWS // P * W // 28
        g.src_i = each_slot("src_i", I32)
        g.dst_i = each_slot("dst_i", I32)
        g.type_i = each_slot("type_i", I32)
        g.slot_i = each_slot("slot_i", I32)
        g.last_node_i = each_slot("last_node_i", I32)
        g.tab_row_i = each_slot("tab_row_i", I32)
        g.src_row_i = each_slot("src_row_i", I32)
        g.src_slot_i = each_slot("src_slot_i", I32)
        g.dst_slot_i = each_slot("dst_slot_i", I32)
        g.own_i = each_slot("own_i", I32)
        g.dst_next_i = sb("dst_next_i", [P, 1], I32)
        g.spare_i = sb("spare_i", [P, 1], I32)
        g.spare = sb("spare", [P, 1])
        g.eps = sb("eps", [P, 1])
        g.idx_ring = sb("idx_ring", [P, RING], I32)
        g.row_ring = sb("row_ring", [P, RING], I32)
        g.dstf = sb("dstf", [P, T + 2])
        g.same = sb("same", [P, T + 1])
        g.typef = each_slot("typef")
        g.is_last = each_slot("is_last")
        g.in_first = each_slot("in_first")
        g.in_last = each_slot("in_last")
        g.tmpT = each_slot("tmpT")
        g.tmpT2 = each_slot("tmpT2")
        g.rcnt = each_slot("rcnt")
        g.w_slot = sb("w_slot", [P, T, R])
        g.ad = sb("ad", [P, T, H])
        g.a_left = sb("a_left", [P, T, H])
        g.ident = sb("ident", [P, P])
        g.ones = sb("ones", [P, P])
        g.below = sb("below", [P, P])
        g.above = sb("above", [P, P])
        g.link_in = sb("link_in", [P, P])
        g.link_out = sb("link_out", [P, P])
        g.no_in = sb("no_in", [P, P])
        g.no_out = sb("no_out", [P, P])
        g.carry = sb("carry", [P, P])
        g.root1 = sb("root1", [P, D])
        g.root2 = sb("root2", [P, D])
        g.Wres = sb("Wres", [P, D])
        g.gamma = sb("gamma", [P, D])
        g.beta = sb("beta", [P, D])
        g.gat_bias = [sb(f"gat_bias{i}", [P, D]) for i in range(3)]
        g.gat_bias_col = sb("gat_bias_col", [P, 2])
        g.Wrel = [sb(f"Wrel{i}", [P, R * D]) for i in range(2)]
        g.WG = [sb(f"WG{i}", [P, W + H]) for i in range(3)]
        g.vd = [g.WG[0][:, W:W + H]]
        g.WH = sb("WH", [P, W])
        g.vleft = sb("vleft", [P, H])
        g.b1_col, g.bself_col, g.bneigh_col = (sb(n, [P, 1]) for n in ("b1_col", "bself_col", "bneigh_col"))
        g.b1_parts, g.b2_parts = (sb(n, [3, D], BF16) for n in ("b1_parts", "b2_parts"))
        g.gate_parts, g.gate_parts_n = (sb(n, [3, 2 * D], BF16) for n in ("gate_parts", "gate_parts_n"))
        g.ones3 = sb("ones3", [3, P], BF16)
        g.A_gate, g.B_gate = (sb(n, [P, 2 * D]) for n in ("A_gate", "B_gate"))
        g.const_row = [sb(f"const_row{i}", [1, W]) for i in range(2)]
        g.edge_ends = sb("edge_ends", [P, 2 * R1])
        two = lambda name, *shape: [sb(f"{name}{h}", [P, *shape]) for h in range(2)]
        g.st, g.mv, g.rs = ({t: two(f"{n}_{t}", *shape) for t in "abcd"}
                            for n, shape in (("st", (G4, 6)), ("mv", (G4, 2)), ("rs", (G4,))))
        g.lnv = two("lnv", G4)
        g.den, g.RW = two("den", G4, H), two("RW", G4, W)
        g.own_ring = [sb(f"own_ring{h}", [P, G4], I32) for h in range(2)]
        g.add_row = [sb(f"add_row{j}", [P, 1], I32) for j in range(G4)]
        g.same_ring = sb("same_ring", [P, RING])
        g.w_ring = sb("w_ring", [P, RING, R])
        g.src_cols = sb("src_cols", [P, G4])
        g.ex_cols = sb("ex_cols", [P, G4, H])
        g.dup = sb("dup", [P, 4])
        psT = [ctx.enter_context(nc.psum_tensor(f"psT{h}", [P, G4, D], F32)) for h in range(2)]
        psM = [ctx.enter_context(nc.psum_tensor(f"psM{h}", [P, G4, D], F32)) for h in range(2)]
        psL = [ctx.enter_context(nc.psum_tensor(f"psL{h}", [P, 1024], F32)) for h in range(2)]
        g.psT, g.psM, g.psL = psT, psM, psL
        flat = lambda t: t[:].rearrange("p j f -> p (j f)")
        g.ps = [flat(psT[0]), flat(psT[1]), psL[0][:, 0:512], psL[0][:, 512:1024], psL[1][:, 0:512], psL[1][:, 512:1024],
                flat(psM[0]), flat(psM[1])]
        sums_all = sb("sums_all", [P, (T + 1) * W])
        g.sums_all, g.sums = sums_all, sums_all[:, W:]

        def carver(region):
            at = [0]

            def carve(*shape, dt=F32):
                n = int(np.prod(shape))
                v = region[:, at[0]:at[0] + n]
                at[0] += n
                assert at[0] <= region.shape[1]
                if dt is not F32:
                    v = v.bitcast(dt)
                names = " ".join(f"a{i}" for i in range(len(shape)))
                return v.rearrange(f"p ({names}) -> p {names}", **{f"a{i}": m for i, m in enumerate(shape)}) if len(shape) > 1 else v
            return carve
        carve = carver(sums_all)
        g.wrel, g.cnt_fwd, g.cnt_bwd = (carve(R1, T) for _ in range(3))
        g.diag_first, g.diag_last, g.bself_rep, g.bneigh_rep, g.att_tmp = (carve(D) for _ in range(5))
        g.WgaT, g.W_self, g.W_neigh, g.WselfT, g.WneighT, g.WgbT = (carve(D) for _ in range(6))
        g.bias_rep = [carve(D) for _ in range(2)]
        g.zero_row = carve(g.ZW)
        g.node_iota = carve(400, dt=I32)
        g.bself_row, g.bneigh_row, g.bgate_row, g.b1_row, g.b2_row = (carve(D)[0:3, :] for _ in range(5))
        g.bias_gate, g.bias_gate_n, g.split_rest, g.split_sum = (carve(2 * D)[0:3, :] for _ in range(4))
        g.split_part = carve(D, dt=BF16)[0:3, :]
        g.att_rows = [carve(D) for _ in range(8)]
        g.Wd = [carve(D) for _ in range(3)]
        carve = carver(sums_all)
        g.UB = [carve(G4, W) for _ in range(2)]
        work = sb("work", [P, 2 * 12 * G4 * D])
        carve = carver(work)
        pair = lambda *shape: [carve(*shape) for _ in range(2)]
        g.X, g.XT, g.Z1T, g.Z1, g.Y, g.G = (pair(G4, D) for _ in range(6))
        g.V, g.X2, g.X3, g.M, g.MT = (pair(G4, D) for _ in range(5))
        carve = carver(work)
        q = g.att = Program()
        q.e, q.v, q.fwd, q.bwd, q.same, q.next = (carve(FT) for _ in range(6))
        q.diag_in, q.diag_out, q.ends, q.pmax, q.gmax = carve(H * P), carve(H * P), carve(2 * H), carve(1), carve(1)
        carve = carver(work)
        g.ring = [carve(W) for _ in range(RING)]
        g.T2 = [carve(D) for _ in range(2)]
        g.acc = [carve(D) for _ in range(2)]
        g.RS = [carve(W) for _ in range(G4)]
        g.diag, g.Sm, g.msg = pair(D), pair(D), pair(W)
        g.dup_tmp = carve(D)

        col = lambda ap: ap.rearrange("(n a) -> n a", a=1)
        spread = lambda ap, at=0, n=P: bass.AP(ap.tensor, at, [[0, n], [1, D]])
        L2 = lambda n: args["L2_gnn_" + n]
        g.dst_next_view = bass.AP(args["dst"].tensor, T, [[T, P - 1], [1, 1]])
        g.weight_loads = [
            (g.W_self, args["L1_gnn_W_self"]), (g.W_neigh, args["L1_gnn_W_neigh"]),
            (g.WselfT, args["W_self_T"]), (g.WneighT, args["W_neigh_T"]),
            (g.WgaT, args["W_gate_T"][0:D, :]), (g.WgbT, args["W_gate_T"][D:2 * D, :]),
            (g.bself_col[:], col(args["L1_gnn_b_self"])), (g.bneigh_col[:], col(args["L1_gnn_b_neigh"])),
            (g.bself_row, spread(args["L1_gnn_b_self"], 0, 3)), (g.bneigh_row, spread(args["L1_gnn_b_neigh"], 0, 3)),
            (g.bgate_row, spread(args["L1_gnn_b_gate"], 0, 3)), (g.b1_col[:], col(args["L0_gnn_b1"])),
            (g.b1_row, spread(args["L0_gnn_b1"], 0, 3)), (g.b2_row, spread(args["L0_gnn_b2"], 0, 3)),
            (g.root1[:], args["L0_gnn_root1"]), (g.root2[:], args["L0_gnn_root2"]),
            (g.Wres[:], args["L3_gnn_residual_projection"]), (g.WH[:, 0:D], args["L3_gnn_W"]),
            (g.gamma[:], spread(args["L1_gnn_ln_gamma"])), (g.beta[:], spread(args["L1_gnn_ln_beta"])),
            (g.Wrel[0][:].rearrange("p (r f) -> p r f", r=R), args["L0_gnn_W1"].rearrange("r i o -> i r o")),
            (g.Wrel[1][:].rearrange("p (r f) -> p r f", r=R), args["L0_gnn_W2"].rearrange("r i o -> i r o")),
            (g.att_rows[6], spread(args["L3_gnn_A_right"])), (g.att_rows[7], spread(args["L3_gnn_A_left"])),
        ]
        for i in range(3):
            g.weight_loads += [
                (g.WG[i][:, 0:D], L2("Ws")[i]), (g.Wd[i], L2("Wd")[i]), (g.gat_bias[i][:], spread(L2("b"), i * D)),
                (g.att_rows[i], spread(L2("att_s"), i * D)), (g.att_rows[3 + i], spread(L2("att_d"), i * D))]
        for i in range(2):
            g.weight_loads.append((g.gat_bias_col[:, i:i + 1], col(L2("b")[i])))
        g.att_products = []
        for i in range(3):
            g.att_products += [(g.WG[i][:, D:W], g.WG[i][:, 0:D], g.att_rows[i]), (g.WG[i][:, W:W + H], g.Wd[i], g.att_rows[3 + i])]
        g.att_products += [(g.WH[:, D:W], g.WH[:, 0:D], g.att_rows[6]), (g.vleft[:], g.WH[:, 0:D], g.att_rows[7])]
        nc.scalar.preload_act_table_set("natural_log_exp_and_others")
        steps = [
            lambda: setup(g),
            lambda: chunks(g, "nodes"),
            lambda: gather(g, "conv", 0), lambda: chunks(g, "z1"),
            lambda: gather(g, "conv", 1), lambda: chunks(g, "x1"),
            lambda: gather(g, "mean"), lambda: chunks(g, "x2"),
            lambda: gather(g, "first"), lambda: attention(g, 0), lambda: chunks(g, "h", 0),
            lambda: gather(g, "rows", 1), lambda: attention(g, 1), lambda: chunks(g, "h", 1),
            lambda: gather(g, "rows", 2), lambda: attention(g, 2), lambda: chunks(g, "x3"),
            lambda: gather(g, "left"), lambda: attention(g, 3), lambda: by_source(g),
            lambda: last_layer(g),
        ]
        for step in steps:
            step()


_INS = ["x", "src", "dst", "edge_type_8", "L0_gnn_W1", "L0_gnn_root1", "L0_gnn_b1", "L0_gnn_W2", "L0_gnn_root2",
        "L0_gnn_b2", "L1_gnn_W_self", "L1_gnn_b_self", "L1_gnn_W_neigh", "L1_gnn_b_neigh", "L1_gnn_b_gate",
        "L1_gnn_ln_gamma", "L1_gnn_ln_beta", "L2_gnn_Ws", "L2_gnn_Wd", "L2_gnn_att_s", "L2_gnn_att_d", "L2_gnn_b",
        "L3_gnn_W", "L3_gnn_A_left", "L3_gnn_A_right", "L3_gnn_residual_projection"]
_TRANSPOSED = {"W_self_T": "L1_gnn_W_self", "W_neigh_T": "L1_gnn_W_neigh", "W_gate_T": "L1_gnn_W_gate"}


def kernel(**inputs):
    import numpy as _np
    import concourse.bacc as _bacc
    from concourse import mybir as _mybir
    from concourse.bass_utils import run_bass_kernel_spmd as _run

    nc = _bacc.Bacc("TRN2", target_bir_lowering=False, num_devices=1)
    laid_out = {name: _np.ascontiguousarray(inputs[name]) for name in _INS}
    for name, of in _TRANSPOSED.items():
        laid_out[name] = _np.ascontiguousarray(_np.asarray(inputs[of]).T)
    arrays = {f"in_{name}": a for name, a in laid_out.items()}
    args = {name: nc.dram_tensor(f"in_{name}", a.shape, _mybir.dt.from_np(a.dtype), kind="ExternalInput").ap()
            for name, a in laid_out.items()}
    out = nc.dram_tensor("out", (N, D), F32, kind="ExternalOutput").ap()
    build(nc, args, out)
    r = _run(nc, [arrays], core_ids=[0])
    return r.results[0]["out"]
```

```python
from contextlib import ExitStack

import numpy as np
import concourse.bass as bass
from concourse import mybir

F32 = mybir.dt.float32
I32 = mybir.dt.int32
BF16 = mybir.dt.bfloat16
ALU = mybir.AluOpType
ACT = mybir.ActivationFunctionType
AX_X = mybir.AxisListType.X

P = 128
N = 50000
E = 25000
D = 128
R = 8
H = 4
C = D // H
T = -(-E // P)
PAD = P * T
FULL = E // T
REST = E - FULL * T
R1 = R + 1
W = D + H
UROWS = 392 * P
SKIP = 1 << 20
LN_EPS = 1e-5
RING = 14


class Program:
    pass


class Phase:

    def __init__(self, nc, name):
        self.nc, self.name, self.sems = nc, name, []

    def sem(self, what):
        s = self.nc.alloc_semaphore(f"{self.name}_{what}")
        self.sems.append(s)
        return s

    def end(self):
        self.nc.clear_and_free_semaphores(self.sems)
        self.nc.all_engine_barrier()


def load_edges(g):
    nc, a = g.nc, g.args
    ph = Phase(nc, "edges")
    s_const, s_edges, s_dve, s_pe = (ph.sem(n) for n in ("const", "loaded", "dve_steps", "pe_steps"))
    with nc.Block() as block:
        @block.sync
        def _(sp):
            sp.wait_ge(s_const, 1)
            for dram, tile in ((a["src"], g.src_i), (a["dst"], g.dst_i), (a["edge_type_8"], g.type_i)):
                sp.dma_start(tile[0:FULL, :], dram[0:FULL * T].rearrange("(p t) -> p t", t=T)).then_inc(s_edges, 16)
                sp.dma_start(tile[FULL:FULL + 1, 0:REST],
                             dram[FULL * T:E].rearrange("(p t) -> p t", t=REST)).then_inc(s_edges, 16)
            with nc.allow_non_contiguous_dma(reason="one value a partition"):
                sp.dma_start(g.dst_next_i[0:P - 1, :], g.dst_next_view).then_inc(s_edges, 16)
            sp.wait_ge(s_edges, 16 * 7)

        @block.gpsimd
        def _(pool):
            nc.gpsimd.memset(g.src_i[:], 0)
            nc.gpsimd.memset(g.dst_i[:], N)
            nc.gpsimd.memset(g.type_i[:], 0)
            nc.gpsimd.memset(g.dst_next_i[:], N + 1).then_inc(s_const, 1)
            nc.gpsimd.memset(g.ones[:], 1.0)
            nc.gpsimd.memset(g.ident[:], 0.0).then_inc(s_const, 1)
            pool.wait_ge(s_const, 2)
            nc.gpsimd.affine_select(out=g.ident[:], in_=g.ident[:], compare_op=ALU.not_equal, fill=1.0,
                                    base=0, pattern=[[-1, P]], channel_multiplier=1).then_inc(s_const, 1)
            nc.gpsimd.affine_select(out=g.below[:], in_=g.ones[:], compare_op=ALU.is_gt, fill=0.0,
                                    base=0, pattern=[[-1, P]], channel_multiplier=1).then_inc(s_const, 1)
            nc.gpsimd.affine_select(out=g.above[:], in_=g.ones[:], compare_op=ALU.is_gt, fill=0.0,
                                    base=0, pattern=[[1, P]], channel_multiplier=-1).then_inc(s_const, 1)

        @block.vector
        def _(dve):
            V = nc.vector
            dve.wait_ge(s_const, 5)
            dve.wait_ge(s_edges, 16 * 7)
            V.tensor_copy(g.dstf[:, 1:T + 1], g.dst_i[:])
            V.tensor_copy(g.dstf[:, T + 1:T + 2], g.dst_next_i[:]).then_inc(s_dve, 1)
            dve.wait_ge(s_dve, 1)
            V.tensor_tensor(g.tmpT[:], g.dstf[:, 1:T + 1], g.dstf[:, 2:T + 2], ALU.is_gt).then_inc(s_dve, 1)
            dve.wait_ge(s_dve, 2)
            V.tensor_reduce(g.spare[:, 0:1], g.tmpT[:], AX_X, ALU.add).then_inc(s_dve, 1)
            dve.wait_ge(s_pe, 1)
            V.tensor_copy(g.unsorted_i[:], g.ps[0][0:1, 0:1]).then_inc(s_dve, 1)

        @block.tensor
        def _(pe):
            pe.wait_ge(s_dve, 3)
            nc.tensor.matmul(g.ps[0][:, 0:1], g.ones[:], g.spare[:, 0:1], start=True, stop=True).then_inc(s_pe, 1)
    ph.end()


def sort_edges(g):
    nc = g.nc
    ph = Phase(nc, "sort")
    s_diag, s_row, s_put, s_dve, s_fill, s_scattered, s_turn, s_back, s_out = (
        ph.sem(n) for n in ("diag", "row", "row_put", "dve_steps", "payload", "scattered", "turn", "read_back", "copied_out"))
    PIECES = 4
    PW = PAD // PIECES
    STEPS = 2 * PIECES + 4
    keys = g.dstf[:, 1:T + 1]
    rank, rank_i = g.tmpT2, g.src_slot_i

    def unsorted(eng):
        return eng.value_load(g.unsorted_i[0:1, 0:1], min_val=0, max_val=PAD)

    with nc.Block() as block:
        @block.vector
        def _(dve):
            with dve.If(unsorted(dve) > 0):
                V = nc.vector
                with dve.Fori(0, T) as t:
                    V.tensor_scalar(g.sort_diag, g.ident[:], keys[:, bass.ds(t, 1)], None, ALU.mult).then_inc(s_diag, 1)
                    dve.wait_ge(s_row, t + 1)
                    V.tensor_copy(g.sort_row[:, bass.ds(t * P, P)], g.ps[0][:, 0:P]).then_inc(s_put, 1)
                    dve.wait_ge(s_put, t + 1)
                with dve.Fori(0, T) as t:
                    key = keys[:, bass.ds(t, 1)]
                    block_of = g.sort_row[:, bass.ds(t * P, P)]
                    n = [0]

                    def link(ins):
                        n[0] += 1
                        ins.then_inc(s_dve, 1)
                        dve.wait_ge(s_dve, t * STEPS + n[0])
                    for i in range(PIECES):
                        link(V.tensor_scalar(g.sort_flags, g.sort_row[:, i * PW:(i + 1) * PW], key, None, ALU.is_lt))
                        link(V.tensor_reduce(g.sort_part[:, i:i + 1], g.sort_flags, AX_X, ALU.add))
                    link(V.scalar_tensor_tensor(g.sort_diag, block_of, key, g.below[:], ALU.is_equal, ALU.mult))
                    link(V.tensor_reduce(g.sort_part[:, PIECES:PIECES + 1], g.sort_diag, AX_X, ALU.add))
                    link(V.tensor_reduce(rank[:, bass.ds(t, 1)], g.sort_part, AX_X, ALU.add))
                    link(V.tensor_scalar(block_of, block_of, -0.5, None, ALU.add))
                V.tensor_copy(rank_i[:], rank[:]).then_inc(s_dve, 1)
                dve.wait_ge(s_back, 32)
                for c, tile in enumerate((g.src_i, g.dst_i, g.type_i)):
                    V.tensor_copy(tile[:], g.sorted_edges[:, :, c]).then_inc(s_out, 1)
            dve.end_ifs()

        @block.tensor
        def _(pe):
            with pe.If(unsorted(pe) > 0):
                with pe.Fori(0, T) as t:
                    pe.wait_ge(s_diag, t + 1)
                    nc.tensor.matmul(g.ps[0][:, 0:P], g.ones[:], g.sort_diag, start=True, stop=True).then_inc(s_row, 1)
            pe.end_ifs()

        @block.gpsimd
        def _(pool):
            with pool.If(unsorted(pool) > 0):
                nc.gpsimd.memset(g.payload[:], 0).then_inc(s_fill, 1)
                pool.wait_ge(s_fill, 1)
                pool.wait_ge(s_dve, T * STEPS + 1)
                with pool.Fori(0, T) as t:
                    nc.gpsimd.tensor_copy(g.idx_ring[:, 0:1], rank_i[:, bass.ds(t, 1)])
                    for c, tile in enumerate((g.src_i, g.dst_i, g.type_i)):
                        ins = nc.gpsimd.tensor_copy(g.payload[:, c:c + 1], tile[:, bass.ds(t, 1)])
                    ins.then_inc(s_fill, 1)
                    pool.wait_ge(s_fill, t + 2)
                    pool.sem_inc(s_turn, 1)
                    nc.gpsimd.indirect_dma_start(g.sorted_dram, bass.IndirectOffsetOnAxis(g.idx_ring[:, 0:1], 0),
                                                 g.payload[:], None).then_inc(s_scattered, 16)
                    pool.wait_ge(s_scattered, t * 16 + 16)
                pool.wait_ge(s_scattered, 16 * T)
            pool.end_ifs()

        @block.sync
        def _(sp):
            with sp.If(unsorted(sp) > 0):
                sp.wait_ge(s_scattered, 16 * T)
                sp.dma_start(g.sorted_edges, g.sorted_dram.rearrange("(p t) c -> p t c", t=T)).then_inc(s_back, 16)
                with nc.allow_non_contiguous_dma(reason="one value a partition"):
                    sp.dma_start(g.dst_next_i[0:P - 1, :],
                                 bass.AP(g.sorted_dram.tensor, 4 * T + 1, [[4 * T, P - 1], [1, 1]])).then_inc(s_back, 16)
                sp.wait_ge(s_back, 32)
            sp.end_ifs()
    ph.end()


def setup(g):
    nc = g.nc
    ph = Phase(nc, "setup")
    s_const, s_w, s_dve, s_pe, s_iota, s_tab0, s_zero = (
        ph.sem(n) for n in ("const", "weights_loaded", "dve_steps", "pe_steps",
                            "iota", "table_filled", "zeros_stored"))
    done = {}
    with nc.Block() as block:
        @block.sync
        def _(sp):
            for tile, view in g.weight_loads:
                sp.dma_start(tile, view).then_inc(s_w, 16)
            sp.wait_ge(s_iota, 1)
            sp.dma_start(g.tab_dram.rearrange("(p t) o -> p (t o)", p=125), g.node_iota[0:125, :]).then_inc(s_tab0, 16)
            sp.wait_ge(s_const, 1)
            sp.dma_start(g.U_dram.rearrange("(p b r) w -> p b (r w)", p=P, b=g.ZB),
                         g.zero_row[:, None, :].to_broadcast([P, g.ZB, g.ZW])).then_inc(s_zero, 16)
            sp.wait_ge(s_w, 16 * len(g.weight_loads))
            sp.wait_ge(s_tab0, 16)
            sp.wait_ge(s_zero, 16)

        @block.gpsimd
        def _(pool):
            nc.gpsimd.memset(g.zero_row, 0.0).then_inc(s_const, 1)
            nc.gpsimd.iota(g.node_iota, [[1, 400]], base=0, channel_multiplier=400).then_inc(s_iota, 1)
            nc.gpsimd.iota(g.spare_i[:], [[1, 1]], base=N, channel_multiplier=1).then_inc(s_const, 1)
            nc.gpsimd.iota(g.slot_i[:], [[1, T]], base=0, channel_multiplier=T).then_inc(s_const, 1)

        @block.vector
        def _(dve):
            n = [0]

            def link(ins):
                n[0] += 1
                ins.then_inc(s_dve, 1)
                dve.wait_ge(s_dve, n[0])

            def mark(what):
                done[what] = n[0]
            V = nc.vector
            dve.wait_ge(s_const, 3)
            dve.wait_ge(s_w, 16 * len(g.weight_loads))
            link(V.tensor_scalar(g.bself_rep, g.ones[:], g.bself_col[:, 0:1], None, ALU.mult))
            link(V.tensor_scalar(g.bneigh_rep, g.ones[:], g.bneigh_col[:, 0:1], None, ALU.mult))
            mark("biases")
            link(V.tensor_copy(g.dstf[:, 1:T + 1], g.dst_i[:]))
            link(V.tensor_copy(g.dstf[:, T + 1:T + 2], g.dst_next_i[:]))
            link(V.tensor_copy(g.typef[:], g.type_i[:]))
            link(V.memset(g.eps[:], LN_EPS))
            link(V.memset(g.ones3[:], 1.0))
            link(V.tensor_scalar(g.own_i[:], g.dst_i[:], float(N - 1), None, ALU.min))
            dst = g.dstf[:, 1:T + 1]
            first, last = g.dstf[:, 1:2], g.dstf[:, T:T + 1]
            link(V.tensor_scalar(g.diag_first, g.ident[:], first, None, ALU.mult))
            link(V.tensor_scalar(g.diag_last, g.ident[:], last, None, ALU.mult))
            mark("ends")
            link(V.memset(g.same[:], 0.0))
            link(V.tensor_tensor(g.same[:, 1:T], g.dstf[:, 2:T + 1], g.dstf[:, 1:T], ALU.is_equal))
            link(V.tensor_tensor(g.is_last[:], dst, g.dstf[:, 2:T + 2], ALU.not_equal))
            link(V.scalar_tensor_tensor(g.is_last[:], dst, float(N), g.is_last[:], ALU.is_lt, ALU.mult))
            link(V.tensor_scalar(g.in_first[:], dst, first, None, ALU.is_equal))
            link(V.tensor_scalar(g.in_last[:], dst, last, None, ALU.is_equal))
            link(V.tensor_scalar(g.tmpT[:], g.is_last[:], -float(SKIP), float(SKIP), ALU.mult, ALU.add))
            link(V.tensor_tensor(g.tmpT[:], g.tmpT[:], dst, ALU.add))
            link(V.tensor_copy(g.last_node_i[:], g.tmpT[:]))
            link(V.tensor_scalar(g.tab_row_i[:], g.slot_i[:], float(N), None, ALU.add))
            dve.wait_ge(s_pe, 6)
            rowF, rowL = g.ps[1][:, 0:P], g.ps[1][:, P:2 * P]
            link(V.scalar_tensor_tensor(g.link_in[:], rowF, last, g.above[:], ALU.is_equal, ALU.mult))
            link(V.scalar_tensor_tensor(g.link_out[:], rowL, first, g.below[:], ALU.is_equal, ALU.mult))
            link(V.scalar_tensor_tensor(g.no_in[:], rowL, first, g.below[:], ALU.is_equal, ALU.mult))
            link(V.scalar_tensor_tensor(g.no_out[:], rowF, last, g.above[:], ALU.is_equal, ALU.mult))
            link(V.tensor_scalar(g.no_in[:], g.no_in[:], 1e30, -1e30, ALU.mult, ALU.add))
            link(V.tensor_scalar(g.no_out[:], g.no_out[:], 1e30, -1e30, ALU.mult, ALU.add))
            link(V.tensor_copy(g.tmpT[:], g.slot_i[:]))
            for r in range(R1):
                oh, fwd, bwd = g.wrel[:, r, :], g.cnt_fwd[:, r, :], g.cnt_bwd[:, r, :]
                if r < R:
                    link(V.tensor_scalar(oh, g.typef[:], float(r), None, ALU.is_equal))
                else:
                    link(V.tensor_tensor(oh, g.tmpT[:], g.is_last[:], ALU.mult))
                link(V.tensor_tensor_scan(fwd, g.same[:, 0:T], oh, 0.0, ALU.mult, ALU.add))
                link(V.tensor_tensor_scan(bwd[:, ::-1], g.same[:, 1:T + 1][:, ::-1], oh[:, ::-1], 0.0, ALU.mult, ALU.add))
            link(V.tensor_copy(g.edge_ends[:, 0:R1], g.cnt_fwd[:, :, T - 1]))
            link(V.tensor_copy(g.edge_ends[:, R1:2 * R1], g.cnt_bwd[:, :, 0]))
            mark("counts")
            dve.wait_ge(s_pe, 8)
            link(V.tensor_copy(g.edge_ends[:], g.ps[2][:, 0:2 * R1]))
            link(V.memset(g.rcnt[:], 0.0))
            for r in range(R1):
                oh, fwd, bwd = g.wrel[:, r, :], g.cnt_fwd[:, r, :], g.cnt_bwd[:, r, :]
                link(V.tensor_tensor(fwd, fwd, bwd, ALU.add))
                link(V.tensor_tensor(fwd, fwd, oh, ALU.subtract))
                link(V.scalar_tensor_tensor(fwd, g.in_first[:], g.edge_ends[:, r:r + 1], fwd, ALU.mult, ALU.add))
                link(V.scalar_tensor_tensor(fwd, g.in_last[:], g.edge_ends[:, R1 + r:R1 + r + 1], fwd, ALU.mult, ALU.add))
                if r == R:
                    link(V.tensor_copy(g.dst_slot_i[:], fwd))
                    continue
                link(V.tensor_tensor(g.rcnt[:], g.rcnt[:], fwd, ALU.add))
                link(V.tensor_scalar(fwd, fwd, 1.0, None, ALU.max))
                link(V.reciprocal(fwd, fwd))
                link(V.tensor_tensor(oh, oh, fwd, ALU.mult))
            link(V.reciprocal(g.rcnt[:], g.rcnt[:]))
            link(V.tensor_copy(g.w_slot[:].rearrange("p t r -> p r t"), g.wrel[:, 0:R, :]))
            dve.wait_ge(s_pe, 4)
            link(V.tensor_tensor(g.A_gate[:, 0:D], g.WselfT, g.ident[:], ALU.subtract))
            link(V.tensor_tensor(g.A_gate[:, D:2 * D], g.WgaT, g.ps[0][:, 0:D], ALU.add))
            link(V.tensor_copy(g.B_gate[:, 0:D], g.WneighT))
            link(V.tensor_copy(g.B_gate[:, D:2 * D], g.ps[0][:, D:2 * D]))
            link(V.tensor_tensor(g.bias_gate[:, D:2 * D], g.bgate_row[:], g.ps[0][0:3, 2 * D:3 * D], ALU.add))
            link(V.tensor_copy(g.bias_gate[:, 0:D], g.bself_row[:]))
            link(V.tensor_tensor(g.bias_gate_n[:, 0:D], g.bself_row[:], g.bneigh_row[:], ALU.add))
            link(V.tensor_tensor(g.bias_gate_n[:, D:2 * D], g.bias_gate[:, D:2 * D], g.ps[0][0:3, 3 * D:4 * D], ALU.add))
            for row, parts, width in ((g.b1_row, g.b1_parts, D), (g.b2_row, g.b2_parts, D),
                                      (g.bias_gate, g.gate_parts, 2 * D), (g.bias_gate_n, g.gate_parts_n, 2 * D)):
                rest, total, piece = g.split_rest[:, 0:width], g.split_sum[:, 0:width], g.split_part[:, 0:width]
                link(V.tensor_copy(rest, row))
                for i in range(3):
                    link(V.tensor_copy(piece, rest))
                    link(V.tensor_tensor(rest, rest, piece, ALU.subtract))
                    pick = g.ident[0:3, i:i + 1]
                    if i == 0:
                        link(V.tensor_scalar(total, piece, pick, None, ALU.mult))
                    else:
                        link(V.scalar_tensor_tensor(total, piece, pick, total, ALU.mult, ALU.add))
                link(V.tensor_copy(parts[:], total))
            for out, w, row in g.att_products:
                link(V.tensor_tensor(g.att_tmp, w, row, ALU.mult))
                link(V.tensor_reduce(out, g.att_tmp[:].rearrange("p (h c) -> p h c", h=H), AX_X, ALU.add))
            for i in range(2):
                link(V.tensor_scalar(g.bias_rep[i], g.ones[:], g.gat_bias_col[:, i:i + 1], 0.0, ALU.mult, ALU.max))
            mark("weights")
            dve.wait_ge(s_pe, 10)
            for i in range(2):
                link(V.tensor_copy(g.const_row[i][:], g.ps[3 + i][0:1, 0:W]))

        @block.tensor
        def _(pe):
            def step(n, ins):
                ins.then_inc(s_pe, 1)
            pe.wait_ge(s_w, 16 * len(g.weight_loads))
            step(1, nc.tensor.matmul(g.ps[0][:, 0:D], g.W_self, g.WgbT, start=True, stop=True))
            step(2, nc.tensor.matmul(g.ps[0][:, D:2 * D], g.W_neigh, g.WgbT, start=True, stop=True))
            pe.wait_ge(s_dve, done["biases"])
            step(3, nc.tensor.matmul(g.ps[0][:, 2 * D:3 * D], g.bself_rep, g.WgbT, start=True, stop=True))
            step(4, nc.tensor.matmul(g.ps[0][:, 3 * D:4 * D], g.bneigh_rep, g.WgbT, start=True, stop=True))
            pe.wait_ge(s_dve, done["ends"])
            step(5, nc.tensor.matmul(g.ps[1][:, 0:P], g.ones[:], g.diag_first, start=True, stop=True))
            step(6, nc.tensor.matmul(g.ps[1][:, P:2 * P], g.ones[:], g.diag_last, start=True, stop=True))
            pe.wait_ge(s_dve, done["counts"])
            step(7, nc.tensor.matmul(g.ps[2][:, 0:R1], g.link_in[:], g.edge_ends[:, 0:R1], start=True, stop=True))
            step(8, nc.tensor.matmul(g.ps[2][:, R1:2 * R1], g.link_out[:], g.edge_ends[:, R1:2 * R1], start=True, stop=True))
            pe.wait_ge(s_dve, done["weights"])
            for i in range(2):
                step(9 + i, nc.tensor.matmul(g.ps[3 + i][:, 0:W], g.bias_rep[i], g.WG[i + 1][:, 0:W], start=True, stop=True))
    ph.end()


G4 = 4
CH = G4 * P
NCH = -(-N // CH)
SCH = T // G4
AHEAD, BEHIND = 4, 2
PEELED = 2


class Chunk:

    def __init__(self, k, h, number, n):
        self.k, self.h, self.number, self.n = k, h, number, n
        self.first = number is not None and number < 2
        self.last = number == n - 1


def rounds(eng, n, turn, *between):
    def step(k, e, number):
        def at(d):
            if number is not None and not 0 <= number + d < n:
                return None
            c = None if number is None else number + d
            return Chunk(k + (e + d) // 2, (e + d) % 2, c, n)
        turn(at)
    end = PEELED + (n - 2 * PEELED - 1 - AHEAD) // 2
    for i in range(-AHEAD, 2 * PEELED):
        step(i // 2, i % 2, i)
    k0 = PEELED
    for first, body, count in between:
        alternate(first())
        with eng.Fori(k0, k0 + count - 1) as k:
            task = body(k - (k0 - 1))
            next(task)
            step(k, 0, None)
            alternate(task)
            step(k, 1, None)
        k0 += count - 1
    with eng.Fori(k0, end) as k:
        step(k, 0, None)
        step(k, 1, None)
    for i in range(2 * end, n + BEHIND):
        step(i // 2, i % 2, i)


def alternate(*parts):
    parts = [p for p in parts if p is not None]
    while parts:
        for p in list(parts):
            try:
                next(p)
            except StopIteration:
                parts.remove(p)


def in_order(names, **parts):
    for name in names.split():
        if parts[name] is not None:
            next(parts[name], None)


def opt(part, c):
    return part(c) if c is not None else None


class Signals:

    def __init__(self, ph):
        self.ph, self.of = ph, {}

    def __call__(self, name):
        if name not in self.of:
            self.of[name] = self.ph.sem(name)
        return self.of[name]

    def after(self, eng, name, c):
        eng.wait_ge(self(name), c.k * 2 + c.h + 1)

    def shifted(self, eng, name, c, by):
        if c.number is None or 0 <= c.number + by < c.n:
            eng.wait_ge(self(name), c.k * 2 + (c.h + 1 + by))

    def before(self, eng, name, c):
        if not c.first:
            eng.wait_ge(self(name), c.k * 2 + c.h - 1)

    def loaded(self, eng, which, c, dmas=1):
        eng.wait_ge(self(f"load_{which}{c.h}"), c.k * (16 * dmas) + 16 * dmas)

    def stored(self, eng, name, c, dmas=1):
        if not c.first:
            eng.wait_ge(self(f"store_{name}{c.h}"), c.k * (16 * dmas))


def node_rows(g, ph, pool):
    nc = g.nc
    s_idx, s_scattered, s_turn = (ph.sem(n) for n in ("tab_index_copied", "tab_scattered", "tab_turn"))
    group = RING // 2
    steps = T // group

    def scatter(k=None):
        if k is not None:
            pool.wait_ge(s_scattered, k * (16 * group))
        columns = slice(0, group) if k is None else bass.ds(k * group, group)
        nc.gpsimd.tensor_copy(g.idx_ring[:, 0:group], g.last_node_i[:, columns])
        nc.gpsimd.tensor_copy(g.row_ring[:, 0:group], g.tab_row_i[:, columns]).then_inc(s_idx, 1)
        pool.wait_ge(s_idx, 1 if k is None else k + 1)
        pool.sem_inc(s_turn, 1)
        for j in range(group):
            if j == group // 2:
                yield
            nc.gpsimd.indirect_dma_start(g.tab_dram, bass.IndirectOffsetOnAxis(g.idx_ring[:, j:j + 1], 0),
                                         g.row_ring[:, j:j + 1], None, bounds_check=N - 1,
                                         oob_is_err=False).then_inc(s_scattered, 16)

    def done():
        pool.wait_ge(s_scattered, 16 * T)
    return (scatter, scatter, steps), done


def slots_of_sources(g, pool, s_slots):
    nc = g.nc
    for i, op in enumerate([
            lambda: nc.gpsimd.tensor_scalar(g.tmpT[:], g.src_row_i[:], -float(N), None, ALU.add),
            lambda: nc.gpsimd.tensor_scalar(g.tmpT2[:], g.tmpT[:], 0.0, float(PAD), ALU.is_lt, ALU.mult),
            lambda: nc.gpsimd.tensor_scalar(g.tmpT[:], g.tmpT[:], 0.0, None, ALU.max),
            lambda: nc.gpsimd.tensor_tensor(g.tmpT[:], g.tmpT[:], g.tmpT2[:], ALU.add),
            lambda: nc.gpsimd.tensor_copy(g.src_slot_i[:], g.tmpT[:])]):
        op().then_inc(s_slots, 1)
        pool.wait_ge(s_slots, i + 1)


def chunks(g, mode, layer=0):
    nc = g.nc
    dense = mode == "nodes"
    ph = Phase(nc, f"{mode}{layer}")
    s = Signals(ph)
    after, before, shifted, loaded, stored = s.after, s.before, s.shifted, s.loaded, s.stored
    A, V, ACTE = nc.tensor, nc.vector, nc.scalar
    n_chunks = NCH if dense else SCH

    def rows(table, c):
        if dense:
            start = N - CH if c.last else c.k * (2 * CH) + c.h * CH
            return table[bass.ds(start, CH), :].rearrange("(p j) f -> p j f", j=G4)
        return table.rearrange("(p t) f -> p t f", t=T)[:, bass.ds(c.k * (2 * G4) + c.h * G4, G4), :]

    def slots(t, c):
        return t[:, bass.ds(c.k * (2 * G4) + c.h * G4, G4)]

    part = (lambda t: t[0:N, :]) if dense else (lambda t: t[N:N + PAD, :])
    loads = {"nodes": [("a", g.X, g.args["x"], "y", 4)],
             "x1": [("a", g.X, g.z1_dram[N:N + PAD, :], "xT", 3), ("b", g.G, g.xd_dram, "y", 3)],
             "x2": [("a", g.X, g.x1_dram[N:N + PAD, :], "x1Tp", 4), ("b", g.Y, g.x1_dram[N:N + PAD, :], "w", 2)],
             "x3": [("a", g.X2, g.x2_dram[N:N + PAD, :], "x3p", 3)]}.get(mode, [])
    stores = {"nodes": [("z1", g.Z1, part(g.z1_dram), "z1r", 3), ("x1", g.Y, part(g.x1_dram), "x1", 2),
                        ("x2", g.X2, part(g.x2_dram), "x2", -1), ("x3", g.X3, g.x3_dram, "x3", -1)],
              "z1": [("xd", g.Y, g.xd_dram, "xd", 2), ("z1", g.Z1, part(g.z1_dram), "z1r", 0)],
              "x1": [("x1", g.V, part(g.x1_dram), "x1", 0)],
              "x2": [("x2", g.X2, part(g.x2_dram), "x2", -1)],
              "h": [("rows", g.RW, g.gat_dram[0:PAD, :], "rw", 0)],
              "x3": [("x3", g.V, g.x3s_dram, "x3", 0), ("rows", g.RW, g.gat_dram[0:PAD, :], "rw", -1)]}[mode]

    def gate_view(c):
        return g.psL[c.h][:].rearrange("p (j w) -> p j w", j=G4)

    def second_half(c):
        return g.psL[c.h][:, 512:1024].rearrange("p (j f) -> p j f", j=G4)

    with nc.Block() as block:
        @block.sync
        def _(sp):
            if mode == "h":
                sp.dma_start(g.gat_dram[PAD:PAD + 1, :], g.const_row[layer][:]).then_inc(s("const_row"), 16)

            def turn(at):
                for which, buf, table, free, ahead in loads:
                    c = at(ahead)
                    if c is not None:
                        before(sp, free, c)
                        sp.sem_inc(s("turn_sp"), 1)
                        sp.dma_start(buf[c.h][:], rows(table, c)).then_inc(s(f"load_{which}{c.h}"), 16)
                for name, buf, table, ready, ahead in sorted(stores, key=lambda st: st[4] == 3):
                    c = at(ahead)
                    if c is not None:
                        after(sp, ready, c)
                        sp.sem_inc(s("turn_sp"), 1)
                        if dense and c.last:
                            sp.wait_ge(s(f"store_{name}{1 - c.h}"), 16 * (n_chunks // 2))
                        sp.dma_start(rows(table, c), buf[c.h][:]).then_inc(s(f"store_{name}{c.h}"), 16)
            rounds(sp, n_chunks, turn)
            if mode == "h":
                sp.wait_ge(s("const_row"), 16)
            for name, *_ in stores:
                for h in (0, 1):
                    sp.wait_ge(s(f"store_{name}{h}"), 16 * ((n_chunks + 1 - h) // 2))

        if dense or mode == "x2":
            @block.gpsimd
            def _(pool):
                def spread(row):
                    return row[:, None, :].to_broadcast([P, G4, D])

                def scaled(c):
                    after(pool, "vn", c)
                    nc.gpsimd.tensor_tensor(g.V[c.h][:], g.V[c.h][:], spread(g.gamma), ALU.mult).then_inc(s("vg"), 1)
                    after(pool, "vg", c)
                    nc.gpsimd.tensor_tensor(g.V[c.h][:], g.V[c.h][:], spread(g.beta), ALU.add).then_inc(s("vb"), 1)

                def shift(c, t, name):
                    after(pool, f"rs{t}", c)
                    before(pool, name, c)
                    pool.sem_inc(s("turn_pool"), 1)
                    nc.gpsimd.tensor_scalar(g.nb[t][c.h][:], g.mv[t][c.h][:, :, 0], -1.0, None, ALU.mult).then_inc(s(f"neg{t}"), 1)
                    after(pool, f"neg{t}", c)
                    nc.gpsimd.tensor_tensor(g.nb[t][c.h][:], g.nb[t][c.h][:], g.rs[t][c.h][:], ALU.mult).then_inc(s(f"nb{t}"), 1)

                def turn(at):
                    if at(0):
                        scaled(at(0))
                    c = at(-1)
                    if c and dense:
                        after(pool, "x2", c)
                        stored(pool, "x3", c)
                        nc.gpsimd.tensor_tensor(g.X3[c.h][:], g.X2[c.h][:], spread(g.gat_bias[2]), ALU.add).then_inc(s("x3p"), 1)
                    if c and dense:
                        shift(c, "d", "x3")
                    if at(0):
                        shift(at(0), "c", "x2")
                if dense:
                    task, task_done = node_rows(g, ph, pool)
                    rounds(pool, n_chunks, turn, task)
                    task_done()
                else:
                    rounds(pool, n_chunks, turn)

        if mode == "z1":
            @block.gpsimd
            def _(pool):
                def turn(at):
                    c = at(3)
                    if c is None:
                        return
                    before(pool, "xTp", c)
                    before(pool, "xd", c)
                    nc.gpsimd.tensor_copy(g.own_ring[c.h][:], slots(g.own_i, c)).then_inc(s("own"), 1)
                    after(pool, "own", c)
                    pool.sem_inc(s("turn"), 1)
                    for j in range(G4):
                        nc.gpsimd.indirect_dma_start(
                            g.X[c.h][:, j, :], None, g.args["x"],
                            bass.IndirectOffsetOnAxis(g.own_ring[c.h][:, j:j + 1], 0)).then_inc(s(f"load_a{c.h}"), 16)
                rounds(pool, n_chunks, turn)

        if mode == "x3":
            @block.gpsimd
            def _(pool):
                def turn(at):
                    c = at(0)
                    if c is None:
                        return
                    if not c.first:
                        pool.wait_ge(s(f"scatter{c.h}"), c.k * (16 * G4))
                    nc.gpsimd.tensor_copy(g.own_ring[c.h][:], slots(g.last_node_i, c)).then_inc(s("own"), 1)
                    after(pool, "own", c)
                    after(pool, "x3", c)
                    pool.sem_inc(s("turn"), 1)
                    for j in range(G4):
                        nc.gpsimd.indirect_dma_start(
                            g.x3_dram, bass.IndirectOffsetOnAxis(g.own_ring[c.h][:, j:j + 1], 0),
                            g.V[c.h][:, j, :], None, bounds_check=N - 1, oob_is_err=False
                        ).then_inc(s(f"scatter{c.h}"), 16)
                rounds(pool, n_chunks, turn)
                for h in (0, 1):
                    pool.wait_ge(s(f"scatter{h}"), 16 * G4 * ((n_chunks + 1 - h) // 2))

        @block.tensor
        def _(pe):
            def transposes(out, src):
                for j in range(G4):
                    ins = A.transpose(out[:, j, :], src[:, j, :], g.ident[:])
                return ins

            def product(out, lhs, weights, bias=None):
                for j in range(G4):
                    if bias is not None:
                        A.matmul(out[:, j, :], g.ones3[:], bias[:], start=True, stop=False)
                    ins = A.matmul(out[:, j, :], lhs[:, j, :], weights, start=bias is None, stop=True)
                return ins

            def x_products(c):
                loaded(pe, "a", c, G4 if mode == "z1" else 1)
                if mode != "z1":
                    before(pe, "y", c)
                transposes(g.psT[c.h], g.X[c.h]).then_inc(s("xTp"), 1)
                yield
                after(pe, "xT", c)
                if mode == "z1":
                    before(pe, "z1q", c)
                    product(second_half(c), g.XT[c.h], g.root1[:], g.b1_parts).then_inc(s("z1p"), 1)
                if dense:
                    before(pe, "v", c)
                    A.matmul(g.psL[c.h][:, 0:512], g.root1[:], g.XT[c.h][:].rearrange("p j f -> p (j f)"),
                             start=True, stop=True).then_inc(s("z1Tp"), 1)
                yield
                if dense:
                    after(pe, "z1T", c)
                if mode != "z1":
                    product(g.psT[c.h], g.Z1T[c.h] if dense else g.XT[c.h], g.root2[:], g.b2_parts).then_inc(s("z2p"), 1)
                yield
                if dense:
                    transposes(second_half(c), g.Z1T[c.h]).then_inc(s("z1p"), 1)
                yield

            def gate_inputs(c):
                if dense:
                    after(pe, "x1", c)
                else:
                    loaded(pe, "a", c)
                    shifted(pe, "adT", c, -6)
                transposes(g.psT[c.h], (g.Y if dense else g.X)[c.h]).then_inc(s("x1Tp"), 1)
                yield
                if not dense:
                    after(pe, "mean", c)
                    shifted(pe, "ad", c, -6)
                    transposes(g.psM[c.h], g.M[c.h]).then_inc(s("mTp"), 1)
                yield

            def gate_products(c):
                after(pe, "x1T", c)
                if not dense:
                    after(pe, "mT", c)
                    before(pe, "v", c)
                L = gate_view(c)
                for j in range(G4):
                    A.matmul(L[:, j, :], g.ones3[:], (g.gate_parts if dense else g.gate_parts_n)[:], start=True, stop=False)
                    ins = A.matmul(L[:, j, :], g.XT[c.h][:, j, :], g.A_gate[:], start=False, stop=dense)
                    if not dense:
                        ins = A.matmul(L[:, j, :], g.MT[c.h][:, j, :], g.B_gate[:], start=False, stop=True)
                ins.then_inc(s("Lp"), 1)
                yield

            def right_values(c):
                after(pe, "x2", c)
                shifted(pe, "x1T", c, 4)
                transposes(g.psT[c.h], g.X2[c.h]).then_inc(s("adTp"), 1)
                yield
                after(pe, "adT", c)
                for j in range(G4):
                    ins = A.matmul(g.psM[c.h][:, j, 0:H], g.Z1[c.h][:, j, :], g.vd[0], start=True, stop=True)
                ins.then_inc(s("adp"), 1)
                yield

            def next_rows(c):
                src, wts, wd = (g.Y, g.WG[layer + 1], W + H) if mode == "h" else (g.V, g.WH, W)
                after(pe, "hr" if mode == "h" else "x3", c)
                transposes(g.psT[c.h], src[c.h]).then_inc(s("hTp"), 1)
                yield
                after(pe, "hT", c)
                before(pe, "rw", c)
                L = gate_view(c)
                for j in range(G4):
                    ins = A.matmul(L[:, j, 0:wd], g.XT[c.h][:, j, :], wts[:], start=True, stop=True)
                ins.then_inc(s("rwp"), 1)
                yield

            def turn(at):
                if dense:
                    in_order("x x inputs x product x", x=opt(x_products, at(3)),
                             inputs=opt(gate_inputs, at(2)), product=opt(gate_products, at(2)))
                elif mode in ("z1", "x1"):
                    alternate(opt(x_products, at(2)))
                elif mode == "x2":
                    in_order("values product values inputs inputs", values=opt(right_values, at(-2)),
                             product=opt(gate_products, at(2)), inputs=opt(gate_inputs, at(3)))
                elif mode == "h":
                    alternate(opt(next_rows, at(0)))
                else:
                    alternate(opt(next_rows, at(-1)))
            rounds(pe, n_chunks, turn)

        @block.scalar
        def _(act):
            def copy(out, src, name):
                ACTE.activation(out, src, ACT.Copy).then_inc(s(name), 1)

            def rstd(c, t):
                after(act, f"mv{t}", c)
                ACTE.activation(g.lnv[t][c.h][:], g.mv[t][c.h][:, :, 1], ACT.Ln, bias=g.eps[:, 0:1]).then_inc(s(f"ln{t}"), 1)
                yield
                after(act, f"ln{t}", c)
                ACTE.activation(g.rs[t][c.h][:], g.lnv[t][c.h][:], ACT.Exp, scale=-0.5).then_inc(s(f"rs{t}"), 1)
                yield

            def norm(c, t):
                return rstd(c, t) if c is not None else None

            def normed(c, t, src, dst, name):
                if c is None:
                    return
                after(act, f"nb{t}", c)
                if name == "x2":
                    stored(act, "x2", c)
                    before(act, "x3p" if dense else "adTp", c)
                for j in range(G4):
                    ins = ACTE.activation(dst[c.h][:, j, :], src[c.h][:, j, :], ACT.Identity,
                                          bias=g.nb[t][c.h][:, j:j + 1], scale=g.rs[t][c.h][:, j:j + 1])
                ins.then_inc(s(name), 1)
                yield

            def x_transposed(c):
                after(act, "xTp", c)
                copy(g.XT[c.h][:], g.psT[c.h][:], "xT")
                yield
                if mode == "z1":
                    stored(act, "xd", c)
                    copy(g.Y[c.h][:], g.X[c.h][:], "xd")
                    yield
                if dense:
                    after(act, "z1Tp", c)
                    ACTE.activation(g.Z1T[c.h][:].rearrange("p j f -> p (j f)"), g.psL[c.h][:, 0:512], ACT.Relu,
                                    bias=g.b1_col[:, 0:1]).then_inc(s("z1T"), 1)
                    yield
                    after(act, "z1p", c)
                    stored(act, "z1", c)
                    copy(g.Z1[c.h][:], second_half(c), "z1r")
                    yield

            def gate_transposed(c):
                after(act, "x1Tp", c)
                copy(g.XT[c.h][:], g.psT[c.h][:], "x1T")
                yield
                if mode == "x2":
                    after(act, "mTp", c)
                    copy(g.MT[c.h][:], g.psM[c.h][:], "mT")
                yield

            def gate(c):
                after(act, "Lp", c)
                before(act, "v2", c)
                ACTE.activation(g.G[c.h][:], gate_view(c)[:, :, D:2 * D], ACT.Exp, scale=-1.0).then_inc(s("g1"), 1)
                yield
                after(act, "g1", c)
                ACTE.activation(g.G[c.h][:], g.G[c.h][:], ACT.Ln, bias=g.ones[:, 0:1]).then_inc(s("g2"), 1)
                yield
                after(act, "g2", c)
                ACTE.activation(g.G[c.h][:], g.G[c.h][:], ACT.Exp, scale=-1.0).then_inc(s("g"), 1)
                yield

            def right_values(c):
                after(act, "adTp", c)
                copy(g.Z1[c.h][:], g.psT[c.h][:], "adT")
                yield
                after(act, "adp", c)
                copy(slots(g.ad, c), g.psM[c.h][:, :, 0:H], "ad")
                yield

            def next_rows(c):
                after(act, "hTp", c)
                copy(g.XT[c.h][:], g.psT[c.h][:], "hT")
                yield
                after(act, "rwp", c)
                stored(act, "rows", c)
                L = gate_view(c)
                ACTE.activation(g.RW[c.h][:], L[:, :, 0:W], ACT.Copy)
                copy(slots(g.ad, c), L[:, :, W:W + H] if mode == "h" else L[:, :, D:W], "rw")
                yield

            def turn(at):
                if dense:
                    in_order("x a a x inputs d d b b c c x3 x2 gate gate gate x",
                             x=opt(x_transposed, at(3)), a=norm(at(2), "a"), b=norm(at(1), "b"),
                             c=norm(at(0), "c"), d=norm(at(-1), "d"),
                             inputs=opt(gate_transposed, at(2)), gate=opt(gate, at(2)),
                             x3=normed(at(-1), "d", g.X3, g.X3, "x3"), x2=normed(at(0), "c", g.V, g.X2, "x2"))
                elif mode == "z1":
                    alternate(opt(x_transposed, at(2)))
                elif mode == "x1":
                    alternate(opt(x_transposed, at(2)))
                    alternate(norm(at(1), "a"))
                elif mode == "x2":
                    in_order("values values gate inputs inputs gate gate b b c c x2",
                             inputs=opt(gate_transposed, at(3)), gate=opt(gate, at(2)), values=opt(right_values, at(-2)),
                             b=norm(at(1), "b"), c=norm(at(0), "c"), x2=normed(at(0), "c", g.V, g.X2, "x2"))
                elif mode == "h":
                    alternate(opt(next_rows, at(0)))
                else:
                    alternate(opt(next_rows, at(-1)), norm(at(1), "d"))
            rounds(act, n_chunks, turn)

        @block.vector
        def _(dve):
            def stats(c, t, src):
                for j in range(G4):
                    ins = V.bn_stats(g.st[t][c.h][:, j, :], src[c.h][:, j, :])
                ins.then_inc(s(f"st{t}"), 1)
                yield
                after(dve, f"st{t}", c)
                dve.sem_inc(s("turn_dve"), 1)
                for j in range(G4):
                    ins = V.bn_aggr(g.mv[t][c.h][:, j, :], g.st[t][c.h][:, j, :])
                ins.then_inc(s(f"mv{t}"), 1)
                yield

            def normed(c, t, src, dst, name):
                after(dve, f"rs{t}", c)
                for j in range(G4):
                    ins = V.tensor_scalar(dst[c.h][:, j, :], src[c.h][:, j, :], g.mv[t][c.h][:, j, 0:1],
                                          g.rs[t][c.h][:, j:j + 1], ALU.subtract, ALU.mult)
                ins.then_inc(s(name), 1)

            def sums_with_carry(dst, c):
                for j in range(G4):
                    t = c.k * (2 * G4) + c.h * G4 + j
                    ins = V.scalar_tensor_tensor(dst[c.h][:, j, :], g.carry[:], g.in_first[:, bass.ds(t, 1)],
                                                 g.sums[:, bass.ds(t * W, D)], ALU.mult, ALU.add)
                return ins

            def spread(row):
                return row[:, None, :].to_broadcast([P, G4, D])

            def sums(c):
                if mode == "z1":
                    before(dve, "z1r", c)
                elif mode == "x1":
                    before(dve, "y", c)
                elif mode == "x2":
                    before(dve, "mTp", c)
                elif mode == "h":
                    before(dve, "hTp", c)
                else:
                    before(dve, "hp", c)
                sums_with_carry(g.Y if mode == "h" else g.M, c).then_inc(s("agg"), 1)
                yield
                if mode == "x2":
                    after(dve, "agg", c)
                    V.tensor_tensor(g.M[c.h][:], g.M[c.h][:], slots(g.rcnt, c)[:, :, None].to_broadcast([P, G4, D]),
                                    ALU.mult).then_inc(s("mean"), 1)
                yield

            def z1(c):
                after(dve, "agg", c)
                after(dve, "z1p", c)
                V.tensor_tensor(g.M[c.h][:], g.M[c.h][:], second_half(c), ALU.add).then_inc(s("z1q"), 1)
                yield
                after(dve, "z1q", c)
                stored(dve, "z1", c)
                V.tensor_scalar(g.Z1[c.h][:], g.M[c.h][:], 0.0, None, ALU.max).then_inc(s("z1r"), 1)
                yield

            def x1(c):
                if not dense:
                    after(dve, "agg", c)
                    after(dve, "z2p", c)
                    V.tensor_tensor(g.M[c.h][:], g.M[c.h][:], g.psT[c.h][:], ALU.add).then_inc(s("z2q"), 1)
                    yield
                    after(dve, "z2q", c)
                    loaded(dve, "b", c)
                    z2, x = g.M, g.G
                else:
                    after(dve, "z2p", c)
                    before(dve, "x1", c)
                    z2, x = g.psT, g.X
                if not dense:
                    before(dve, "x1", c)
                y = g.M if dense else g.Y
                V.scalar_tensor_tensor(y[c.h][:], z2[c.h][:], 0.0, x[c.h][:], ALU.max, ALU.add).then_inc(s("y"), 1)
                yield
                after(dve, "y", c)
                yield from stats(c, "a", y)
                if dense:
                    yield from x1_norm(c)

            def x1_norm(c):
                stored(dve, "x1", c)
                if dense:
                    before(dve, "w", c)
                    normed(c, "a", g.M, g.Y, "x1")
                else:
                    normed(c, "a", g.Y, g.V, "x1")
                yield

            def gated(c):
                if not dense:
                    loaded(dve, "b", c)
                after(dve, "g", c)
                V.tensor_tensor(g.G[c.h][:], g.G[c.h][:], gate_view(c)[:, :, 0:D], ALU.mult).then_inc(s("v"), 1)
                yield
                after(dve, "v", c)
                before(dve, "x2", c)
                V.tensor_tensor(g.V[c.h][:], g.G[c.h][:], g.Y[c.h][:], ALU.add).then_inc(s("v2"), 1)
                yield
                after(dve, "v2", c)
                yield from stats(c, "b", g.V)

            def x2(c):
                normed(c, "b", g.V, g.V, "vn")
                yield
                yield
                yield
                after(dve, "vb", c)
                V.scalar_tensor_tensor(g.V[c.h][:], g.V[c.h][:], 0.0, g.Y[c.h][:], ALU.max, ALU.add).then_inc(s("w"), 1)
                yield
                after(dve, "w", c)
                yield from stats(c, "c", g.V)

            def x3(c):
                after(dve, "x3p", c)
                yield from stats(c, "d", g.X3)

            def layer_out(c):
                X = g.Y if mode == "h" else g.X3
                if mode == "x3":
                    before(dve, "x3", c)
                after(dve, "agg", c)
                V.tensor_tensor(X[c.h][:], (g.Y if mode == "h" else g.M)[c.h][:], spread(g.gat_bias[layer if mode == "h" else 2]), ALU.add).then_inc(s("hp"), 1)
                yield
                after(dve, "hp", c)
                if mode == "h":
                    V.tensor_scalar(X[c.h][:], X[c.h][:], 0.0, None, ALU.max).then_inc(s("hr"), 1)
                    yield
                    return
                loaded(dve, "a", c)
                V.tensor_tensor(X[c.h][:], X[c.h][:], g.X2[c.h][:], ALU.add).then_inc(s("x3p"), 1)
                yield
                after(dve, "x3p", c)
                yield from stats(c, "d", X)

            def x3_norm(c):
                stored(dve, "x3", c)
                before(dve, "hTp", c)
                if not c.first:
                    dve.wait_ge(s(f"scatter{c.h}"), c.k * (16 * G4))
                normed(c, "d", g.X3, g.V, "x3")
                yield

            def turn(at):
                if dense:
                    in_order("x1 x2 x1 x1 gated gated x2 x2 x2 x1 x3 x3 gated gated x2 x2",
                             x1=opt(x1, at(2)), x2=opt(x2, at(0)), x3=opt(x3, at(-1)), gated=opt(gated, at(1)))
                elif mode == "z1":
                    alternate(opt(sums, at(2)), opt(z1, at(1)))
                elif mode == "x1":
                    in_order("x1 sums x1 norm x1 x1", norm=opt(x1_norm, at(0)), x1=opt(x1, at(1)),
                             sums=opt(sums, at(2)))
                elif mode == "x2":
                    in_order("gated x2 sums sums gated gated gated x2 x2 x2 x2 x2",
                             x2=opt(x2, at(0)), gated=opt(gated, at(1)), sums=opt(sums, at(3)))
                elif mode == "h":
                    alternate(opt(layer_out, at(1)), opt(sums, at(2)))
                else:
                    in_order("out sums out norm out out", norm=opt(x3_norm, at(0)), out=opt(layer_out, at(1)),
                             sums=opt(sums, at(2)))
            rounds(dve, n_chunks, turn)
    ph.end()


FT = H * T


def gather(g, mode, layer=0):
    nc, A, V, ACTE = g.nc, g.nc.tensor, g.nc.vector, g.nc.scalar
    ph = Phase(nc, f"{mode}{layer}g")
    sems = {}

    def s(name):
        if name not in sems:
            sems[name] = ph.sem(name)
        return sems[name]
    table, index, width = {
        "conv": (g.z1_dram if layer else g.args["x"], g.src_row_i if layer else g.src_i, D),
        "mean": (g.x1_dram, g.src_row_i, D), "first": (g.x2_dram, g.src_row_i, D),
        "rows": (g.gat_dram, g.src_slot_i, W), "left": (g.x3_dram, g.src_i, D)}[mode]
    steps = T // RING
    rows_of_sources = mode == "conv" and layer == 0
    used = {"conv": "tp", "mean": "sum", "first": "tp", "rows": "put", "left": "tp"}[mode]

    def over(eng, body):
        body(0, True)
        with eng.Fori(1, steps) as k:
            body(k, False)

    def after(eng, name, k, j, back=0):
        eng.wait_ge(s(name), k * RING + j + 1 - back)

    def row_of(k, j, shift=0, width=D):
        return g.sums_all[:, bass.ds((k * RING + j + shift) * W, width)]

    with nc.Block() as block:
        @block.gpsimd
        def _(pool):
            def body(k, half, number=None):
                at = half * RING
                if number is None or number >= 2:
                    for j in range(RING):
                        pool.wait_ge(s(f"row{j}"), (k - 1) * 16)
                if rows_of_sources and number != 0:
                    pool.wait_ge(s("tab_row"), k * (16 * RING))
                    nc.gpsimd.tensor_copy(g.src_row_i[:, bass.ds((k - 1) * RING, RING)], g.row_ring[:]).then_inc(s("tab_moved"), 1)
                nc.gpsimd.tensor_copy(g.idx_ring[:, at:at + RING], index[:, bass.ds(k * RING, RING)]).then_inc(s("index"), 1)
                pool.wait_ge(s("index"), k + 1)
                for j in range(RING):
                    row_index = bass.IndirectOffsetOnAxis(g.idx_ring[:, at + j:at + j + 1], 0)
                    if number != 0:
                        pool.wait_ge(s(used), k * RING + (j + 1 - RING))
                    pool.sem_inc(s("turn"), 1)
                    nc.gpsimd.indirect_dma_start(g.ring[j][:, 0:width], None, table, row_index).then_inc(s(f"row{j}"), 16)
                    if rows_of_sources:
                        if j == 0 and number != 0:
                            pool.wait_ge(s("tab_moved"), k)
                            pool.sem_inc(s("turn"), 1)
                        nc.gpsimd.indirect_dma_start(g.row_ring[:, j:j + 1], None, g.tab_dram, row_index).then_inc(s("tab_row"), 16)
            body(0, 0, 0)
            body(1, 1, 1)
            with pool.Fori(1, steps // 2) as pair:
                body(pair * 2, 0)
                body(pair * 2 + 1, 1)
            if rows_of_sources:
                pool.wait_ge(s("tab_row"), 16 * T)
                nc.gpsimd.tensor_copy(g.src_row_i[:, T - RING:T], g.row_ring[:]).then_inc(s("tab_moved"), 1)
                pool.wait_ge(s("tab_moved"), steps)
                slots_of_sources(g, pool, s("slots"))

        if mode in ("conv", "first", "left"):
            @block.tensor
            def _(pe):
                def turn(k, first, j):
                    pe.wait_ge(s(f"row{j}"), k * 16 + 16)
                    if not (first and j < 2):
                        after(pe, "t", k, j, 2)
                    A.transpose(g.psT[j % 2][:, 0, :], g.ring[j][:, 0:D], g.ident[:]).then_inc(s("tp"), 1)

                def product(k, first, j):
                    after(pe, "t", k, j)
                    if not (first and j < 2):
                        if mode == "conv":
                            pe.wait_ge(s("even"), (k * RING + (j - 1)) * (R // 2))
                            pe.wait_ge(s("odd"), (k * RING + (j - 1)) * (R // 2))
                        else:
                            after(pe, "read", k, j, 2)
                    out = g.psL[j % 2]
                    if mode == "conv":
                        A.matmul(out[:, 0:512], g.T2[j % 2], g.Wrel[layer][:, 0:512], start=True, stop=True)
                        ins = A.matmul(out[:, 512:1024], g.T2[j % 2], g.Wrel[layer][:, 512:1024], start=True, stop=True)
                    elif mode == "first":
                        ins = A.matmul(out[:, 0:W], g.T2[j % 2], g.WG[0][:, 0:W], start=True, stop=True)
                    else:
                        ins = A.matmul(out[:, 0:H], g.T2[j % 2], g.vleft[:], start=True, stop=True)
                    ins.then_inc(s("prod"), 1)

                def body(k, first):
                    turn(k, first, 0)
                    for j in range(1, RING):
                        turn(k, first, j)
                        product(k, first, j - 1)
                    product(k, first, RING - 1)
                over(pe, body)
                if mode == "conv":
                    pe.wait_ge(s("sum"), T)
                    A.matmul(g.ps[6][:, 0:D], g.link_in[:], g.sums[:, (T - 1) * W:(T - 1) * W + D],
                             start=True, stop=True).then_inc(s("carry"), 1)

            @block.scalar
            def _(act):
                def body(k, first):
                    for j in range(RING):
                        after(act, "tp", k, j)
                        if not (first and j < 2):
                            after(act, "prod", k, j, 2)
                        ACTE.activation(g.T2[j % 2], g.psT[j % 2][:, 0, :], ACT.Copy).then_inc(s("t"), 1)
                over(act, body)

        if mode == "mean":
            @block.tensor
            def _(pe):
                pe.wait_ge(s("sum"), T)
                A.matmul(g.ps[6][:, 0:D], g.link_in[:], g.sums[:, (T - 1) * W:(T - 1) * W + D],
                         start=True, stop=True).then_inc(s("carry"), 1)

        @block.vector
        def _(dve):
            def copy_columns(dst, src, k):
                V.tensor_copy(dst, src).then_inc(s("cols"), 1)
                dve.wait_ge(s("cols"), k + 1)

            def convolve(k, first):
                half = R // 2

                def weighted(j, r):
                    name = ("even", "odd")[r % 2]
                    out = g.acc[r % 2][j % 2]
                    p, w = g.psL[j % 2][:, r * D:(r + 1) * D], g.w_ring[:, j, r:r + 1]
                    if r < 2:
                        ins = V.tensor_scalar(out, p, w, None, ALU.mult)
                    else:
                        dve.wait_ge(s(name), (k * RING + j) * half + r // 2)
                        ins = V.scalar_tensor_tensor(out, p, w, out, ALU.mult, ALU.add)
                    ins.then_inc(s(name), 1)

                def add_even(j):
                    dve.wait_ge(s("even"), (k * RING + j + 1) * half)
                    if not (first and j == 0):
                        after(dve, "sum", k, j, 1)
                    V.scalar_tensor_tensor(row_of(k, j, 1), row_of(k, j), g.same_ring[:, j:j + 1], g.acc[0][j % 2],
                                           ALU.mult, ALU.add).then_inc(s("half_sum"), 1)

                def add_odd(j):
                    dve.wait_ge(s("odd"), (k * RING + j + 1) * half)
                    after(dve, "half_sum", k, j)
                    V.tensor_tensor(row_of(k, j, 1), row_of(k, j, 1), g.acc[1][j % 2], ALU.add).then_inc(s("sum"), 1)
                for j in range(RING):
                    after(dve, "prod", k, j)
                    if j >= 2 or not first:
                        after(dve, "sum", k, j, 2)
                    for r in range(R):
                        weighted(j, r)
                        if j > 0 and r == 2:
                            add_even(j - 1)
                        if j > 0 and r == 5:
                            add_odd(j - 1)
                add_even(RING - 1)
                add_odd(RING - 1)

            def body(k, first):
                if mode in ("conv", "mean"):
                    if not first:
                        dve.wait_ge(s("sum"), k * RING)
                    if mode == "conv":
                        V.tensor_copy(g.w_ring[:], g.w_slot[:, bass.ds(k * RING, RING), :])
                    copy_columns(g.same_ring[:], g.same[:, bass.ds(k * RING, RING)], k)
                if mode == "conv":
                    convolve(k, first)
                    return
                for j in range(RING):
                    if mode == "mean":
                        dve.wait_ge(s(f"row{j}"), k * 16 + 16)
                        if not (first and j == 0):
                            after(dve, "sum", k, j, 1)
                        V.scalar_tensor_tensor(row_of(k, j, 1), row_of(k, j), g.same_ring[:, j:j + 1], g.ring[j][:, 0:D],
                                               ALU.mult, ALU.add).then_inc(s("sum"), 1)
                    if mode == "rows":
                        dve.wait_ge(s(f"row{j}"), k * 16 + 16)
                        V.tensor_copy(row_of(k, j, 1, W), g.ring[j][:, 0:W]).then_inc(s("put"), 1)
                    if mode == "first":
                        after(dve, "prod", k, j)
                        V.tensor_copy(row_of(k, j, 1, W), g.psL[j % 2][:, 0:W]).then_inc(s("read"), 1)
                    if mode == "left":
                        after(dve, "prod", k, j)
                        V.tensor_copy(g.a_left[:, bass.ds(k * RING + j, 1), :], g.psL[j % 2][:, None, 0:H]).then_inc(s("read"), 1)
            if mode in ("conv", "mean"):
                V.memset(g.sums_all[:, 0:W], 0.0).then_inc(s("zero"), 1)
                dve.wait_ge(s("zero"), 1)
            over(dve, body)
            if mode in ("conv", "mean"):
                dve.wait_ge(s("carry"), 1)
                V.tensor_copy(g.carry[:], g.ps[6][:, 0:D]).then_inc(s("zero"), 1)
    ph.end()


RMAX = bass.bass_isa.ReduceOp.max


def attention(g, layer):
    nc, A, V, ACTE = g.nc, g.nc.tensor, g.nc.vector, g.nc.scalar
    final = layer == 3
    ph = Phase(nc, f"att{layer}")
    s_dve, s_pe, s_exp, s_max, s_mul, s_ready, s_left, s_sum, s_col, s_zero = (
        ph.sem(n) for n in ("dve_steps", "pe_steps", "exp", "greatest", "weighed", "weights_ready", "left_sum", "sum", "columns", "zero"))
    heads = lambda t: t.rearrange("p (h t) -> p h t", h=H)
    q = g.att
    reached = []
    with nc.Block() as block:
        @block.scalar
        def _(act):
            act.wait_ge(s_max, 2 if final else 1)
            ACTE.activation(q.e, q.e, ACT.Exp).then_inc(s_exp, 1)

        if final:
            @block.gpsimd
            def _(pool):
                pool.wait_ge(s_max, 1)
                nc.gpsimd.partition_all_reduce(q.gmax, q.pmax, P, RMAX).then_inc(s_mul, 1)
        else:
            @block.gpsimd
            def _(pool):
                def body(k):
                    part = g.sums[:, bass.ds(k * (RING * W), RING * W)].rearrange("p (t w) -> p t w", w=W)[:, :, 0:D] \
                        .rearrange("p t (h c) -> p t h c", h=H)
                    weights = q.e.rearrange("p (h t) -> p t h", h=H)[:, bass.ds(k * RING, RING), :, None]
                    nc.gpsimd.tensor_tensor(part, part, weights.to_broadcast([P, RING, H, C]), ALU.mult).then_inc(s_mul, 1)
                pool.wait_ge(s_ready, 1)
                body(0)
                with pool.Fori(1, T // RING) as k:
                    body(k)

        @block.vector
        def _(dve):
            n = [0]

            def link(ins):
                n[0] += 1
                ins.then_inc(s_dve, 1)
                dve.wait_ge(s_dve, n[0])

            def wide(t):
                return t[:, None, :].to_broadcast([P, H, T])

            def segment_sum(v, out, pe_step):
                link(V.tensor_tensor_scan(q.fwd, q.same, v, 0.0, ALU.mult, ALU.add))
                link(V.tensor_tensor_scan(q.bwd[:, ::-1], q.next[:, ::-1], v[:, ::-1], 0.0, ALU.mult, ALU.add))
                link(V.tensor_copy(q.ends[:, 0:H], heads(q.fwd)[:, :, T - 1]))
                link(V.tensor_copy(q.ends[:, H:2 * H], heads(q.bwd)[:, :, 0]))
                reached.append(n[0])
                link(V.tensor_tensor(q.fwd, q.fwd, q.bwd, ALU.add))
                link(V.tensor_tensor(out, q.fwd, v, ALU.subtract))
                dve.wait_ge(s_pe, pe_step)
                link(V.tensor_copy(q.ends, g.ps[0][:, 0:2 * H]))
                for h in range(H):
                    oh = heads(out)[:, h, :]
                    link(V.scalar_tensor_tensor(oh, g.in_first[:], q.ends[:, h:h + 1], oh, ALU.mult, ALU.add))
                    link(V.scalar_tensor_tensor(oh, g.in_last[:], q.ends[:, H + h:H + h + 1], oh, ALU.mult, ALU.add))

            link(V.tensor_copy(heads(q.same), wide(g.same[:, 0:T])))
            link(V.tensor_copy(heads(q.next), wide(g.same[:, 1:T + 1])))
            link(V.tensor_tensor(heads(q.v), g.ad[:].rearrange("p t h -> p h t"), wide(g.is_last[:]), ALU.mult))
            segment_sum(q.v, q.e, 1)
            left = (g.a_left[:] if final else g.sums.rearrange("p (t w) -> p t w", w=W)[:, :, D:W]).rearrange("p t h -> p h t")
            link(V.tensor_tensor(heads(q.e), heads(q.e), left, ALU.add))
            link(V.scalar_tensor_tensor(q.e, q.e, 0.2, q.e, ALU.mult, ALU.max))
            if final:
                link(V.tensor_scalar(g.tmpT[:], g.dstf[:, 1:T + 1], float(N), -1e30, ALU.is_equal, ALU.mult))
                link(V.tensor_tensor(heads(q.e), heads(q.e), wide(g.tmpT[:]), ALU.add))
                link(V.tensor_reduce(q.pmax, q.e, AX_X, ALU.max))
                dve.sem_inc(s_max, 1)
                dve.wait_ge(s_mul, 1)
                V.tensor_scalar(q.e, q.e, q.gmax[:, 0:1], None, ALU.subtract).then_inc(s_max, 1)
                dve.wait_ge(s_exp, 1)
                link(V.tensor_copy(g.ad[:].rearrange("p t h -> p h t"), heads(q.e)))
                return
            link(V.tensor_scalar(q.same, q.same, 1e30, -1e30, ALU.mult, ALU.add))
            link(V.tensor_scalar(q.next, q.next, 1e30, -1e30, ALU.mult, ALU.add))
            link(V.tensor_tensor_scan(q.fwd, q.same, q.e, -1e30, ALU.add, ALU.max))
            link(V.tensor_tensor_scan(q.bwd[:, ::-1], q.next[:, ::-1], q.e[:, ::-1], -1e30, ALU.add, ALU.max))
            for h in range(H):
                c = slice(h * P, (h + 1) * P)
                link(V.tensor_scalar(q.diag_in[:, c], g.ident[:], heads(q.fwd)[:, h, T - 1:T], None, ALU.mult))
                link(V.tensor_scalar(q.diag_out[:, c], g.ident[:], heads(q.bwd)[:, h, 0:1], None, ALU.mult))
            reached.append(n[0])
            link(V.tensor_tensor(q.v, q.fwd, q.bwd, ALU.max))
            dve.wait_ge(s_pe, 2)
            for bank, mask, col in ((1, g.no_in, 0), (2, g.no_out, H)):
                both = q.diag_in.rearrange("p (h k) -> p h k", h=H)
                link(V.tensor_tensor(both, g.ps[bank].rearrange("p (h k) -> p h k", h=H),
                                     mask[:, None, :].to_broadcast([P, H, P]), ALU.add))
                link(V.tensor_reduce(q.ends[:, col:col + H], both, AX_X, ALU.max))
            link(V.tensor_scalar(g.tmpT[:], g.in_first[:], 1e30, -1e30, ALU.mult, ALU.add))
            link(V.tensor_scalar(g.tmpT2[:], g.in_last[:], 1e30, -1e30, ALU.mult, ALU.add))
            for h in range(H):
                vh = heads(q.v)[:, h, :]
                link(V.scalar_tensor_tensor(vh, g.tmpT[:], q.ends[:, h:h + 1], vh, ALU.add, ALU.max))
                link(V.scalar_tensor_tensor(vh, g.tmpT2[:], q.ends[:, H + h:H + h + 1], vh, ALU.add, ALU.max))
            V.tensor_tensor(q.e, q.e, q.v, ALU.subtract).then_inc(s_max, 1)
            link(V.tensor_copy(heads(q.same), wide(g.same[:, 0:T])))
            link(V.tensor_copy(heads(q.next), wide(g.same[:, 1:T + 1])))
            dve.wait_ge(s_exp, 1)
            segment_sum(q.e, q.v, 3)
            link(V.tensor_scalar(q.v, q.v, 1e-16, None, ALU.add))
            link(V.reciprocal(q.v, q.v))
            link(V.tensor_tensor(q.e, q.e, q.v, ALU.mult))
            V.memset(g.sums_all[:, 0:W], 0.0).then_inc(s_ready, 1)
            dve.wait_ge(s_ready, 1)

            def body(k, first):
                if not first:
                    dve.wait_ge(s_left, k * RING)
                    dve.wait_ge(s_sum, k * RING)
                V.tensor_copy(g.same_ring[:], g.same[:, bass.ds(k * RING, RING)]).then_inc(s_col, 1)
                dve.wait_ge(s_col, k + 1)
                dve.wait_ge(s_mul, k + 1)
                for j in range(RING):
                    for s_half, start in ((s_left, 0), (s_sum, D // 2)):
                        if not (first and j == 0):
                            dve.wait_ge(s_half, k * RING + j)
                        at = lambda shift: g.sums_all[:, bass.ds((k * RING + j + shift) * W + start, D // 2)]
                        V.scalar_tensor_tensor(at(1), at(0), g.same_ring[:, j:j + 1], at(1), ALU.mult, ALU.add).then_inc(s_half, 1)
            body(0, True)
            with dve.Fori(1, T // RING) as k:
                body(k, False)
            dve.wait_ge(s_pe, 4)
            V.tensor_copy(g.carry[:], g.ps[6][:, 0:D]).then_inc(s_zero, 1)

        @block.tensor
        def _(pe):
            def links(n, sem_at):
                pe.wait_ge(s_dve, sem_at)
                A.matmul(g.ps[0][:, 0:H], g.link_in[:], q.ends[:, 0:H], start=True, stop=True)
                A.matmul(g.ps[0][:, H:2 * H], g.link_out[:], q.ends[:, H:2 * H], start=True, stop=True).then_inc(s_pe, 1)
            links(1, reached[0])
            if final:
                return
            pe.wait_ge(s_dve, reached[1])
            A.matmul(g.ps[1], g.ones[:], q.diag_in, start=True, stop=True)
            A.matmul(g.ps[2], g.ones[:], q.diag_out, start=True, stop=True).then_inc(s_pe, 1)
            links(3, reached[2])
            pe.wait_ge(s_left, T)
            pe.wait_ge(s_sum, T)
            A.matmul(g.ps[6][:, 0:D], g.link_in[:], g.sums[:, (T - 1) * W:(T - 1) * W + D],
                     start=True, stop=True).then_inc(s_pe, 1)
    ph.end()


def by_source(g):
    nc, A, V, ACTE = g.nc, g.nc.tensor, g.nc.vector, g.nc.scalar
    ph = Phase(nc, "bysrc")
    sems = {}

    def s(name):
        if name not in sems:
            sems[name] = ph.sem(name)
        return sems[name]
    B = G4
    steps = T // B

    def over(eng, body):
        body(0, True)
        with eng.Fori(1, steps) as k:
            body(k, False)

    def after(eng, name, k, j, back=0):
        eng.wait_ge(s(name), k * B + j + 1 - back)
    with nc.Block() as block:
        @block.gpsimd
        def _(pool):
            def body(k, first):
                if first != "all":
                    for j in range(B):
                        pool.wait_ge(s(f"row{j}"), k * 16)
                nc.gpsimd.tensor_copy(g.idx_ring[:, 0:B], g.dst_slot_i[:, bass.ds(k * B, B)]).then_inc(s("index"), 1)
                pool.wait_ge(s("index"), k + 1)
                for j in range(B):
                    if first != "all":
                        after(pool, "msg", k, j, B)
                    pool.sem_inc(s("turn"), 1)
                    nc.gpsimd.indirect_dma_start(g.ring[j][:, 0:W], None, g.gat_dram,
                                                 bass.IndirectOffsetOnAxis(g.idx_ring[:, j:j + 1], 0)).then_inc(s(f"row{j}"), 16)
                    if first != "all":
                        add(k - 1, j, first)

            def add(k, j, first):
                after(pool, "sum", k, j)
                after(pool, "index_out", k, j)
                if not (first and j == 0):
                    pool.wait_ge(s("added"), (k * B + j) * 16)
                pool.sem_inc(s("turn"), 1)
                nc.gpsimd.indirect_dma_start(g.U_dram, bass.IndirectOffsetOnAxis(g.add_row[j][:, 0:1], 0), g.RS[j], None,
                                             compute_op=ALU.add).then_inc(s("added"), 16)
            body(0, "all")
            body(1, True)
            with pool.Fori(2, steps) as k:
                body(k, False)
            for j in range(B):
                add(steps - 1, j, False)
            pool.wait_ge(s("added"), 16 * T)

        @block.tensor
        def _(pe):
            def body(k, first):
                for j in range(B):
                    after(pe, "diag", k, j)
                    if not first or j >= 2:
                        after(pe, "same_src", k, j, 2)
                    A.matmul(g.ps[j % 2][:, 0:P], g.ones[:], g.diag[j % 2], start=True, stop=True).then_inc(s("srcrow"), 1)
                    after(pe, "same_src", k, j)
                    after(pe, "msg", k, j)
                    if not first or j >= 2:
                        after(pe, "sum", k, j, 2)
                    A.matmul(g.ps[2 + j % 2][:, 0:W], g.Sm[j % 2], g.msg[j % 2], start=True, stop=True).then_inc(s("sump"), 1)
            over(pe, body)

        @block.scalar
        def _(act):
            def body(k, first):
                for j in range(B):
                    after(act, "sump", k, j)
                    if not first:
                        act.wait_ge(s("added"), (k * B + (j + 1 - B)) * 16)
                    ACTE.activation(g.RS[j], g.ps[2 + j % 2][:, 0:W], ACT.Copy).then_inc(s("sum"), 1)
            over(act, body)

        @block.vector
        def _(dve):
            V.tensor_copy(g.tmpT[:], g.src_i[:]).then_inc(s("pre"), 1)
            V.tensor_copy(g.spare[:], g.spare_i[:]).then_inc(s("pre"), 1)
            dve.wait_ge(s("pre"), 2)
            V.tensor_scalar(g.tmpT2[:], g.dstf[:, 1:T + 1], float(N), g.spare[:, 0:1], ALU.is_equal, ALU.mult).then_inc(s("pre"), 1)
            dve.wait_ge(s("pre"), 3)
            V.tensor_tensor(g.tmpT[:], g.tmpT[:], g.tmpT2[:], ALU.add).then_inc(s("pre"), 1)
            dve.wait_ge(s("pre"), 4)

            def body(k, first):
                V.tensor_copy(g.src_cols[:], g.tmpT[:, bass.ds(k * B, B)])
                V.tensor_copy(g.ex_cols[:], g.ad[:, bass.ds(k * B, B), :]).then_inc(s("cols"), 1)
                dve.wait_ge(s("cols"), k + 1)
                for j in range(B):
                    src = g.src_cols[:, j:j + 1]
                    if not first or j >= 2:
                        after(dve, "srcrow", k, j, 2)
                    V.tensor_scalar(g.diag[j % 2], g.ident[:], src, None, ALU.mult).then_inc(s("diag"), 1)
                    dve.wait_ge(s(f"row{j}"), k * 16 + 16)
                    if not first or j >= 2:
                        after(dve, "sump", k, j, 2)
                    V.tensor_tensor(g.msg[j % 2][:, 0:D].rearrange("p (h c) -> p h c", h=H),
                                    g.ring[j][:, 0:D].rearrange("p (h c) -> p h c", h=H),
                                    g.ex_cols[:, j, :, None].to_broadcast([P, H, C]), ALU.mult)
                    V.tensor_copy(g.msg[j % 2][:, D:W], g.ex_cols[:, j, :]).then_inc(s("msg"), 1)
                    after(dve, "srcrow", k, j)
                    V.tensor_scalar(g.Sm[j % 2], g.ps[j % 2][:, 0:P], src, None, ALU.is_equal).then_inc(s("same_src"), 1)
                    after(dve, "same_src", k, j)
                    V.scalar_tensor_tensor(g.dup_tmp, g.Sm[j % 2], 1.0, g.below[:], ALU.mult, ALU.mult,
                                           accum_out=g.dup[:, 0:1]).then_inc(s("dup"), 1)
                    V.tensor_tensor(g.dup[:, 1:2], g.spare[:], src, ALU.subtract).then_inc(s("dup"), 1)
                    after_dup = (k * B + j) * 4
                    dve.wait_ge(s("dup"), after_dup + 2)
                    V.tensor_scalar(g.dup[:, 2:3], g.dup[:, 0:1], 0.5, g.dup[:, 1:2], ALU.is_gt, ALU.mult).then_inc(s("dup"), 1)
                    dve.wait_ge(s("dup"), after_dup + 3)
                    V.tensor_tensor(g.dup[:, 3:4], g.dup[:, 2:3], src, ALU.add).then_inc(s("dup"), 1)
                    dve.wait_ge(s("dup"), after_dup + 4)
                    if not first:
                        dve.wait_ge(s("added"), (k * B + (j + 1 - B)) * 16)
                    V.tensor_copy(g.add_row[j][:], g.dup[:, 3:4]).then_inc(s("index_out"), 1)
            over(dve, body)
    ph.end()


def last_layer(g):
    nc, A, V, ACTE = g.nc, g.nc.tensor, g.nc.vector, g.nc.scalar
    ph = Phase(nc, "last")
    s = Signals(ph)
    after, before, loaded, stored = s.after, s.before, s.loaded, s.stored
    out_rows = g.X2

    def rows(table, c):
        start = N - CH if c.last else c.k * (2 * CH) + c.h * CH
        return table[bass.ds(start, CH), :].rearrange("(p j) f -> p j f", j=G4)

    def flat(t):
        return t[:].rearrange("p j f -> p (j f)")
    with nc.Block() as block:
        @block.sync
        def _(sp):
            def turn(at):
                c = at(4)
                if c:
                    before(sp, "agg", c)
                    sp.sem_inc(s("turn_sp"), 1)
                    sp.dma_start(g.UB[c.h][:], rows(g.U_dram, c)).then_inc(s(f"load_u{c.h}"), 16)
                c = at(3)
                if c:
                    before(sp, "y", c)
                    sp.sem_inc(s("turn_sp"), 1)
                    sp.dma_start(g.X[c.h][:], rows(g.x3_dram, c)).then_inc(s(f"load_x{c.h}"), 16)
                c = at(-1)
                if c:
                    after(sp, "o", c)
                    sp.sem_inc(s("turn_sp"), 1)
                    if c.last:
                        sp.wait_ge(s(f"store_o{1 - c.h}"), 16 * (NCH // 2))
                    sp.dma_start(rows(g.out, c), out_rows[c.h][:]).then_inc(s(f"store_o{c.h}"), 16)
            rounds(sp, NCH, turn)
            for h in (0, 1):
                sp.wait_ge(s(f"store_o{h}"), 16 * ((NCH + 1 - h) // 2))

        @block.gpsimd
        def _(pool):
            def turn(at):
                c = at(2)
                if c:
                    after(pool, "recip", c)
                    before(pool, "y", c)
                    before(pool, "neg", c)
                    nc.gpsimd.tensor_tensor(g.V[c.h][:].rearrange("p j (h c) -> p j h c", h=H),
                                            g.UB[c.h][:, :, 0:D].rearrange("p j (h c) -> p j h c", h=H),
                                            g.den[c.h][:, :, :, None].to_broadcast([P, G4, H, C]), ALU.mult).then_inc(s("agg"), 1)
                c = at(0)
                if c:
                    after(pool, "rs", c)
                    before(pool, "o", c)
                    pool.sem_inc(s("turn_pool"), 1)
                    nc.gpsimd.tensor_scalar(g.nb["a"][c.h][:], g.mv["a"][c.h][:, :, 0], -1.0, None, ALU.mult).then_inc(s("neg_mean"), 1)
                    after(pool, "neg_mean", c)
                    nc.gpsimd.tensor_tensor(g.nb["a"][c.h][:], g.nb["a"][c.h][:], g.rs["a"][c.h][:], ALU.mult).then_inc(s("nb"), 1)
            rounds(pool, NCH, turn)

        @block.tensor
        def _(pe):
            def turn(at):
                c = at(2)
                if c:
                    loaded(pe, "x", c)
                    for j in range(G4):
                        ins = A.transpose(g.psT[c.h][:, j, :], g.X[c.h][:, j, :], g.ident[:])
                    ins.then_inc(s("xTp"), 1)
                    after(pe, "xT", c)
                    before(pe, "u", c)
                    for j in range(G4):
                        ins = A.matmul(g.psL[c.h][:, j * D:(j + 1) * D], g.XT[c.h][:, j, :], g.Wres[:], start=True, stop=True)
                    ins.then_inc(s("up"), 1)
            rounds(pe, NCH, turn)

        @block.scalar
        def _(act):
            def turn(at):
                c = at(2)
                if c:
                    after(act, "xTp", c)
                    ACTE.activation(g.XT[c.h][:], g.psT[c.h][:], ACT.Copy).then_inc(s("xT"), 1)
                c = at(1)
                if c:
                    after(act, "u", c)
                    before(act, "z", c)
                    ACTE.activation(g.G[c.h][:], g.V[c.h][:], ACT.Relu, scale=-1.0).then_inc(s("neg"), 1)
                    after(act, "neg", c)
                    ACTE.activation(g.G[c.h][:], g.G[c.h][:], ACT.Exp, scale=-1.0).then_inc(s("e"), 1)
                c = at(0)
                if c:
                    after(act, "mv", c)
                    before(act, "rs", c)
                    ACTE.activation(g.lnv["a"][c.h][:], g.mv["a"][c.h][:, :, 1], ACT.Ln, bias=g.eps[:, 0:1]).then_inc(s("ln"), 1)
                    after(act, "ln", c)
                    before(act, "o", c)
                    ACTE.activation(g.rs["a"][c.h][:], g.lnv["a"][c.h][:], ACT.Exp, scale=-0.5).then_inc(s("rs"), 1)
                    after(act, "nb", c)
                    stored(act, "o", c)
                    for j in range(G4):
                        ins = ACTE.activation(out_rows[c.h][:, j, :], g.Y[c.h][:, j, :], ACT.Identity,
                                              bias=g.nb["a"][c.h][:, j:j + 1], scale=g.rs["a"][c.h][:, j:j + 1])
                    ins.then_inc(s("o"), 1)
            rounds(act, NCH, turn)

        @block.vector
        def _(dve):
            def reciprocals(c):
                loaded(dve, "u", c)
                before(dve, "agg", c)
                V.tensor_scalar(g.den[c.h][:], g.UB[c.h][:, :, D:W], 1e-8, None, ALU.add).then_inc(s("eps"), 1)
                yield
                after(dve, "eps", c)
                V.reciprocal(g.den[c.h][:], g.den[c.h][:]).then_inc(s("recip"), 1)
                yield

            def elu_argument(c):
                after(dve, "agg", c)
                after(dve, "up", c)
                V.tensor_tensor(flat(g.V[c.h]), flat(g.V[c.h]), g.psL[c.h][:, 0:512], ALU.add).then_inc(s("u"), 1)
                yield
                after(dve, "u", c)
                before(dve, "o", c)
                V.scalar_tensor_tensor(g.Y[c.h][:], g.V[c.h][:], 0.0, g.X[c.h][:], ALU.max, ALU.add).then_inc(s("y"), 1)
                yield

            def residual(c):
                after(dve, "y", c)
                after(dve, "e", c)
                V.scalar_tensor_tensor(g.Y[c.h][:], g.G[c.h][:], -1.0, g.Y[c.h][:], ALU.add, ALU.add).then_inc(s("z"), 1)
                yield
                after(dve, "z", c)
                for j in range(G4):
                    ins = V.bn_stats(g.st["a"][c.h][:, j, :], g.Y[c.h][:, j, :])
                ins.then_inc(s("st"), 1)
                yield
                after(dve, "st", c)
                before(dve, "nb", c)
                dve.sem_inc(s("turn_dve"), 1)
                for j in range(G4):
                    ins = V.bn_aggr(g.mv["a"][c.h][:, j, :], g.st["a"][c.h][:, j, :])
                ins.then_inc(s("mv"), 1)
                yield

            def turn(at):
                alternate(opt(residual, at(0)), opt(elu_argument, at(1)))
                alternate(opt(reciprocals, at(3)))
            rounds(dve, NCH, turn)
    ph.end()


def build(nc, args, out):
    with ExitStack() as ctx:
        g = Program()
        g.nc, g.args, g.out = nc, args, out

        def sb(name, shape, dt=F32):
            return ctx.enter_context(nc.sbuf_tensor(name, shape, dt))

        def each_slot(name, dt=F32):
            return sb(name, [P, T], dt)

        def dram(name, shape, dt=F32):
            return nc.dram_tensor(name, shape, dt).ap()
        g.tab_dram = dram("tab_dram", (N, 1), I32)
        g.z1_dram, g.x1_dram, g.x2_dram = (dram(n, (N + PAD, D)) for n in ("z1_dram", "x1_dram", "x2_dram"))
        g.xd_dram = dram("xd_dram", (PAD, D))
        g.x3_dram = dram("x3_dram", (N, D))
        g.x3s_dram = dram("x3s_dram", (PAD, D))
        g.gat_dram = dram("gat_dram", (PAD + 1, W))
        g.sorted_dram = dram("sorted_dram", (PAD, 4), I32)
        g.U_dram = dram("U_dram", (UROWS, W))
        g.ZB, g.ZW = 28, UROWS // P * W // 28
        g.src_i = each_slot("src_i", I32)
        g.dst_i = each_slot("dst_i", I32)
        g.type_i = each_slot("type_i", I32)
        g.slot_i = each_slot("slot_i", I32)
        g.last_node_i = each_slot("last_node_i", I32)
        g.tab_row_i = each_slot("tab_row_i", I32)
        g.src_row_i = each_slot("src_row_i", I32)
        g.src_slot_i = each_slot("src_slot_i", I32)
        g.dst_slot_i = each_slot("dst_slot_i", I32)
        g.own_i = each_slot("own_i", I32)
        g.dst_next_i = sb("dst_next_i", [P, 1], I32)
        g.unsorted_i = sb("unsorted_i", [1, 1], I32)
        g.payload = sb("payload", [P, 4], I32)
        g.spare_i = sb("spare_i", [P, 1], I32)
        g.spare = sb("spare", [P, 1])
        g.eps = sb("eps", [P, 1])
        g.idx_ring = sb("idx_ring", [P, 2 * RING], I32)
        g.row_ring = sb("row_ring", [P, RING], I32)
        g.dstf = sb("dstf", [P, T + 2])
        g.same = sb("same", [P, T + 1])
        g.typef = each_slot("typef")
        g.is_last = each_slot("is_last")
        g.in_first = each_slot("in_first")
        g.in_last = each_slot("in_last")
        g.tmpT = each_slot("tmpT")
        g.tmpT2 = each_slot("tmpT2")
        g.rcnt = each_slot("rcnt")
        g.w_slot = sb("w_slot", [P, T, R])
        g.ad = sb("ad", [P, T, H])
        g.a_left = sb("a_left", [P, T, H])
        g.ident = sb("ident", [P, P])
        g.ones = sb("ones", [P, P])
        g.below = sb("below", [P, P])
        g.above = sb("above", [P, P])
        g.link_in = sb("link_in", [P, P])
        g.link_out = sb("link_out", [P, P])
        g.no_in = sb("no_in", [P, P])
        g.no_out = sb("no_out", [P, P])
        g.carry = sb("carry", [P, P])
        g.root1 = sb("root1", [P, D])
        g.root2 = sb("root2", [P, D])
        g.Wres = sb("Wres", [P, D])
        g.gamma = sb("gamma", [P, D])
        g.beta = sb("beta", [P, D])
        g.gat_bias = [sb(f"gat_bias{i}", [P, D]) for i in range(3)]
        g.gat_bias_col = sb("gat_bias_col", [P, 2])
        g.Wrel = [sb(f"Wrel{i}", [P, R * D]) for i in range(2)]
        g.WG = [sb(f"WG{i}", [P, W + H]) for i in range(3)]
        g.vd = [g.WG[0][:, W:W + H]]
        g.WH = sb("WH", [P, W])
        g.vleft = sb("vleft", [P, H])
        g.b1_col, g.bself_col, g.bneigh_col = (sb(n, [P, 1]) for n in ("b1_col", "bself_col", "bneigh_col"))
        g.b1_parts, g.b2_parts = (sb(n, [3, D], BF16) for n in ("b1_parts", "b2_parts"))
        g.gate_parts, g.gate_parts_n = (sb(n, [3, 2 * D], BF16) for n in ("gate_parts", "gate_parts_n"))
        g.ones3 = sb("ones3", [3, P], BF16)
        g.A_gate, g.B_gate = (sb(n, [P, 2 * D]) for n in ("A_gate", "B_gate"))
        g.const_row = [sb(f"const_row{i}", [1, W]) for i in range(2)]
        g.edge_ends = sb("edge_ends", [P, 2 * R1])
        two = lambda name, *shape: [sb(f"{name}{h}", [P, *shape]) for h in range(2)]
        g.st, g.mv, g.rs = ({t: two(f"{n}_{t}", *shape) for t in "abcd"}
                            for n, shape in (("st", (G4, 6)), ("mv", (G4, 2)), ("rs", (G4,))))
        g.nb = {t: two(f"nb_{t}", G4) for t in "acd"}
        g.lnv = {t: two(f"lnv_{t}", G4) for t in "abcd"}
        g.den, g.RW = two("den", G4, H), two("RW", G4, W)
        g.own_ring = [sb(f"own_ring{h}", [P, G4], I32) for h in range(2)]
        g.add_row = [sb(f"add_row{j}", [P, 1], I32) for j in range(G4)]
        g.same_ring = sb("same_ring", [P, RING])
        g.w_ring = sb("w_ring", [P, RING, R])
        g.src_cols = sb("src_cols", [P, G4])
        g.ex_cols = sb("ex_cols", [P, G4, H])
        g.dup = sb("dup", [P, 4])
        psT = [ctx.enter_context(nc.psum_tensor(f"psT{h}", [P, G4, D], F32)) for h in range(2)]
        psM = [ctx.enter_context(nc.psum_tensor(f"psM{h}", [P, G4, D], F32)) for h in range(2)]
        psL = [ctx.enter_context(nc.psum_tensor(f"psL{h}", [P, 1024], F32)) for h in range(2)]
        g.psT, g.psM, g.psL = psT, psM, psL
        flat = lambda t: t[:].rearrange("p j f -> p (j f)")
        g.ps = [flat(psT[0]), flat(psT[1]), psL[0][:, 0:512], psL[0][:, 512:1024], psL[1][:, 0:512], psL[1][:, 512:1024],
                flat(psM[0]), flat(psM[1])]
        sums_all = sb("sums_all", [P, (T + 1) * W])
        g.sums_all, g.sums = sums_all, sums_all[:, W:]

        def carver(region):
            at = [0]

            def carve(*shape, dt=F32):
                n = int(np.prod(shape))
                v = region[:, at[0]:at[0] + n]
                at[0] += n
                assert at[0] <= region.shape[1]
                if dt is not F32:
                    v = v.bitcast(dt)
                names = " ".join(f"a{i}" for i in range(len(shape)))
                return v.rearrange(f"p ({names}) -> p {names}", **{f"a{i}": m for i, m in enumerate(shape)}) if len(shape) > 1 else v
            return carve
        g.sort_row = sums_all[:, 0:PAD]
        carve = carver(sums_all)
        g.wrel, g.cnt_fwd, g.cnt_bwd = (carve(R1, T) for _ in range(3))
        g.diag_first, g.diag_last, g.bself_rep, g.bneigh_rep, g.att_tmp = (carve(D) for _ in range(5))
        g.WgaT, g.W_self, g.W_neigh, g.WselfT, g.WneighT, g.WgbT = (carve(D) for _ in range(6))
        g.bias_rep = [carve(D) for _ in range(2)]
        g.zero_row = carve(g.ZW)
        g.node_iota = carve(400, dt=I32)
        g.bself_row, g.bneigh_row, g.bgate_row, g.b1_row, g.b2_row = (carve(D)[0:3, :] for _ in range(5))
        g.bias_gate, g.bias_gate_n, g.split_rest, g.split_sum = (carve(2 * D)[0:3, :] for _ in range(4))
        g.split_part = carve(D, dt=BF16)[0:3, :]
        g.att_rows = [carve(D) for _ in range(8)]
        g.Wd = [carve(D) for _ in range(3)]
        carve = carver(sums_all)
        g.UB = [carve(G4, W) for _ in range(2)]
        work = sb("work", [P, 2 * 12 * G4 * D])
        carve = carver(work)
        pair = lambda *shape: [carve(*shape) for _ in range(2)]
        g.X, g.XT, g.Z1T, g.Z1, g.Y, g.G = (pair(G4, D) for _ in range(6))
        g.V, g.X2, g.X3, g.M, g.MT = (pair(G4, D) for _ in range(5))
        carve = carver(work)
        g.sort_diag, g.sort_part, g.sort_flags = carve(P), carve(5), carve(PAD // 4)
        g.sorted_edges = carve(T, 4, dt=I32)
        carve = carver(work)
        q = g.att = Program()
        q.e, q.v, q.fwd, q.bwd, q.same, q.next = (carve(FT) for _ in range(6))
        q.diag_in, q.diag_out, q.ends, q.pmax, q.gmax = carve(H * P), carve(H * P), carve(2 * H), carve(1), carve(1)
        carve = carver(work)
        g.ring = [carve(W) for _ in range(RING)]
        g.T2 = [carve(D) for _ in range(2)]
        g.acc = [[carve(D) for _ in range(2)] for _ in range(2)]
        g.RS = [carve(W) for _ in range(G4)]
        g.diag, g.Sm, g.msg = pair(D), pair(D), pair(W)
        g.dup_tmp = carve(D)

        col = lambda ap: ap.rearrange("(n a) -> n a", a=1)
        spread = lambda ap, at=0, n=P: bass.AP(ap.tensor, at, [[0, n], [1, D]])
        L2 = lambda n: args["L2_gnn_" + n]
        g.dst_next_view = bass.AP(args["dst"].tensor, T, [[T, P - 1], [1, 1]])
        g.weight_loads = [
            (g.W_self, args["L1_gnn_W_self"]), (g.W_neigh, args["L1_gnn_W_neigh"]),
            (g.WselfT, args["W_self_T"]), (g.WneighT, args["W_neigh_T"]),
            (g.WgaT, args["W_gate_T"][0:D, :]), (g.WgbT, args["W_gate_T"][D:2 * D, :]),
            (g.bself_col[:], col(args["L1_gnn_b_self"])), (g.bneigh_col[:], col(args["L1_gnn_b_neigh"])),
            (g.bself_row, spread(args["L1_gnn_b_self"], 0, 3)), (g.bneigh_row, spread(args["L1_gnn_b_neigh"], 0, 3)),
            (g.bgate_row, spread(args["L1_gnn_b_gate"], 0, 3)), (g.b1_col[:], col(args["L0_gnn_b1"])),
            (g.b1_row, spread(args["L0_gnn_b1"], 0, 3)), (g.b2_row, spread(args["L0_gnn_b2"], 0, 3)),
            (g.root1[:], args["L0_gnn_root1"]), (g.root2[:], args["L0_gnn_root2"]),
            (g.Wres[:], args["L3_gnn_residual_projection"]), (g.WH[:, 0:D], args["L3_gnn_W"]),
            (g.gamma[:], spread(args["L1_gnn_ln_gamma"])), (g.beta[:], spread(args["L1_gnn_ln_beta"])),
            (g.Wrel[0][:].rearrange("p (r f) -> p r f", r=R), args["L0_gnn_W1"].rearrange("r i o -> i r o")),
            (g.Wrel[1][:].rearrange("p (r f) -> p r f", r=R), args["L0_gnn_W2"].rearrange("r i o -> i r o")),
            (g.att_rows[6], spread(args["L3_gnn_A_right"])), (g.att_rows[7], spread(args["L3_gnn_A_left"])),
        ]
        for i in range(3):
            g.weight_loads += [
                (g.WG[i][:, 0:D], L2("Ws")[i]), (g.Wd[i], L2("Wd")[i]), (g.gat_bias[i][:], spread(L2("b"), i * D)),
                (g.att_rows[i], spread(L2("att_s"), i * D)), (g.att_rows[3 + i], spread(L2("att_d"), i * D))]
        for i in range(2):
            g.weight_loads.append((g.gat_bias_col[:, i:i + 1], col(L2("b")[i])))
        g.att_products = []
        for i in range(3):
            g.att_products += [(g.WG[i][:, D:W], g.WG[i][:, 0:D], g.att_rows[i]), (g.WG[i][:, W:W + H], g.Wd[i], g.att_rows[3 + i])]
        g.att_products += [(g.WH[:, D:W], g.WH[:, 0:D], g.att_rows[6]), (g.vleft[:], g.WH[:, 0:D], g.att_rows[7])]
        nc.scalar.preload_act_table_set("natural_log_exp_and_others")
        steps = [
            lambda: (load_edges(g), sort_edges(g), setup(g)),
            lambda: chunks(g, "nodes"),
            lambda: gather(g, "conv", 0), lambda: chunks(g, "z1"),
            lambda: gather(g, "conv", 1), lambda: chunks(g, "x1"),
            lambda: gather(g, "mean"), lambda: chunks(g, "x2"),
            lambda: gather(g, "first"), lambda: attention(g, 0), lambda: chunks(g, "h", 0),
            lambda: gather(g, "rows", 1), lambda: attention(g, 1), lambda: chunks(g, "h", 1),
            lambda: gather(g, "rows", 2), lambda: attention(g, 2), lambda: chunks(g, "x3"),
            lambda: gather(g, "left"), lambda: attention(g, 3), lambda: by_source(g),
            lambda: last_layer(g),
        ]
        for step in steps:
            step()


_INS = ["x", "src", "dst", "edge_type_8", "L0_gnn_W1", "L0_gnn_root1", "L0_gnn_b1", "L0_gnn_W2", "L0_gnn_root2",
        "L0_gnn_b2", "L1_gnn_W_self", "L1_gnn_b_self", "L1_gnn_W_neigh", "L1_gnn_b_neigh", "L1_gnn_b_gate",
        "L1_gnn_ln_gamma", "L1_gnn_ln_beta", "L2_gnn_Ws", "L2_gnn_Wd", "L2_gnn_att_s", "L2_gnn_att_d", "L2_gnn_b",
        "L3_gnn_W", "L3_gnn_A_left", "L3_gnn_A_right", "L3_gnn_residual_projection"]
_TRANSPOSED = {"W_self_T": "L1_gnn_W_self", "W_neigh_T": "L1_gnn_W_neigh", "W_gate_T": "L1_gnn_W_gate"}


def kernel(**inputs):
    import numpy as _np
    import concourse.bacc as _bacc
    from concourse import mybir as _mybir
    from concourse.bass_utils import run_bass_kernel_spmd as _run

    nc = _bacc.Bacc("TRN2", target_bir_lowering=False, num_devices=1)
    laid_out = {name: _np.ascontiguousarray(inputs[name]) for name in _INS}
    for name, of in _TRANSPOSED.items():
        laid_out[name] = _np.ascontiguousarray(_np.asarray(inputs[of]).T)
    arrays = {f"in_{name}": a for name, a in laid_out.items()}
    args = {name: nc.dram_tensor(f"in_{name}", a.shape, _mybir.dt.from_np(a.dtype), kind="ExternalInput").ap()
            for name, a in laid_out.items()}
    out = nc.dram_tensor("out", (N, D), F32, kind="ExternalOutput").ap()
    build(nc, args, out)
    r = _run(nc, [arrays], core_ids=[0])
    return r.results[0]["out"]
```
